# Optimizing a Trainium2 kernel written in Bass

```python
import numpy as np
import jax
import jax.numpy as jnp

def _softmax(x, axis=-1):
    return jax.nn.softmax(x, axis=axis)

def _gelu(x):
    return jax.nn.gelu(x, approximate=True)

def _silu(x):
    return jax.nn.silu(x)

def _sigmoid(x):
    return jax.nn.sigmoid(x)

def _layernorm(x, axis=-1, eps=1e-05):
    m = jnp.mean(x, axis=axis, keepdims=True)
    v = jnp.var(x, axis=axis, keepdims=True)
    return (x - m) / jnp.sqrt(v + eps)

def _scatter_add(tgt, idx, src, axis=0):
    return tgt.at[idx].add(src)

def _segment_sum(src, seg, n):
    return jax.ops.segment_sum(src, seg, n)
kernel_name = 'mk_hybrid_d1_jaxref_r4_13092d'

def setup_inputs(seed: int=0):
    np.random.seed(seed)
    _w = jnp.asarray

    def _L0_attn_a_setup():
        import jax, jax.numpy as jnp
        import numpy as np
        B, T, D = (2, 512, 1024)
        H = 32
        HKV = 1
        HD = D // H
        key = jax.random.key(seed)
        ks = jax.random.split(key, 9)
        s = lambda fan_in: 1.0 / np.sqrt(fan_in)
        return {'x': jax.random.normal(ks[0], (B, T, D), dtype=jnp.float32), 'wq_w': jax.random.normal(ks[1], (H * HD, D), dtype=jnp.float32) * s(D), 'wq_b': jax.random.normal(ks[2], (H * HD,), dtype=jnp.float32) * 0.02, 'wk_w': jax.random.normal(ks[3], (HKV * HD, D), dtype=jnp.float32) * s(D), 'wk_b': jax.random.normal(ks[4], (HKV * HD,), dtype=jnp.float32) * 0.02, 'wv_w': jax.random.normal(ks[5], (HKV * HD, D), dtype=jnp.float32) * s(D), 'wv_b': jax.random.normal(ks[6], (HKV * HD,), dtype=jnp.float32) * 0.02, 'wo_w': jax.random.normal(ks[7], (D, H * HD), dtype=jnp.float32) * s(H * HD), 'wo_b': jax.random.normal(ks[8], (D,), dtype=jnp.float32) * 0.02}
    _L0_attn_a_in = _L0_attn_a_setup()

    def _L0_attn_b_setup():
        import jax, jax.numpy as jnp
        import numpy as np
        HID = 1024
        DM = 128
        DIN = 2 * DM
        DST = 16
        HD = 64
        NH = DIN // HD
        DCONV = 7
        CONV_DIM = DIN + 2 * DST
        DIN_PROJ = 2 * DIN + 2 * DST + 2 * NH
        SEQ, BATCH = (512, 4)

        def _causal_conv(x, w, b):
            y = jax.lax.conv_general_dilated(jnp.transpose(x, (0, 2, 1)), w, (1,), [(DCONV - 1, 0)], feature_group_count=CONV_DIM, dimension_numbers=('NCH', 'OIH', 'NCH'))
            return jnp.transpose(y, (0, 2, 1)) + b

        def _ssm_scan(x, dt, A, B, C):
            dA = jnp.exp(dt * A)
            dBx = dt[..., None] * x

            def step(h, t):
                dA_t, dBx_t, B_t, C_t = t
                h = dA_t[:, :, None, None] * h + dBx_t[..., None] * B_t[:, None, None, :]
                y = jnp.einsum('bhpn,bn->bhp', h, C_t)
                return (h, y)
            h0 = jnp.zeros((x.shape[0], NH, HD, DST), x.dtype)
            _, ys = jax.lax.scan(step, h0, (jnp.moveaxis(dA, 1, 0), jnp.moveaxis(dBx, 1, 0), jnp.moveaxis(B, 1, 0), jnp.moveaxis(C, 1, 0)))
            return jnp.moveaxis(ys, 0, 1)

        def _hydra(u, in_w, conv_w, conv_b, dt_bias, A_log, D, fcD_w, norm_w, out_w):
            b, l, _ = u.shape
            zxbcdt = u @ in_w.T
            z = zxbcdt[..., :DIN]
            xBC = zxbcdt[..., DIN:DIN + CONV_DIM]
            dt2 = zxbcdt[..., DIN + CONV_DIM:]
            dt_fw = jax.nn.softplus(dt2[..., :NH] + dt_bias)
            dt_bw = jax.nn.softplus(jnp.flip(dt2[..., NH:], 1) + dt_bias)
            xBC = jax.nn.silu(_causal_conv(xBC, conv_w, conv_b))
            xs = xBC[..., :DIN]
            Bm = xBC[..., DIN:DIN + DST]
            Cm = xBC[..., DIN + DST:]
            A = -jnp.exp(A_log)
            x4 = xs.reshape(b, l, NH, HD)
            y_fw = _ssm_scan(x4, dt_fw, A, Bm, Cm).reshape(b, l, DIN)
            y_bw = jnp.flip(_ssm_scan(jnp.flip(x4, 1), dt_bw, A, jnp.flip(Bm, 1), jnp.flip(Cm, 1)).reshape(b, l, DIN), 1)
            zero = jnp.zeros((b, 1, DIN), u.dtype)
            y = jnp.concatenate([zero, y_fw[:, :-1]], 1) + jnp.concatenate([y_bw[:, 1:], zero], 1)
            y = y + xs * jnp.repeat(xs @ fcD_w.T + D, HD, axis=-1)
            yz = y * jax.nn.silu(z)
            y = yz * jax.lax.rsqrt(jnp.mean(jnp.square(yz), -1, keepdims=True) + 1e-05) * norm_w
            return y @ out_w.T
        key = jax.random.key(seed)
        ks = jax.random.split(key, 12)
        rn = lambda k, shape, s=0.02: jax.random.normal(k, shape, jnp.float32) * s
        dt = jnp.exp(jax.random.uniform(ks[5], (NH,), jnp.float32, np.log(0.001), np.log(0.1)))
        return dict(x=jax.random.normal(ks[0], (SEQ, BATCH, HID), jnp.float32), w_down=rn(ks[1], (DM, HID)), b_down=jnp.zeros((DM,), jnp.float32), w_up=rn(ks[2], (HID, DM)), b_up=jnp.zeros((HID,), jnp.float32), gate1=jnp.asarray(0.6, jnp.float32), hy_in_w=rn(ks[3], (DIN_PROJ, DM)), hy_conv_w=rn(ks[4], (CONV_DIM, 1, DCONV), 0.2), hy_conv_b=jnp.zeros((CONV_DIM,), jnp.float32), hy_dt_bias=jnp.log(jnp.expm1(dt)), hy_A_log=jnp.log(jax.random.uniform(ks[6], (NH,), jnp.float32, 1.0, 16.0)), hy_D=jnp.ones((NH,), jnp.float32), hy_fcD_w=rn(ks[7], (NH, DIN)), hy_norm_w=jnp.ones((DIN,), jnp.float32), hy_out_w=rn(ks[8], (DM, DIN)))
    _L0_attn_b_in = _L0_attn_b_setup()

    def _L0_ffn_setup():
        import math
        import jax, jax.numpy as jnp
        import numpy as np
        SCALING = 16.0 / 32.0

        def real_fourier_orthogonal_multiply(c):
            n = c.shape[-1]
            sqrt_n = math.sqrt(n)
            pair_scale = math.sqrt(n / 2.0)
            max_f = (n - 1) // 2
            work = c.astype(jnp.float32)
            dc = (work[..., 0] * sqrt_n)[..., None].astype(jnp.complex64)
            cos = work[..., 1:1 + 2 * max_f:2] * pair_scale
            sin = work[..., 2:2 + 2 * max_f:2] * pair_scale
            mid = (cos - 1j * sin).astype(jnp.complex64)
            parts = [dc, mid]
            if n % 2 == 0:
                parts.append((work[..., -1] * sqrt_n)[..., None].astype(jnp.complex64))
            spectrum = jnp.concatenate(parts, axis=-1)
            return jnp.fft.irfft(spectrum, n=n, axis=-1).astype(c.dtype)
        key = jax.random.key(seed)
        ks = jax.random.split(key, 9)
        B, S, D_in, D_out, R0, R1, E = (4, 512, 1024, 1024, 32, 8, 3)
        x = jax.random.normal(ks[0], (B, S, D_in), dtype=jnp.float32)
        W_base = jax.random.normal(ks[1], (D_out, D_in), dtype=jnp.float32) * 0.02
        b_base = jax.random.normal(ks[2], (D_out,), dtype=jnp.float32) * 0.02
        enc0 = jax.random.normal(ks[3], (R0, D_in), dtype=jnp.float32) * 0.02
        enc1 = jax.random.normal(ks[4], (R1, D_in), dtype=jnp.float32) * 0.02
        coefs0 = jax.random.normal(ks[5], (E, D_out, R0), dtype=jnp.float32) * 0.02
        coefs1 = jax.random.normal(ks[6], (E, D_out, R1), dtype=jnp.float32) * 0.02
        mask0 = jax.random.randint(ks[7], (E, D_out, R0), 0, 2).astype(bool)
        mask1 = jax.random.randint(ks[8], (E, D_out, R1), 0, 2).astype(bool)
        return dict(x=x, W_base=W_base, b_base=b_base, enc0=enc0, enc1=enc1, coefs0=coefs0, coefs1=coefs1, mask0=mask0, mask1=mask1)
    _L0_ffn_in = _L0_ffn_setup()
    _d = {'L0_attn_a_x': _L0_attn_a_in['x'], 'L0_attn_a_wq_w': _L0_attn_a_in['wq_w'], 'L0_attn_a_wq_b': _L0_attn_a_in['wq_b'], 'L0_attn_a_wk_w': _L0_attn_a_in['wk_w'], 'L0_attn_a_wk_b': _L0_attn_a_in['wk_b'], 'L0_attn_a_wv_w': _L0_attn_a_in['wv_w'], 'L0_attn_a_wv_b': _L0_attn_a_in['wv_b'], 'L0_attn_a_wo_w': _L0_attn_a_in['wo_w'], 'L0_attn_a_wo_b': _L0_attn_a_in['wo_b'], 'L0_attn_b_w_down': _L0_attn_b_in['w_down'], 'L0_attn_b_b_down': _L0_attn_b_in['b_down'], 'L0_attn_b_w_up': _L0_attn_b_in['w_up'], 'L0_attn_b_b_up': _L0_attn_b_in['b_up'], 'L0_attn_b_gate1': _L0_attn_b_in['gate1'], 'L0_attn_b_hy_in_w': _L0_attn_b_in['hy_in_w'], 'L0_attn_b_hy_conv_w': _L0_attn_b_in['hy_conv_w'], 'L0_attn_b_hy_conv_b': _L0_attn_b_in['hy_conv_b'], 'L0_attn_b_hy_dt_bias': _L0_attn_b_in['hy_dt_bias'], 'L0_attn_b_hy_A_log': _L0_attn_b_in['hy_A_log'], 'L0_attn_b_hy_D': _L0_attn_b_in['hy_D'], 'L0_attn_b_hy_fcD_w': _L0_attn_b_in['hy_fcD_w'], 'L0_attn_b_hy_norm_w': _L0_attn_b_in['hy_norm_w'], 'L0_attn_b_hy_out_w': _L0_attn_b_in['hy_out_w'], 'L0_ffn_W_base': _L0_ffn_in['W_base'], 'L0_ffn_b_base': _L0_ffn_in['b_base'], 'L0_ffn_enc0': _L0_ffn_in['enc0'], 'L0_ffn_enc1': _L0_ffn_in['enc1'], 'L0_ffn_coefs0': _L0_ffn_in['coefs0'], 'L0_ffn_coefs1': _L0_ffn_in['coefs1'], 'L0_ffn_mask0': _L0_ffn_in['mask0'], 'L0_ffn_mask1': _L0_ffn_in['mask1']}
    _x0 = _d['L0_attn_a_x']
    _d['L0_attn_a_x'] = jax.random.normal(jax.random.fold_in(jax.random.key(seed), 1), (8, 512, 1024), dtype=_x0.dtype)
    del _x0
    return _d

def reference(L0_attn_a_x, L0_attn_a_wq_w, L0_attn_a_wq_b, L0_attn_a_wk_w, L0_attn_a_wk_b, L0_attn_a_wv_w, L0_attn_a_wv_b, L0_attn_a_wo_w, L0_attn_a_wo_b, L0_attn_b_w_down, L0_attn_b_b_down, L0_attn_b_w_up, L0_attn_b_b_up, L0_attn_b_gate1, L0_attn_b_hy_in_w, L0_attn_b_hy_conv_w, L0_attn_b_hy_conv_b, L0_attn_b_hy_dt_bias, L0_attn_b_hy_A_log, L0_attn_b_hy_D, L0_attn_b_hy_fcD_w, L0_attn_b_hy_norm_w, L0_attn_b_hy_out_w, L0_ffn_W_base, L0_ffn_b_base, L0_ffn_enc0, L0_ffn_enc1, L0_ffn_coefs0, L0_ffn_coefs1, L0_ffn_mask0, L0_ffn_mask1):

    def _L0_attn_a_ref(x, wq_w, wq_b, wk_w, wk_b, wv_w, wv_b, wo_w, wo_b):
        import jax, jax.numpy as jnp
        import numpy as np
        B, T, D = (2, 512, 1024)
        H = 32
        HKV = 1
        HD = D // H
        b, t, d = x.shape
        q = (x @ wq_w.T + wq_b).reshape(b, t, H, HD)
        k = (x @ wk_w.T + wk_b).reshape(b, t, HKV, HD)
        v = (x @ wv_w.T + wv_b).reshape(b, t, HKV, HD)
        k1 = k[:, :, 0, :]
        v1 = v[:, :, 0, :]
        scores = jnp.einsum('bqhd,bkd->bhqk', q, k1) / jnp.sqrt(jnp.float32(HD))
        causal = jnp.tril(jnp.ones((t, t), dtype=bool))
        scores = jnp.where(causal, scores, -jnp.inf)
        weights = jax.nn.softmax(scores, axis=-1)
        attn = jnp.einsum('bhqk,bkd->bqhd', weights, v1)
        attn = attn.reshape(b, t, H * HD)
        return attn @ wo_w.T + wo_b

    def _L0_attn_b_ref(x, w_down, b_down, w_up, b_up, gate1, hy_in_w, hy_conv_w, hy_conv_b, hy_dt_bias, hy_A_log, hy_D, hy_fcD_w, hy_norm_w, hy_out_w):
        import jax, jax.numpy as jnp
        import numpy as np
        HID = 1024
        DM = 128
        DIN = 2 * DM
        DST = 16
        HD = 64
        NH = DIN // HD
        DCONV = 7
        CONV_DIM = DIN + 2 * DST
        DIN_PROJ = 2 * DIN + 2 * DST + 2 * NH
        SEQ, BATCH = (512, 4)

        def _causal_conv(x, w, b):
            y = jax.lax.conv_general_dilated(jnp.transpose(x, (0, 2, 1)), w, (1,), [(DCONV - 1, 0)], feature_group_count=CONV_DIM, dimension_numbers=('NCH', 'OIH', 'NCH'))
            return jnp.transpose(y, (0, 2, 1)) + b

        def _ssm_scan(x, dt, A, B, C):
            dA = jnp.exp(dt * A)
            dBx = dt[..., None] * x

            def step(h, t):
                dA_t, dBx_t, B_t, C_t = t
                h = dA_t[:, :, None, None] * h + dBx_t[..., None] * B_t[:, None, None, :]
                y = jnp.einsum('bhpn,bn->bhp', h, C_t)
                return (h, y)
            h0 = jnp.zeros((x.shape[0], NH, HD, DST), x.dtype)
            _, ys = jax.lax.scan(step, h0, (jnp.moveaxis(dA, 1, 0), jnp.moveaxis(dBx, 1, 0), jnp.moveaxis(B, 1, 0), jnp.moveaxis(C, 1, 0)))
            return jnp.moveaxis(ys, 0, 1)

        def _hydra(u, in_w, conv_w, conv_b, dt_bias, A_log, D, fcD_w, norm_w, out_w):
            b, l, _ = u.shape
            zxbcdt = u @ in_w.T
            z = zxbcdt[..., :DIN]
            xBC = zxbcdt[..., DIN:DIN + CONV_DIM]
            dt2 = zxbcdt[..., DIN + CONV_DIM:]
            dt_fw = jax.nn.softplus(dt2[..., :NH] + dt_bias)
            dt_bw = jax.nn.softplus(jnp.flip(dt2[..., NH:], 1) + dt_bias)
            xBC = jax.nn.silu(_causal_conv(xBC, conv_w, conv_b))
            xs = xBC[..., :DIN]
            Bm = xBC[..., DIN:DIN + DST]
            Cm = xBC[..., DIN + DST:]
            A = -jnp.exp(A_log)
            x4 = xs.reshape(b, l, NH, HD)
            y_fw = _ssm_scan(x4, dt_fw, A, Bm, Cm).reshape(b, l, DIN)
            y_bw = jnp.flip(_ssm_scan(jnp.flip(x4, 1), dt_bw, A, jnp.flip(Bm, 1), jnp.flip(Cm, 1)).reshape(b, l, DIN), 1)
            zero = jnp.zeros((b, 1, DIN), u.dtype)
            y = jnp.concatenate([zero, y_fw[:, :-1]], 1) + jnp.concatenate([y_bw[:, 1:], zero], 1)
            y = y + xs * jnp.repeat(xs @ fcD_w.T + D, HD, axis=-1)
            yz = y * jax.nn.silu(z)
            y = yz * jax.lax.rsqrt(jnp.mean(jnp.square(yz), -1, keepdims=True) + 1e-05) * norm_w
            return y @ out_w.T
        x_init = x
        h = x @ w_down.T + b_down
        h = jnp.transpose(h, (1, 0, 2))
        h = jax.nn.gelu(h, approximate=False)
        xmid = h
        hp = (hy_in_w, hy_conv_w, hy_conv_b, hy_dt_bias, hy_A_log, hy_D, hy_fcD_w, hy_norm_w, hy_out_w)
        h = _hydra(h, *hp)
        h = _hydra(h, *hp)
        alpha = jax.nn.sigmoid(gate1)
        h = alpha * xmid + (1.0 - alpha) * h
        h = xmid + h
        h = h @ w_up.T + b_up
        return x_init + jnp.transpose(h, (1, 0, 2))

    def _L0_ffn_ref(x, W_base, b_base, enc0, enc1, coefs0, coefs1, mask0, mask1):
        import math
        import jax, jax.numpy as jnp
        import numpy as np
        SCALING = 16.0 / 32.0

        def real_fourier_orthogonal_multiply(c):
            n = c.shape[-1]
            sqrt_n = math.sqrt(n)
            pair_scale = math.sqrt(n / 2.0)
            max_f = (n - 1) // 2
            work = c.astype(jnp.float32)
            dc = (work[..., 0] * sqrt_n)[..., None].astype(jnp.complex64)
            cos = work[..., 1:1 + 2 * max_f:2] * pair_scale
            sin = work[..., 2:2 + 2 * max_f:2] * pair_scale
            mid = (cos - 1j * sin).astype(jnp.complex64)
            parts = [dc, mid]
            if n % 2 == 0:
                parts.append((work[..., -1] * sqrt_n)[..., None].astype(jnp.complex64))
            spectrum = jnp.concatenate(parts, axis=-1)
            return jnp.fft.irfft(spectrum, n=n, axis=-1).astype(c.dtype)
        base = jnp.einsum('bsd,od->bso', x, W_base) + b_base
        e0 = jnp.einsum('bsd,rd->bsr', x, enc0)
        e1 = jnp.einsum('bsd,rd->bsr', x, enc1)
        w0 = coefs0 * mask0.astype(coefs0.dtype)
        w1 = coefs1 * mask1.astype(coefs1.dtype)
        decoded = jnp.einsum('bsr,eor->ebso', e0, w0) + jnp.einsum('bsr,eor->ebso', e1, w1)
        transformed = real_fourier_orthogonal_multiply(decoded)
        update = transformed.sum(axis=0)
        return base + update * SCALING
    x = L0_attn_a_x
    x = x + _L0_attn_a_ref(_layernorm(x, axis=-1), L0_attn_a_wq_w, L0_attn_a_wq_b, L0_attn_a_wk_w, L0_attn_a_wk_b, L0_attn_a_wv_w, L0_attn_a_wv_b, L0_attn_a_wo_w, L0_attn_a_wo_b)
    x = x + _L0_ffn_ref(_layernorm(x, axis=-1), L0_ffn_W_base, L0_ffn_b_base, L0_ffn_enc0, L0_ffn_enc1, L0_ffn_coefs0, L0_ffn_coefs1, L0_ffn_mask0, L0_ffn_mask1)
    x = x + _L0_attn_b_ref(_layernorm(x, axis=-1), L0_attn_b_w_down, L0_attn_b_b_down, L0_attn_b_w_up, L0_attn_b_b_up, L0_attn_b_gate1, L0_attn_b_hy_in_w, L0_attn_b_hy_conv_w, L0_attn_b_hy_conv_b, L0_attn_b_hy_dt_bias, L0_attn_b_hy_A_log, L0_attn_b_hy_D, L0_attn_b_hy_fcD_w, L0_attn_b_hy_norm_w, L0_attn_b_hy_out_w)
    x = x + _L0_ffn_ref(_layernorm(x, axis=-1), L0_ffn_W_base, L0_ffn_b_base, L0_ffn_enc0, L0_ffn_enc1, L0_ffn_coefs0, L0_ffn_coefs1, L0_ffn_mask0, L0_ffn_mask1)
    return x

_drawn_inputs = setup_inputs


def setup_inputs(seed=0):
    import zlib

    import numpy as np

    out = dict(_drawn_inputs(seed))
    spreads = {'L0_attn_b_b_down': (0.0, 0.8),
     'L0_attn_b_b_up': (0.0, 0.1),
     'L0_attn_b_hy_conv_b': (0.0, 0.8),
     'L0_attn_b_hy_D': (1.0, 0.6),
     'L0_attn_b_hy_norm_w': (1.0, 0.6)}
    factors = {'L0_attn_a_wq_b': 8.0,
     'L0_attn_a_wk_b': 8.0,
     'L0_attn_a_wo_b': 3.198,
     'L0_attn_b_hy_in_w': 8.0,
     'L0_attn_b_hy_conv_w': 8.0,
     'L0_attn_b_hy_dt_bias': 8.0,
     'L0_attn_b_hy_A_log': 8.0,
     'L0_attn_b_hy_fcD_w': 8.0,
     'L0_attn_b_hy_out_w': 8.0}
    for name, (base, spread) in spreads.items():
        noise = np.random.default_rng([zlib.crc32(name.encode()), seed]).standard_normal(out[name].shape)
        drawn = base * np.exp(spread * noise) if base else spread * noise
        out[name] = jnp.asarray(drawn.astype(out[name].dtype))
    for name, factor in factors.items():
        out[name] = (out[name] * factor).astype(out[name].dtype)
    return out
```

```python
from contextlib import ExitStack

import concourse.bass as bass
from concourse import mybir

P = 128
EPS = 1e-5
ALU = mybir.AluOpType
ACT = mybir.ActivationFunctionType
AX = mybir.AxisListType
F32 = mybir.dt.float32
F32R = mybir.dt.float32r
BF16 = mybir.dt.bfloat16
U8 = mybir.dt.uint8
def attention_program(nc, x, wq_t, wkv_t, wo_t, bq, bkv, kv_scale, bo, ident, ident_b, causal_b, wq_split, x1):
    BATCH, T, D = x.shape
    HEAD = wkv_t.shape[1] // 4
    TILES, CH = T // P, D // P
    GROUPS, GH = D // P, P // HEAD
    UNITS = GROUPS * TILES * GH
    PER_GROUP = TILES * GH
    HALF = 512
    KROWS = 3 * HEAD
    S_RING, P_RING, T_RING, STAT = 3, 3, 2, 8
    T_LAG, AV_LAG = 3, 4
    PROJ = 3
    INV_AT, SPREAD_AT, COPY_AT, SCALE_AT, HIGH_AT, LOW_AT = 2, 10, 11, 12, 13, 14

    def unit(u):
        g, r = u // PER_GROUP, u % PER_GROUP
        return g, r // GH, r % GH, (r // GH + 1) * P

    with ExitStack() as ctx:
        def sb(name, shape, dt=F32):
            return ctx.enter_context(nc.sbuf_tensor(name, shape, dt))

        def sem(name):
            return ctx.enter_context(nc.semaphore(name))

        wo_hi, wo_lo = sb("wo_hi", [P, CH, D], F32R), sb("wo_lo", [P, CH, D], F32R)
        wkv_hi, wkv_lo = sb("wkv_hi", [P, CH, P], F32R), sb("wkv_lo", [P, CH, P], F32R)
        wq_hi, wq_lo = sb("wq_hi", [P, CH, P], F32R), sb("wq_lo", [P, CH, P], F32R)
        x_ring = sb("x_ring", [P, 2, D])
        r_ring = sb("r_ring", [P, 2, D])
        xn_hi, xn_lo = sb("xn_hi", [P, CH, T], F32R), sb("xn_lo", [P, CH, T], F32R)
        at_hi, at_lo = sb("at_hi", [P, CH, T], F32R), sb("at_lo", [P, CH, T], F32R)
        q_hi, q_lo = sb("q_hi", [P, T], F32R), sb("q_lo", [P, T], F32R)
        q_stack = sb("q_stack", [KROWS, 2, GH, T], F32R)
        k_stack = sb("k_stack", [KROWS, T], F32R)
        kv = sb("kv", [P, T])
        v_pad = sb("v_pad", [P, TILES, 7 * HEAD])
        probs = sb("probs", [P, P_RING, T])
        probs_t = sb("probs_t", [P, T_RING, T])
        neg_max = sb("neg_max", [P, STAT])
        den, inv_den = sb("den", [P, 2, TILES, GH]), sb("inv_den", [P, 2, TILES, GH])
        inv_rows, att = sb("inv_rows", [P, T]), sb("att", [P, T])
        stats, mean_var = sb("stats", [P, 2, 2, 6]), sb("mean_var", [P, 2, 2])
        var_eps, inv_std, neg_half = sb("var_eps", [P, 2]), sb("inv_std", [P, 2]), sb("neg_half", [P, 1])
        bo_rows = sb("bo_rows", [P, D])
        bq_sb, bkv_sb, kvs_sb, bkv_scaled = sb("bq_sb", [P, CH]), sb("bkv_sb", [P, 1]), sb("kvs_sb", [P, 1]), sb("bkv_scaled", [P, 1])
        ident_sb, identb_sb, causal_sb = sb("ident_sb", [P, P]), sb("identb_sb", [P, P], BF16), sb("causal_sb", [P, P], BF16)
        ps = ctx.enter_context(nc.psum_tensor("ps_attn", [P, 8, HALF], F32))

        params_in, stage_in, stage_used, staged_hi, staged_lo = (sem("params_in"), [sem("stage_in_0"), sem("stage_in_1")], sem("stage_used"),
                                                                 sem("staged_hi"), sem("staged_lo"))
        wq_out, setup_done, bkv_ready = sem("wq_out"), sem("setup_done"), sem("bkv_ready")
        DMA = 16
        STACK_DMAS = 3 * GH
        staged = [(wkv_t.rearrange("(c p) m -> p c m", p=P), wkv_hi[:, :, :], wkv_lo[:, :, :])]
        for w in (wq_t, wo_t):
            staged += [(w[c * P:(c + 1) * P, :], wo_hi[:, c, :], wo_lo[:, c, :]) for c in range(CH)]
        WQ_STAGED = 1 + CH

        def stage(n):
            s = r_ring[:, n % 2, :]
            return s.rearrange("p (c m) -> p c m", c=CH) if n == 0 else s

        with nc.Block() as block:
            @block.sync
            def _(sp):
                params = [(ident_sb[:, :], ident), (identb_sb[:, :], ident_b), (causal_sb[:, :], causal_b),
                          (bo_rows[:, :], bo), (bq_sb[:, :], bq), (bkv_sb[:, :], bkv), (kvs_sb[:, :], kv_scale)]
                for dst, src in params:
                    sp.dma_start(dst, src).then_inc(params_in, DMA)
                for n, (src, _, _) in enumerate(staged):
                    if n >= 2:
                        sp.wait_ge(staged_lo, n - 1)
                    sp.dma_start(stage(n), src).then_inc(stage_in[n % 2], DMA)
                    if n == WQ_STAGED - 1:
                        sp.wait_ge(staged_lo, WQ_STAGED)
                        for c in range(CH):
                            for part, w in ((0, wo_hi), (1, wo_lo)):
                                sp.dma_start(wq_split[part, :, :, c, :].rearrange("g p m -> p g m"),
                                             w[:, c, :].bitcast(F32).rearrange("p (g m) -> p g m", g=GROUPS)).then_inc(wq_out, DMA)
                        sp.wait_ge(wq_out, 2 * CH * DMA)

            @block.gpsimd
            def _(pool):
                nc.gpsimd.memset(neg_half[:, :], -0.5).then_inc(setup_done, 1)
                nc.gpsimd.memset(v_pad[:, :, :], 0.0).then_inc(setup_done, 1)
                pool.wait_ge(params_in, 7 * DMA)
                nc.gpsimd.tensor_tensor(bkv_scaled[:, :], bkv_sb[:, :], kvs_sb[:, :], ALU.mult).then_inc(bkv_ready, 1)
                pool.wait_ge(setup_done, 2)

            @block.scalar
            def _(act):
                for n, (_, hi, _) in enumerate(staged):
                    act.wait_ge(stage_in[n % 2], DMA * (n // 2 + 1))
                    if n == WQ_STAGED:
                        act.wait_ge(wq_out, 2 * CH * DMA)
                    nc.scalar.copy(hi, stage(n)).then_inc(staged_hi, 1)
                act.wait_ge(bkv_ready, 1)
                act.wait_ge(params_in, 7 * DMA)

            @block.vector
            def _(dve):
                for n, (_, hi, lo) in enumerate(staged):
                    dve.wait_ge(staged_hi, n + 1)
                    nc.vector.tensor_tensor(lo, stage(n), hi.bitcast(F32), ALU.subtract).then_inc(staged_lo, 1)
                dve.wait_ge(setup_done, 2)
                dve.wait_ge(params_in, 7 * DMA)

            @block.tensor
            def _(pe):
                pe.wait_ge(params_in, 7 * DMA)
                pe.wait_ge(staged_lo, len(staged))

        row_sems = []

        def row_sem(name):
            row_sems.append(sem(name))
            return row_sems[-1]

        x_in, stats_done, mv_done, eps_done, std_done, xn_done = ([row_sem("x_in_0"), row_sem("x_in_1")], row_sem("stats_done"), row_sem("mv_done"),
                                                                  row_sem("eps_done"), row_sem("std_done"), row_sem("xn_done"))
        xt_ready, xhi_done, xlo_done = row_sem("xt_ready"), row_sem("xhi_done"), row_sem("xlo_done")
        kv_ready, kv_done, khi_done, k_done, vt_ready, v_done = (row_sem("kv_ready"), row_sem("kv_done"), row_sem("khi_done"),
                                                                 row_sem("k_done"), row_sem("vt_ready"), row_sem("v_done"))
        wq_in, q_ready, qhi_done, qlo_done, qs_in = row_sem("wq_in"), row_sem("q_ready"), row_sem("qhi_done"), row_sem("qlo_done"), row_sem("qs_in")
        s_ready, max_done, exp_done, inv_done, wide_done, spread_ready, spread_done, att_done = (
            row_sem("s_ready"), row_sem("max_done"), row_sem("exp_done"), row_sem("inv_done"), row_sem("wide_done"), row_sem("spread_ready"),
            row_sem("spread_done"), row_sem("att_done"))
        pt_ready, pt_done, av_done, ohi_done, olo_done = (row_sem("pt_ready"), row_sem("pt_done"), row_sem("av_done"),
                                                          row_sem("ohi_done"), row_sem("olo_done"))
        r_in, r_bias, y_ready, y_used, x1_done, x1_out = ([row_sem("r_in_0"), row_sem("r_in_1")], row_sem("r_bias"), row_sem("y_ready"), row_sem("y_used"),
                                                          row_sem("x1_done"), [row_sem("x1_out_0"), row_sem("x1_out_1")])

        with nc.Fori(0, BATCH) as b:
            with nc.Block(no_gpsimd_drain=True) as block:

                @block.sync
                def _(sp):
                    def load_wq(g):
                        for part, w in ((0, wq_hi), (1, wq_lo)):
                            sp.dma_start(w[:, :, :].bitcast(F32), wq_split[part, g]).then_inc(wq_in, DMA)

                    for t in range(TILES):
                        if t >= 2:
                            sp.wait_ge(xt_ready, 2 * (t - 1))
                        sp.dma_start(x_ring[:, t % 2, :], x[b, t * P:(t + 1) * P, :]).then_inc(x_in[t % 2], DMA)
                    load_wq(0)
                    for g in range(GROUPS):
                        sp.wait_ge(qhi_done, g + 1)
                        if g >= 2:
                            sp.wait_ge(s_ready, (g - 1) * PER_GROUP)
                        sp.wait_ge(qlo_done, g + 1)
                        for j in range(GH):
                            rows = slice(j * HEAD, (j + 1) * HEAD)
                            for place, src in ((0, q_hi), (1, q_lo), (2, q_hi)):
                                sp.dma_start(q_stack[place * HEAD:(place + 1) * HEAD, g % 2, j, :].bitcast(F32),
                                             src[rows, :].bitcast(F32)).then_inc(qs_in, DMA)
                        if g + 1 < GROUPS:
                            load_wq(g + 1)
                    for t in range(TILES):
                        if t >= 2:
                            sp.wait_ge(x1_done, t - 1)
                            sp.dma_start(x1[b, (t - 2) * P:(t - 1) * P, :], r_ring[:, t % 2, :]).then_inc(x1_out[t % 2], DMA)
                            sp.wait_ge(x1_out[t % 2], (t // 2) * DMA)
                        sp.dma_start(r_ring[:, t % 2, :], x[b, t * P:(t + 1) * P, :]).then_inc(r_in[t % 2], DMA)
                    for t in range(TILES - 2, TILES):
                        sp.wait_ge(x1_done, t + 1)
                        sp.dma_start(x1[b, t * P:(t + 1) * P, :], r_ring[:, t % 2, :]).then_inc(x1_out[t % 2], DMA)
                    for n in range(2):
                            sp.wait_ge(x1_out[n], TILES // 2 * DMA)

                @block.gpsimd
                def _(pool):
                    for t in range(TILES):
                        pool.wait_ge(mv_done, t + 1)
                        nc.gpsimd.tensor_scalar(var_eps[:, t % 2:t % 2 + 1], mean_var[:, t % 2, 1:2], EPS, None,
                                                ALU.add).then_inc(eps_done, 1)
                        pool.wait_ge(eps_done, t + 1)
                        nc.gpsimd.tensor_tensor(inv_std[:, t % 2:t % 2 + 1], var_eps[:, t % 2:t % 2 + 1], neg_half[:, :],
                                                ALU.pow).then_inc(std_done, 1)
                    for g in range(GROUPS):
                        pool.wait_ge(inv_done, g + 1)
                        if g:
                            pool.wait_ge(olo_done, g)
                        nc.gpsimd.tensor_copy(att[:, :].rearrange("p (i j d) -> p i j d", i=TILES, j=GH),
                                              inv_den[:, g % 2, :, :, None].to_broadcast([P, TILES, GH, HEAD])).then_inc(wide_done, 1)
                    for t in range(TILES):
                        pool.wait_ge(r_in[t % 2], (t // 2 + 1) * DMA)
                        nc.gpsimd.tensor_tensor(r_ring[:, t % 2, :], r_ring[:, t % 2, :], bo_rows[:, :],
                                                ALU.add).then_inc(r_bias, 1)

                @block.scalar
                def _(act):
                    def q_high(g):
                        act.wait_ge(q_ready, g + 1)
                        if g:
                            act.wait_ge(qs_in, g * STACK_DMAS * DMA)
                        nc.scalar.activation(q_hi[:, :], ps[:, PROJ, :], ACT.Identity,
                                             bias=bq_sb[:, g:g + 1]).then_inc(qhi_done, 1)

                    def finish_copy(g):
                        act.wait_ge(spread_ready, g + 1)
                        if g:
                            act.wait_ge(att_done, g)
                        nc.scalar.copy(inv_rows[:, :], ps[:, PROJ, :]).then_inc(spread_done, 1)

                    def finish_high(g):
                        act.wait_ge(att_done, g + 1)
                        nc.scalar.copy(at_hi[:, g, :], att[:, :]).then_inc(ohi_done, 1)

                    for t in range(TILES):
                        for h in range(2):
                            act.wait_ge(xt_ready, 2 * t + h + 1)
                            nc.scalar.copy(xn_hi[:, 4 * h:4 * h + 4, t * P:(t + 1) * P],
                                           ps[:, h, :].rearrange("p (c t) -> p c t", t=P)).then_inc(xhi_done, 1)
                    act.wait_ge(kv_ready, 1)
                    nc.scalar.activation(kv[:, :], ps[:, PROJ, :], ACT.Identity, bias=bkv_scaled[:, :],
                                         scale=kvs_sb[:, :]).then_inc(kv_done, 1)
                    q_high(0)
                    for s in range(UNITS):
                        g, i, j, n = unit(s)
                        r = s % PER_GROUP
                        if r == 0 and g >= 2:
                            act.wait_ge(inv_done, g - 1)
                        act.wait_ge(max_done, s + 1)
                        if s >= P_RING:
                            act.wait_ge(pt_ready, s - P_RING + 1)
                        nc.scalar.activation(probs[:, s % P_RING, 0:n], ps[:, s % S_RING, 0:n], ACT.Exp,
                                             bias=neg_max[:, s % STAT:s % STAT + 1],
                                             accum_out=den[:, g % 2, i, j:j + 1]).then_inc(exp_done, 1)
                        if r == 9 and g + 1 < GROUPS:
                            q_high(g + 1)
                        if r == COPY_AT and g >= 1:
                            finish_copy(g - 1)
                        if r == HIGH_AT and g >= 1:
                            finish_high(g - 1)
                    finish_copy(GROUPS - 1)
                    finish_high(GROUPS - 1)

                @block.vector
                def _(dve):
                    def q_low(g):
                        dve.wait_ge(qhi_done, g + 1)
                        if g:
                            dve.wait_ge(qs_in, g * STACK_DMAS * DMA)
                        nc.vector.scalar_tensor_tensor(q_lo[:, :], ps[:, PROJ, :], bq_sb[:, g:g + 1],
                                                       q_hi[:, :].bitcast(F32), ALU.add, ALU.subtract).then_inc(qlo_done, 1)

                    def finish_inverse(g):
                        dve.wait_ge(exp_done, (g + 1) * PER_GROUP)
                        if g >= 2:
                            dve.wait_ge(wide_done, g - 1)
                        nc.vector.reciprocal(inv_den[:, g % 2, :, :], den[:, g % 2, :, :]).then_inc(inv_done, 1)

                    def finish_scale(g):
                        dve.wait_ge(av_done, (g + 1) * PER_GROUP)
                        dve.wait_ge(spread_done, g + 1)
                        if g:
                            dve.wait_ge(olo_done, g)
                        nc.vector.tensor_tensor(att[:, :], ps[:, 6 + g % 2, :], inv_rows[:, :], ALU.mult).then_inc(att_done, 1)

                    def finish_low(g):
                        dve.wait_ge(ohi_done, g + 1)
                        nc.vector.tensor_tensor(at_lo[:, g, :], att[:, :], at_hi[:, g, :].bitcast(F32),
                                                ALU.subtract).then_inc(olo_done, 1)

                    def x_low(t):
                        for h in range(2):
                            dve.wait_ge(xhi_done, 2 * t + h + 1)
                            cols = (slice(None), slice(4 * h, 4 * h + 4), slice(t * P, (t + 1) * P))
                            nc.vector.tensor_tensor(xn_lo[cols], ps[:, h, :].rearrange("p (c t) -> p c t", t=P),
                                                    xn_hi[cols].bitcast(F32), ALU.subtract).then_inc(xlo_done, 1)

                    for t in range(TILES):
                        dve.wait_ge(x_in[t % 2], (t // 2 + 1) * DMA)
                        for h in range(2):
                            nc.vector.bn_stats(stats[:, t % 2, h, :], x_ring[:, t % 2, h * HALF:(h + 1) * HALF]).then_inc(stats_done, 1)
                        dve.wait_ge(stats_done, (t + 1) * 2)
                        nc.vector.bn_aggr(mean_var[:, t % 2, :], stats[:, t % 2, :, :]).then_inc(mv_done, 1)
                        if t:
                            x_low(t - 1)
                        dve.wait_ge(mv_done, t + 1)
                        dve.wait_ge(std_done, t + 1)
                        nc.vector.tensor_scalar(x_ring[:, t % 2, :], x_ring[:, t % 2, :], mean_var[:, t % 2, 0:1],
                                                inv_std[:, t % 2:t % 2 + 1], ALU.subtract, ALU.mult).then_inc(xn_done, 1)
                    x_low(TILES - 1)
                    dve.wait_ge(kv_done, 1)
                    nc.vector.tensor_copy(k_stack[:, :], kv[0:KROWS, :]).then_inc(khi_done, 1)
                    dve.wait_ge(khi_done, 1)
                    low = slice(2 * HEAD, 3 * HEAD)
                    nc.vector.tensor_tensor(k_stack[low, :], kv[low, :], k_stack[low, :].bitcast(F32),
                                            ALU.subtract).then_inc(k_done, 1)
                    dve.wait_ge(vt_ready, 1)
                    nc.vector.tensor_copy(v_pad[:, :, 3 * HEAD:4 * HEAD],
                                          ps[:, 4, 0:TILES * HEAD].rearrange("p (k d) -> p k d", d=HEAD)).then_inc(v_done, 1)
                    q_low(0)
                    for s in range(UNITS + T_LAG):
                        if s < UNITS:
                            g, i, j, n = unit(s)
                            dve.wait_ge(s_ready, s + 1)
                            nc.vector.tensor_reduce(neg_max[:, s % STAT:s % STAT + 1], ps[:, s % S_RING, 0:n], AX.X,
                                                    ALU.max, negate=True).then_inc(max_done, 1)
                        if s % PER_GROUP == INV_AT and s >= PER_GROUP:
                            finish_inverse(s // PER_GROUP - 1)
                        if s >= T_LAG:
                            u = s - T_LAG
                            n = unit(u)[3]
                            dve.wait_ge(pt_ready, u + 1)
                            if u >= T_RING:
                                dve.wait_ge(av_done, u - T_RING + 1)
                            nc.vector.tensor_copy(probs_t[:, u % T_RING, 0:n], ps[:, 4 + u % T_RING, 0:n]).then_inc(pt_done, 1)
                        if s < UNITS and s % PER_GROUP == 9 and s // PER_GROUP + 1 < GROUPS:
                            q_low(s // PER_GROUP + 1)
                        if s >= PER_GROUP and s % PER_GROUP == SCALE_AT:
                            finish_scale(s // PER_GROUP - 1)
                        if s >= PER_GROUP and s % PER_GROUP == LOW_AT:
                            finish_low(s // PER_GROUP - 1)
                    finish_scale(GROUPS - 1)
                    finish_low(GROUPS - 1)
                    for t in range(TILES):
                        dve.wait_ge(r_bias, t + 1)
                        for h in range(2):
                            dve.wait_ge(y_ready, 2 * t + h + 1)
                            half = r_ring[:, t % 2, h * HALF:(h + 1) * HALF]
                            add = nc.vector.tensor_tensor(half, ps[:, h, :], half, ALU.add)
                            if h == 0:
                                add.then_inc(y_used, 1)
                            else:
                                add.then_inc(x1_done, 1)

                @block.tensor
                def _(pe):
                    def split_product(out, a_hi, a_lo, b_hi, b_lo, first, last):
                        nc.tensor.matmul(out, a_hi, b_hi, start=first, stop=False)
                        nc.tensor.matmul(out, a_lo, b_hi, start=False, stop=False)
                        return nc.tensor.matmul(out, a_hi, b_lo, start=False, stop=last)

                    def q_part(g, c):
                        if c == 0:
                            pe.wait_ge(wq_in, (g + 1) * 2 * DMA)
                            if g:
                                pe.wait_ge(qlo_done, g)
                                if g >= 3:
                                    pe.wait_ge(spread_done, g - 2)
                            else:
                                pe.wait_ge(kv_done, 1)
                        mm = split_product(ps[:, PROJ, :], wq_hi[:, c, :], wq_lo[:, c, :], xn_hi[:, c, :], xn_lo[:, c, :],
                                           c == 0, c == CH - 1)
                        if c == CH - 1:
                            mm.then_inc(q_ready, 1)

                    def finish_spread(g):
                        pe.wait_ge(wide_done, g + 1)
                        pe.wait_ge(qlo_done, min(g + 3, GROUPS))
                        if g:
                            pe.wait_ge(spread_done, g)
                        for i in range(TILES):
                            mm = nc.tensor.matmul(ps[:, PROJ, i * P:(i + 1) * P],
                                                  att[:, i * P:(i + 1) * P], ident_sb[:, :],
                                                  start=True, stop=True)
                        mm.then_inc(spread_ready, 1)

                    for t in range(TILES):
                        pe.wait_ge(xn_done, t + 1)
                        for h in range(2):
                            if t:
                                pe.wait_ge(xlo_done, 2 * (t - 1) + h + 1)
                            for c in range(4):
                                mm = nc.tensor.transpose(ps[:, h, c * P:(c + 1) * P],
                                                         x_ring[:, t % 2, (4 * h + c) * P:(4 * h + c + 1) * P], ident_sb[:, :])
                            mm.then_inc(xt_ready, 1)
                    pe.wait_ge(xlo_done, 2 * TILES)
                    for c in range(CH):
                        mm = split_product(ps[:, PROJ, :], wkv_hi[:, c, :], wkv_lo[:, c, :], xn_hi[:, c, :], xn_lo[:, c, :],
                                           c == 0, c == CH - 1)
                    mm.then_inc(kv_ready, 1)
                    pe.wait_ge(params_in, 7 * DMA)
                    pe.wait_ge(kv_done, 1)
                    for k in range(TILES):
                        mm = nc.tensor.transpose(ps[:, 4, k * HEAD:(k + 1) * HEAD], kv[3 * HEAD:4 * HEAD, k * P:(k + 1) * P],
                                                 ident_sb[3 * HEAD:4 * HEAD, 3 * HEAD:4 * HEAD])
                    mm.then_inc(vt_ready, 1)
                    for c in range(CH):
                        q_part(0, c)
                    pe.wait_ge(k_done, 1)
                    pe.wait_ge(v_done, 1)
                    for s in range(UNITS + AV_LAG):
                        if s < UNITS:
                            g, i, j, n = unit(s)
                            r = s % PER_GROUP
                            if r == 0:
                                pe.wait_ge(qs_in, (g + 1) * STACK_DMAS * DMA)
                            if s >= S_RING:
                                pe.wait_ge(exp_done, s - S_RING + 1)
                            nc.tensor.matmul(ps[:, s % S_RING, 0:n], q_stack[:, g % 2, j, i * P:(i + 1) * P],
                                             k_stack[:, 0:n], start=True, stop=False)
                            nc.tensor.matmul(ps[:, s % S_RING, n - P:n], identb_sb[:, :], causal_sb[:, :],
                                             start=False, stop=True).then_inc(s_ready, 1)
                            if r < CH and g + 1 < GROUPS:
                                q_part(g + 1, r)
                            if r == SPREAD_AT and g:
                                finish_spread(g - 1)
                        if T_LAG <= s < UNITS + T_LAG:
                            u = s - T_LAG
                            g, i, j, n = unit(u)
                            pe.wait_ge(exp_done, u + 1)
                            if u >= T_RING:
                                pe.wait_ge(pt_done, u - T_RING + 1)
                            for k in range(i + 1):
                                mm = nc.tensor.transpose(ps[:, 4 + u % T_RING, k * P:(k + 1) * P],
                                                         probs[:, u % P_RING, k * P:(k + 1) * P], ident_sb[:, :])
                            mm.then_inc(pt_ready, 1)
                        if s >= AV_LAG:
                            u = s - AV_LAG
                            g, i, j, n = unit(u)
                            pe.wait_ge(pt_done, u + 1)
                            if u % PER_GROUP == 0 and g >= 2:
                                pe.wait_ge(att_done, g - 1)
                            for k in range(i + 1):
                                lead = (GH - 1 - j) * HEAD
                                mm = nc.tensor.matmul(ps[:, 6 + g % 2, i * P:(i + 1) * P], v_pad[:, k, lead:lead + P],
                                                      probs_t[:, u % T_RING, k * P:(k + 1) * P],
                                                      start=(j == 0 and k == 0), stop=(j == GH - 1 and k == i))
                            mm.then_inc(av_done, 1)
                    finish_spread(GROUPS - 1)
                    pe.wait_ge(olo_done, GROUPS)
                    for t in range(TILES):
                        for h in range(2):
                            if t:
                                if h:
                                    pe.wait_ge(x1_done, t)
                                else:
                                    pe.wait_ge(y_used, t)
                            for c in range(CH):
                                tok = slice(t * P, (t + 1) * P)
                                out = slice(h * HALF, (h + 1) * HALF)
                                mm = split_product(ps[:, h, :], at_hi[:, c, tok], at_lo[:, c, tok], wo_hi[:, c, out],
                                                   wo_lo[:, c, out], c == 0, c == CH - 1)
                            mm.then_inc(y_ready, 1)
            nc.all_engine_barrier(sems_to_clear=range(row_sems[0].num, row_sems[-1].num + 1))


def mixer_program(nc, x1, w, c, out):
    L, T, D = x1.shape
    PB = P // L
    TILES = 4
    STEPS = T // (PB * TILES)
    CH = D // P
    HALF = 512
    COLS = TILES * P
    DM = 128
    DIN, NH, DST, TAPS = 2 * DM, 4, 16, 7
    HD = DIN // NH
    C_ROW = 32
    RANK = w["enc"].shape[0]
    EXPERTS = w["coefs"].shape[2]
    SCALING = 0.5
    SP_STEPS = 13
    DMA = 16
    NORMS = [(1, 0), (1, 1), (2, 0), (1, 2), (2, 1), (1, 3), (2, 2), (2, 3), (3, 0), (3, 1), (3, 2), (3, 3)]
    KIND2 = [e for e, (k, _) in enumerate(NORMS) if k == 2]
    GEMMS = [e for e, (k, _) in enumerate(NORMS) if k != 2]
    Y0, XT0, DOWN, UP0 = 0, 2, 4, 5

    with ExitStack() as ctx:
        def sb(name, shape, dt=F32):
            return ctx.enter_context(nc.sbuf_tensor("m_" + name, shape, dt))

        def sem(name):
            return ctx.enter_context(nc.semaphore("m_" + name))

        w_hi, w_lo = sb("w_hi", [P, CH, D], F32R), sb("w_lo", [P, CH, D], F32R)
        wd_hi, wd_lo = sb("wd_hi", [P, CH, DM], F32R), sb("wd_lo", [P, CH, DM], F32R)
        xs = sb("xs", [P, TILES, D])
        xn = sb("xn", [P, 2, D])
        xt_hi, xt_lo = sb("xt_hi", [P, 2, CH, P], F32R), sb("xt_lo", [P, 2, CH, P], F32R)
        stats, mean_var = sb("stats", [P, 2, 2, 6]), sb("mean_var", [P, 2, 2])
        var_eps, inv_std, neg_half = sb("var_eps", [P, 2]), sb("inv_std", [P, 2]), sb("neg_half", [P, TILES])
        h_mid, h_next, h_out, h_skip = sb("h_mid", [P, COLS]), sb("h_next", [P, COLS]), sb("h_out", [P, COLS]), sb("h_skip", [P, COLS])
        conv = sb("conv", [P, 3, COLS])
        x_feat = sb("x_feat", [P, 2, COLS])
        b_feat, c_feat = sb("b_feat", [DST, COLS]), sb("c_feat", [DST, COLS])
        x_tok, z_gate = sb("x_tok", [P, TILES, DIN]), sb("z_gate", [P, TILES, DIN])
        dt_raw, dt_tmp, dt, dta = (sb("dt_raw", [P, TILES, 2 * NH]), sb("dt_tmp", [P, TILES, 2 * NH]),
                                   sb("dt", [P, TILES, 2 * NH]), sb("dta", [P, TILES, 2 * NH]))
        sp_s, sp_s2, sp_t, sp_log = (sb(n, [P, TILES, 2 * NH]) for n in ("sp_s", "sp_s2", "sp_t", "sp_log"))
        dt_reach = sb("dt_reach", [P, TILES, 2 * NH, L])
        decay = sb("decay", [P, 2, TILES, NH, L])
        dt_mask = sb("dt_mask", [P, 2, TILES, NH, L])
        weight = sb("weight", [P, TILES, NH, L])
        d_term, d_diag = sb("d_term", [P, TILES, NH]), sb("d_diag", [P, TILES, NH, L])
        cb_fw, cb_bw, cb = sb("cb_fw", [P, TILES, P]), sb("cb_bw", [P, TILES, P]), sb("cb", [P, TILES, P])
        mixer = sb("mixer", [P, 2, NH, P])
        yz, square, sum_sq, y_std, y_inv = (sb("yz", [P, TILES, DIN]), sb("square", [P, DIN]), sb("sum_sq", [P, TILES]),
                                            sb("y_std", [P, TILES]), sb("y_inv", [P, TILES]))
        yn_feat = sb("yn_feat", [P, 2, COLS])
        enc, coef, mask, wsum3, wsum, basis = (sb("enc", [RANK, D]), sb("coef", [P, CH, EXPERTS, RANK]),
                                               sb("mask", [P, CH, EXPERTS, RANK], U8), sb("wsum3", [P, CH, EXPERTS, RANK]),
                                               sb("wsum", [P, CH, RANK]), sb("basis", [RANK, D]))
        names = ["up_t", "base_b", "up_b", "down_b", "gate", "wx_t", "wbc_t", "wz_t", "wdt_t", "conv_w", "conv_b", "dt_b",
                 "a_log", "d_row", "fcd_t", "norm_w", "wout_t"]
        par = {n: sb("p_" + n, list(w[n].shape)) for n in names}
        con = {n: sb("c_" + n, list(a.shape)) for n, a in c.items() if n != "dft_t"}
        a_row, wout, alpha, keep, skip = (sb("a_row", [P, 2 * NH]), sb("wout", [P, 2, DM]), sb("alpha", [P, 1]),
                                          sb("keep", [P, 1]), sb("skip", [P, 1]))
        ps = ctx.enter_context(nc.psum_tensor("ps_mixer", [P, 8, HALF], F32))
        PARAMS = (len(names) + len(con) + 3) * DMA

        params_in, stage_in = sem("params_in"), [sem("stage_in_0"), sem("stage_in_1")]
        wsum_step, wsum_done, basis_part, basis_ready, basis_done = (sem("wsum_step"), sem("wsum_done"), sem("basis_part"),
                                                                     sem("basis_ready"), sem("basis_done"))
        delta_ready, sum_done, whi_done, wlo_done = sem("delta_ready"), sem("sum_done"), sem("whi_done"), sem("wlo_done")
        setup, small, gate_exp, a_exp = sem("setup"), sem("small"), sem("gate_exp"), sem("a_exp")

        def stage(n):
            return xs[:, n % 2, :]

        with nc.Block() as block:
            @block.sync
            def _(sp):
                for n in names:
                    sp.dma_start(par[n][:], w[n]).then_inc(params_in, DMA)
                for n in con:
                    sp.dma_start(con[n][:], c[n]).then_inc(params_in, DMA)
                for dst, n in ((enc, "enc"), (coef, "coefs"), (mask, "masks")):
                    sp.dma_start(dst[:], w[n]).then_inc(params_in, DMA)
                for n in range(2 * CH + 1):
                    if 2 <= n < CH + 2:
                        if n - 2 < CH - 1:
                            sp.wait_ge(basis_part, n - 1)
                        else:
                            sp.wait_ge(basis_ready, 2)
                    elif n >= CH + 2:
                        sp.wait_ge(sum_done, n - CH - 1)
                    src = (c["dft_t"][n * P:(n + 1) * P, :] if n < CH else
                           w["base_t"][(n - CH) * P:(n - CH + 1) * P, :] if n < 2 * CH else w["down_t"])
                    sp.dma_start(stage(n), src).then_inc(stage_in[n % 2], DMA)

            @block.gpsimd
            def _(pool):
                nc.gpsimd.memset(neg_half[:, :], -0.5).then_inc(setup, 1)
                nc.gpsimd.memset(cb_fw[:, :, :], 0.0).then_inc(setup, 1)
                nc.gpsimd.memset(cb_bw[:, :, :], 0.0).then_inc(setup, 1)
                pool.wait_ge(setup, 3)

            @block.scalar
            def _(act):
                act.wait_ge(params_in, PARAMS)
                nc.scalar.activation(alpha[:, :], par["gate"][:, :], ACT.Exp, scale=-1.0).then_inc(gate_exp, 1)
                nc.scalar.activation(a_row[:, :], par["a_log"][:, :], ACT.Exp).then_inc(a_exp, 1)
                for n in range(CH + 1):
                    act.wait_ge(sum_done, n + 1)
                    if n < CH:
                        nc.scalar.copy(w_hi[:, n, :], xn[:, n % 2, :]).then_inc(whi_done, 1)
                    else:
                        nc.scalar.copy(wd_hi[:, :, :], xn[:, n % 2, :].rearrange("p (c m) -> p c m", c=CH)).then_inc(whi_done, 1)

            @block.vector
            def _(dve):
                dve.wait_ge(params_in, PARAMS)
                nc.vector.tensor_tensor(wsum3[:, :, :, :], coef[:, :, :, :], mask[:, :, :, :], ALU.mult).then_inc(wsum_step, 1)
                dve.wait_ge(wsum_step, 1)
                nc.vector.tensor_tensor(wsum[:, :, :], wsum3[:, :, 0, :], wsum3[:, :, 1, :], ALU.add).then_inc(wsum_step, 1)
                for n in range(2, EXPERTS):
                    dve.wait_ge(wsum_step, n)
                    nc.vector.tensor_tensor(wsum[:, :, :], wsum[:, :, :], wsum3[:, :, n, :], ALU.add).then_inc(
                        wsum_done if n == EXPERTS - 1 else wsum_step, 1)
                dve.wait_ge(gate_exp, 1)
                nc.vector.tensor_scalar(keep[:, :], alpha[:, :], 1.0, None, ALU.add).then_inc(small, 1)
                dve.wait_ge(small, 1)
                nc.vector.reciprocal(alpha[:, :], keep[:, :]).then_inc(small, 1)
                dve.wait_ge(small, 2)
                nc.vector.tensor_scalar(keep[:, :], alpha[:, :], -1.0, 1.0, ALU.mult, ALU.add).then_inc(small, 1)
                nc.vector.tensor_scalar(skip[:, :], alpha[:, :], 1.0, None, ALU.add).then_inc(small, 1)
                dve.wait_ge(a_exp, 1)
                nc.vector.tensor_scalar(a_row[:, :], a_row[:, :], -1.0, None, ALU.mult).then_inc(small, 1)
                for k in range(2):
                    nc.vector.tensor_scalar(wout[:, k, :], par["wout_t"][:, k, :], par["norm_w"][:, k:k + 1], None,
                                            ALU.mult).then_inc(small, 1)
                dve.wait_ge(basis_ready, 2)
                nc.vector.tensor_copy(basis[:, :].rearrange("r (h n) -> r h n", h=2), ps[0:RANK, 0:2, :]).then_inc(basis_done, 1)
                for n in range(CH + 1):
                    dve.wait_ge(stage_in[(n + CH) % 2], DMA * ((n + CH) // 2 + 1))
                    if n >= 2:
                        dve.wait_ge(wlo_done, n - 1)
                    if n < CH:
                        dve.wait_ge(delta_ready, 2 * (n + 1))
                        nc.vector.scalar_tensor_tensor(xn[:, n % 2, :].rearrange("p (h n) -> p h n", h=2),
                                                       ps[:, 2 + 2 * (n % 2):4 + 2 * (n % 2), :], SCALING,
                                                       stage(n + CH).rearrange("p (h n) -> p h n", h=2), ALU.mult, ALU.add
                                                       ).then_inc(sum_done, 1)
                    else:
                        nc.vector.tensor_copy(xn[:, n % 2, :], stage(n + CH)).then_inc(sum_done, 1)
                    dve.wait_ge(whi_done, n + 1)
                    if n < CH:
                        nc.vector.tensor_tensor(w_lo[:, n, :], xn[:, n % 2, :], w_hi[:, n, :].bitcast(F32),
                                                ALU.subtract).then_inc(wlo_done, 1)
                    else:
                        nc.vector.tensor_tensor(wd_lo[:, :, :], xn[:, n % 2, :].rearrange("p (c m) -> p c m", c=CH),
                                                wd_hi[:, :, :].bitcast(F32), ALU.subtract).then_inc(wlo_done, 1)

            @block.tensor
            def _(pe):
                pe.wait_ge(wsum_done, 1)
                for n in range(CH):
                    pe.wait_ge(stage_in[n % 2], DMA * (n // 2 + 1))
                    for h in range(2):
                        mm = nc.tensor.matmul(ps[0:RANK, h, :], wsum[:, n, :], stage(n)[:, h * HALF:(h + 1) * HALF],
                                              start=(n == 0), stop=(n == CH - 1))
                        if n == CH - 1:
                            mm.then_inc(basis_ready, 1)
                        elif h == 1:
                            mm.then_inc(basis_part, 1)
                pe.wait_ge(basis_done, 1)
                for n in range(CH):
                    if n >= 2:
                        pe.wait_ge(sum_done, n - 1)
                    for h in range(2):
                        nc.tensor.matmul(ps[:, 2 + 2 * (n % 2) + h, :], enc[:, n * P:(n + 1) * P],
                                         basis[:, h * HALF:(h + 1) * HALF], start=True, stop=True).then_inc(delta_ready, 1)

        step_sems = []

        def step_sem(name):
            step_sems.append(sem(name))
            return step_sems[-1]

        x_in = [step_sem(f"x_in_{t}") for t in range(TILES)]
        out_sent = step_sem("out_sent")
        stats_done, mv_done, eps_done, std_done, xn_done, post_done, up_bias = (
            step_sem("stats_done"), step_sem("mv_done"), step_sem("eps_done"), step_sem("std_done"), step_sem("xn_done"),
            step_sem("post_done"), step_sem("up_bias"))
        xt_ready, xhi_done, xlo_done = step_sem("xt_ready"), step_sem("xhi_done"), step_sem("xlo_done")
        y_ready, y_added, down_ready, h_done = step_sem("y_ready"), step_sem("y_added"), step_sem("down_ready"), step_sem("h_done")
        up_ready, up_added, skip_done = step_sem("up_ready"), step_sem("up_added"), step_sem("skip_done")
        xbc_ready, dt_ready, tap0_done, taps_done = (step_sem("xbc_ready"), step_sem("dt_ready"), step_sem("tap0_done"),
                                                     step_sem("taps_done"))
        dt_step, nabs_done, sp_exp, sp_inv, sp_step, sp_done, reach_done = (
            step_sem("dt_step"), step_sem("nabs_done"), step_sem("sp_exp"), step_sem("sp_inv"), step_sem("sp_step"), step_sem("sp_done"),
            step_sem("reach_done"))
        xf_done, bc_done, z_ready, z_done, xtok_ready, xtok_done = (step_sem("xf_done"), step_sem("bc_done"), step_sem("z_ready"),
                                                                    step_sem("z_done"), step_sem("xtok_ready"), step_sem("xtok_done"))
        cb_ready, cb_step, cb_done, decay_ready, decay_done, w_step, w_done = (
            step_sem("cb_ready"), step_sem("cb_step"), step_sem("cb_done"), step_sem("decay_ready"), step_sem("decay_done"),
            step_sem("w_step"), step_sem("w_done"))
        mixer_done, ym_ready, yz_done, sq_done, ystd_done, yinv_done, yn_done = (
            step_sem("mixer_done"), step_sem("ym_ready"), step_sem("yz_done"), step_sem("sq_done"), step_sem("ystd_done"),
            step_sem("yinv_done"), step_sem("yn_done"))
        yf_ready, yf_done, o_ready, h_new = step_sem("yf_ready"), step_sem("yf_done"), step_sem("o_ready"), step_sem("h_new")

        x1_v = x1.rearrange("l (i t b) d -> i t l b d", t=TILES, b=PB)
        out_v = out.rearrange("l (i t b) d -> i t l b d", t=TILES, b=PB)

        with nc.Fori(0, STEPS) as i:
            with nc.Block(no_gpsimd_drain=True) as block:
                @block.sync
                def _(sp):
                    for t in range(TILES):
                        sp.dma_start(xs[:, t, :], x1_v[i, t]).then_inc(x_in[t], DMA)
                    for t in range(TILES):
                        sp.wait_ge(y_added, 2 * (TILES + t + 1))
                        sp.dma_start(out_v[i, t], xs[:, t, :]).then_inc(out_sent, DMA)
                    sp.wait_ge(out_sent, TILES * DMA)

                @block.gpsimd
                def _(pool):
                    def inv_sqrt(e):
                        pool.wait_ge(mv_done, e + 1)
                        s = slice(e % 2, e % 2 + 1)
                        nc.gpsimd.tensor_scalar(var_eps[:, s], mean_var[:, e % 2, 1:2], EPS, None, ALU.add).then_inc(eps_done, 1)
                        pool.wait_ge(eps_done, e + 1)
                        nc.gpsimd.tensor_tensor(inv_std[:, s], var_eps[:, s], neg_half[:, 0:1], ALU.pow).then_inc(std_done, 1)

                    def post(e):
                        kind, t = NORMS[e]
                        pool.wait_ge(xn_done, e + 1)
                        if kind == 2:
                            nc.gpsimd.tensor_tensor(xs[:, t, :], xs[:, t, :], xn[:, e % 2, :], ALU.add).then_inc(up_bias, 1)
                            pool.wait_ge(up_bias, KIND2.index(e) + 1)
                        b = par["up_b"] if kind == 2 else par["base_b"]
                        nc.gpsimd.tensor_tensor(xs[:, t, :], xs[:, t, :], b[:, :], ALU.add).then_inc(post_done, 1)

                    def softplus(q):
                        step = [SP_STEPS * q]

                        def then(op):
                            op.then_inc(sp_step, 1)
                            step[0] += 1
                            pool.wait_ge(sp_step, step[0])

                        y, s, s2, t = dt_tmp[:, :, :], sp_s[:, :, :], sp_s2[:, :, :], sp_t[:, :, :]
                        pool.wait_ge(sp_inv, 2 * (q + 1))
                        then(nc.gpsimd.tensor_tensor(s, y, t, ALU.mult))
                        then(nc.gpsimd.tensor_tensor(s2, s, s, ALU.mult))
                        then(nc.gpsimd.tensor_scalar(t, s2, 1.0 / 13, 1.0 / 11, ALU.mult, ALU.add))
                        for n in (9, 7, 5, 3, 1):
                            then(nc.gpsimd.tensor_tensor(t, t, s2, ALU.mult))
                            then(nc.gpsimd.tensor_scalar(t, t, 1.0 / n, None, ALU.add))
                        nc.gpsimd.tensor_tensor(sp_log[:, :, :], t, s, ALU.mult).then_inc(sp_done, 1)

                    def hydra_inv_std(q):
                        pool.wait_ge(sq_done, TILES * (q + 1))
                        nc.gpsimd.tensor_scalar(y_std[:, :], sum_sq[:, :], 1.0 / DIN, EPS, ALU.mult, ALU.add).then_inc(ystd_done, 1)
                        pool.wait_ge(ystd_done, q + 1)
                        nc.gpsimd.tensor_tensor(y_inv[:, :], y_std[:, :], neg_half[:, :], ALU.pow).then_inc(yinv_done, 1)

                    first = [e for e in range(len(NORMS)) if NORMS[e][0] != 3]
                    for e in first:
                        inv_sqrt(e)
                        if e:
                            post(e - 1)
                    post(first[-1])
                    pool.wait_ge(h_done, TILES)
                    nc.gpsimd.tensor_scalar(h_skip[:, :], h_mid[:, :], skip[:, :], None, ALU.mult).then_inc(skip_done, 1)
                    for q in range(2):
                        softplus(q)
                        hydra_inv_std(q)
                    for e in range(len(first), len(NORMS)):
                        inv_sqrt(e)
                        if e > len(first):
                            post(e - 1)
                    post(len(NORMS) - 1)

                @block.scalar
                def _(act):
                    def x_high(e):
                        for h in range(2):
                            act.wait_ge(xt_ready, 2 * e + h + 1)
                            nc.scalar.copy(xt_hi[:, e % 2, 4 * h:4 * h + 4, :],
                                           ps[:, XT0 + h, :].rearrange("p (c t) -> p c t", t=P)).then_inc(xhi_done, 1)

                    def gelu(e):
                        t = NORMS[e][1]
                        act.wait_ge(down_ready, KIND2.index(e) + 1)
                        nc.scalar.activation(h_mid[:, t * P:(t + 1) * P], ps[:, DOWN, 0:P], ACT.Gelu,
                                             bias=par["down_b"][:, :]).then_inc(h_done, 1)

                    def hydra(q):
                        for m in range(3):
                            rows = slice(0, P if m < 2 else C_ROW + DST)
                            act.wait_ge(xbc_ready, 3 * q + m + 1)
                            nc.scalar.activation(conv[rows, m, :], ps[rows, 4 + m, :], ACT.Identity, bias=par["conv_b"][rows, m:m + 1],
                                                 scale=par["conv_w"][rows, m, TAPS - 1:TAPS]).then_inc(tap0_done, 1)
                        act.wait_ge(nabs_done, q + 1)
                        nc.scalar.activation(dt_tmp[:, :, :], dt_tmp[:, :, :], ACT.Exp).then_inc(sp_exp, 1)
                        for m in range(2):
                            act.wait_ge(taps_done, 3 * (TAPS - 1) * q + 3 * (TAPS - 2) + m + 1)
                            nc.scalar.activation(x_feat[:, m, :], conv[:, m, :], ACT.Silu).then_inc(xf_done, 1)
                        act.wait_ge(taps_done, 3 * (TAPS - 1) * (q + 1))
                        nc.scalar.activation(b_feat[:, :], conv[0:DST, 2, :], ACT.Silu).then_inc(bc_done, 1)
                        nc.scalar.activation(c_feat[:, :], conv[C_ROW:C_ROW + DST, 2, :], ACT.Silu).then_inc(bc_done, 1)
                        for k in range(2):
                            act.wait_ge(z_ready, 2 * q + k + 1)
                            nc.scalar.activation(z_gate[:, 2 * k:2 * k + 2, :], ps[:, 4 + k, :].rearrange("p (t n) -> p t n", t=2),
                                                 ACT.Silu).then_inc(z_done, 1)
                        act.wait_ge(decay_ready, q + 1)
                        nc.scalar.activation(decay[:, :, :, :, :].rearrange("p d t h l -> p (d t h l)"), ps[:, 5, 0:2 * TILES * NH * L],
                                             ACT.Exp).then_inc(decay_done, 1)
                        for t in range(TILES):
                            act.wait_ge(yz_done, TILES * q + t + 1)
                            if t or q:
                                act.wait_ge(sq_done, TILES * q + t)
                            nc.scalar.activation(square[:, :], yz[:, t, :], ACT.Square,
                                                 accum_out=sum_sq[:, t:t + 1]).then_inc(sq_done, 1)
                        for k in range(2):
                            act.wait_ge(yf_ready, 2 * q + k + 1)
                            nc.scalar.copy(yn_feat[:, k, :], ps[:, 4 + k, :]).then_inc(yf_done, 1)
                        if q == 0:
                            act.wait_ge(o_ready, 1)
                            nc.scalar.copy(h_next[:, :], ps[:, 6, :]).then_inc(h_new, 1)

                    first = [e for e in range(len(NORMS)) if NORMS[e][0] != 3]
                    for e in range(0, len(first), 2):
                        x_high(e)
                        x_high(e + 1)
                        for f in (e, e + 1):
                            if NORMS[f][0] == 2:
                                gelu(f)
                    hydra(0)
                    hydra(1)
                    for e in range(len(first), len(NORMS)):
                        x_high(e)

                @block.vector
                def _(dve):
                    def norm(e):
                        kind, t = NORMS[e]
                        if kind == 1:
                            dve.wait_ge(x_in[t], DMA)
                        elif kind == 2:
                            dve.wait_ge(y_added, 2 * (t + 1))
                        else:
                            dve.wait_ge(up_added, 2 * (t + 1))
                        for h in range(2):
                            nc.vector.bn_stats(stats[:, e % 2, h, :], xs[:, t, h * HALF:(h + 1) * HALF]).then_inc(stats_done, 1)
                        dve.wait_ge(stats_done, 2 * (e + 1))
                        nc.vector.bn_aggr(mean_var[:, e % 2, :], stats[:, e % 2, :, :]).then_inc(mv_done, 1)
                        dve.wait_ge(mv_done, e + 1)
                        dve.wait_ge(std_done, e + 1)
                        if e >= 2:
                            dve.wait_ge(xt_ready, 2 * (e - 1))
                            dve.wait_ge(post_done, e - 1)
                        nc.vector.tensor_scalar(xn[:, e % 2, :], xs[:, t, :], mean_var[:, e % 2, 0:1], inv_std[:, e % 2:e % 2 + 1],
                                                ALU.subtract, ALU.mult).then_inc(xn_done, 1)

                    def x_low(e):
                        for h in range(2):
                            dve.wait_ge(xhi_done, 2 * e + h + 1)
                            part = (slice(None), e % 2, slice(4 * h, 4 * h + 4), slice(None))
                            nc.vector.tensor_tensor(xt_lo[part], ps[:, XT0 + h, :].rearrange("p (c t) -> p c t", t=P),
                                                    xt_hi[part].bitcast(F32), ALU.subtract).then_inc(xlo_done, 1)

                    def add(e):
                        t, g = NORMS[e][1], GEMMS.index(e)
                        dve.wait_ge(post_done, e + 1)
                        for h in range(2):
                            dve.wait_ge(y_ready, 2 * g + h + 1)
                            half = xs[:, t, h * HALF:(h + 1) * HALF]
                            nc.vector.tensor_tensor(half, ps[:, Y0 + h, :], half, ALU.add).then_inc(y_added, 1)

                    def add_up(t):
                        dve.wait_ge(post_done, KIND2[t] + 1)
                        for h in range(2):
                            dve.wait_ge(up_ready, 2 * t + h + 1)
                            half = xs[:, t, h * HALF:(h + 1) * HALF]
                            nc.vector.tensor_tensor(half, ps[:, UP0 + h, :], half, ALU.add).then_inc(up_added, 1)

                    def hydra(q):
                        dve.wait_ge(dt_ready, TILES * (q + 1))
                        nc.vector.tensor_tensor(dt_raw[:, :, :], ps[:, 7, 0:TILES * 2 * NH].rearrange("p (t n) -> p t n", t=TILES),
                                                par["dt_b"][:, None, :].to_broadcast([P, TILES, 2 * NH]), ALU.add).then_inc(dt_step, 1)
                        dve.wait_ge(dt_step, 4 * q + 1)
                        nc.vector.scalar_tensor_tensor(dt_tmp[:, :, :], dt_raw[:, :, :], -1.0, dt_raw[:, :, :], ALU.mult,
                                                       ALU.min).then_inc(nabs_done, 1)
                        taps = 3 * (TAPS - 1) * q
                        for j in range(1, TAPS):
                            for m in range(3):
                                if j == 1:
                                    dve.wait_ge(tap0_done, 3 * q + m + 1)
                                else:
                                    dve.wait_ge(taps_done, taps + 3 * (j - 2) + m + 1)
                                rows = slice(0, P if m < 2 else C_ROW + DST)
                                acc = conv[rows, m, :].rearrange("p (t n) -> p t n", t=TILES)[:, :, j * PB:P]
                                nc.vector.scalar_tensor_tensor(
                                    acc, ps[rows, 4 + m, :].rearrange("p (t n) -> p t n", t=TILES)[:, :, 0:P - j * PB],
                                    par["conv_w"][rows, m, TAPS - 1 - j:TAPS - j], acc, ALU.mult, ALU.add).then_inc(taps_done, 1)
                            if j == 2:
                                dve.wait_ge(sp_exp, q + 1)
                                nc.vector.tensor_scalar(sp_t[:, :, :], dt_tmp[:, :, :], 2.0, None, ALU.add).then_inc(sp_inv, 1)
                            if j == 3:
                                dve.wait_ge(sp_inv, 2 * q + 1)
                                nc.vector.reciprocal(sp_t[:, :, :], sp_t[:, :, :]).then_inc(sp_inv, 1)
                        dve.wait_ge(sp_done, q + 1)
                        nc.vector.tensor_scalar(dt_raw[:, :, :], dt_raw[:, :, :], 0.0, None, ALU.max).then_inc(dt_step, 1)
                        dve.wait_ge(dt_step, 4 * q + 2)
                        nc.vector.scalar_tensor_tensor(dt[:, :, :], sp_log[:, :, :], 2.0, dt_raw[:, :, :], ALU.mult,
                                                       ALU.add).then_inc(dt_step, 1)
                        dve.wait_ge(dt_step, 4 * q + 3)
                        nc.vector.tensor_tensor(dta[:, :, :], dt[:, :, :], a_row[:, None, :].to_broadcast([P, TILES, 2 * NH]),
                                                ALU.mult).then_inc(dt_step, 1)
                        dve.wait_ge(dt_step, 4 * q + 4)
                        nc.vector.tensor_tensor(dt_reach[:, :, :, :], dta[:, :, :, None].to_broadcast([P, TILES, 2 * NH, L]),
                                                con["reach"][:, None, :, :].to_broadcast([P, TILES, 2 * NH, L]),
                                                ALU.mult).then_inc(reach_done, 1)
                        for d in range(2):
                            nc.vector.tensor_tensor(dt_mask[:, d, :, :, :],
                                                    dt[:, :, d * NH:(d + 1) * NH, None].to_broadcast([P, TILES, NH, L]),
                                                    con["side"][:, d, None, None, :].to_broadcast([P, TILES, NH, L]),
                                                    ALU.mult).then_inc(w_step, 1)
                        for k in range(2):
                            dve.wait_ge(xtok_ready, 2 * q + k + 1)
                            nc.vector.tensor_copy(x_tok[:, 2 * k:2 * k + 2, :],
                                                  ps[:, 6 + k, :].rearrange("p (t n) -> p t n", t=2)).then_inc(xtok_done, 1)
                        dve.wait_ge(cb_ready, q + 1)
                        cb_ps = ps[:, 4, :].rearrange("p (t n) -> p t n", t=TILES)
                        cut = P - PB
                        nc.vector.tensor_tensor(cb_fw[:, :, PB:P], cb_ps[:, :, 0:cut],
                                                con["before"][:, None, PB:P].to_broadcast([P, TILES, cut]), ALU.mult).then_inc(cb_step, 1)
                        nc.vector.tensor_tensor(cb_bw[:, :, 0:cut], cb_ps[:, :, PB:P],
                                                con["after"][:, None, 0:cut].to_broadcast([P, TILES, cut]), ALU.mult).then_inc(cb_step, 1)
                        dve.wait_ge(cb_step, 3 * q + 2)
                        nc.vector.tensor_tensor(cb[:, :, :], cb_fw[:, :, :], cb_bw[:, :, :], ALU.add).then_inc(cb_step, 1)
                        dve.wait_ge(cb_step, 3 * q + 3)
                        nc.vector.tensor_tensor(cb[:, :, :], cb[:, :, :], con["ident"][:, None, :].to_broadcast([P, TILES, P]),
                                                ALU.add).then_inc(cb_done, 1)
                        dve.wait_ge(decay_ready, q + 1)
                        dve.wait_ge(decay_done, q + 1)
                        nc.vector.tensor_tensor(d_term[:, :, :], ps[:, 5, 256:256 + TILES * NH].rearrange("p (t h) -> p t h", t=TILES),
                                                par["d_row"][:, None, :].to_broadcast([P, TILES, NH]), ALU.add).then_inc(w_step, 1)
                        nc.vector.tensor_tensor(decay[:, :, :, :, :].rearrange("p d t h l -> p (d t h l)"),
                                                decay[:, :, :, :, :].rearrange("p d t h l -> p (d t h l)"),
                                                dt_mask[:, :, :, :, :].rearrange("p d t h l -> p (d t h l)"), ALU.mult).then_inc(w_step, 1)
                        dve.wait_ge(w_step, 6 * q + 4)
                        nc.vector.tensor_tensor(d_diag[:, :, :, :], d_term[:, :, :, None].to_broadcast([P, TILES, NH, L]),
                                                con["same"][:, None, None, :].to_broadcast([P, TILES, NH, L]), ALU.mult).then_inc(w_step, 1)
                        nc.vector.tensor_tensor(weight[:, :, :, :], decay[:, 0, :, :, :], decay[:, 1, :, :, :], ALU.add).then_inc(w_step, 1)
                        dve.wait_ge(w_step, 6 * q + 6)
                        nc.vector.tensor_tensor(weight[:, :, :, :], weight[:, :, :, :], d_diag[:, :, :, :], ALU.add).then_inc(w_done, 1)
                        dve.wait_ge(w_done, q + 1)
                        dve.wait_ge(cb_done, q + 1)

                        def mix(t):
                            if t >= 2:
                                dve.wait_ge(ym_ready, TILES * q + t - 1)
                            nc.vector.tensor_tensor(
                                mixer[:, t % 2, :, :].rearrange("p h (l b) -> p h l b", b=PB),
                                cb[:, t, :].rearrange("p (l b) -> p l b", b=PB)[:, None, :, :].to_broadcast([P, NH, L, PB]),
                                weight[:, t, :, :, None].to_broadcast([P, NH, L, PB]), ALU.mult).then_inc(mixer_done, 1)

                        def gate(t):
                            dve.wait_ge(ym_ready, TILES * q + t + 1)
                            if t == 0:
                                dve.wait_ge(z_done, 2 * (q + 1))
                            nc.vector.tensor_tensor(yz[:, t, :], ps[:, 6 + t % 2, 0:DIN], z_gate[:, t, :], ALU.mult).then_inc(yz_done, 1)

                        mix(0)
                        for t in range(TILES):
                            if t + 1 < TILES:
                                mix(t + 1)
                            gate(t)
                        dve.wait_ge(yinv_done, q + 1)
                        for t in range(TILES):
                            nc.vector.tensor_scalar(yz[:, t, :], yz[:, t, :], y_inv[:, t:t + 1], None, ALU.mult).then_inc(yn_done, 1)
                        if q == 1:
                            dve.wait_ge(o_ready, 2)
                            dve.wait_ge(skip_done, 1)
                            nc.vector.scalar_tensor_tensor(h_out[:, :], ps[:, 6, :], keep[:, :], h_skip[:, :], ALU.mult,
                                                           ALU.add).then_inc(h_new, 1)

                    norm(0)
                    norm(1)
                    for e in range(0, 8, 2):
                        x_low(e)
                        x_low(e + 1)
                        for f in (e, e + 1):
                            if NORMS[f][0] != 2:
                                add(f)
                            if f + 2 < 8:
                                norm(f + 2)
                    hydra(0)
                    hydra(1)
                    add_up(0)
                    norm(8)
                    add_up(1)
                    norm(9)
                    x_low(8)
                    x_low(9)
                    add_up(2)
                    norm(10)
                    add(8)
                    add_up(3)
                    norm(11)
                    add(9)
                    x_low(10)
                    x_low(11)
                    add(10)
                    add(11)

                @block.tensor
                def _(pe):
                    def transposes(e):
                        pe.wait_ge(xn_done, e + 1)
                        for h in range(2):
                            if e:
                                pe.wait_ge(xlo_done, 2 * (e - 1) + h + 1)
                            for k in range(4):
                                mm = nc.tensor.transpose(ps[:, XT0 + h, k * P:(k + 1) * P],
                                                         xn[:, e % 2, (4 * h + k) * P:(4 * h + k + 1) * P], con["ident"][:, :])
                            mm.then_inc(xt_ready, 1)

                    def split_product(out, a_hi, a_lo, b_hi, b_lo, first, last):
                        nc.tensor.matmul(out, a_hi, b_hi, start=first, stop=False)
                        nc.tensor.matmul(out, a_lo, b_hi, start=False, stop=False)
                        return nc.tensor.matmul(out, a_hi, b_lo, start=False, stop=last)

                    def gemm(e):
                        g, s = GEMMS.index(e), e % 2
                        pe.wait_ge(xlo_done, 2 * (e + 1))
                        for h in range(2):
                            if g:
                                pe.wait_ge(y_added, 2 * (g - 1) + h + 1)
                            cols = slice(h * HALF, (h + 1) * HALF)
                            for k in range(CH):
                                mm = split_product(ps[:, Y0 + h, :], xt_hi[:, s, k, :], xt_lo[:, s, k, :], w_hi[:, k, cols],
                                                   w_lo[:, k, cols], k == 0, k == CH - 1)
                            mm.then_inc(y_ready, 1)

                    def down(e):
                        s, n = e % 2, KIND2.index(e)
                        pe.wait_ge(xlo_done, 2 * (e + 1))
                        if n:
                            pe.wait_ge(h_done, n)
                        for k in range(CH):
                            mm = split_product(ps[:, DOWN, 0:P], wd_hi[:, k, :], wd_lo[:, k, :], xt_hi[:, s, k, :],
                                               xt_lo[:, s, k, :], k == 0, k == CH - 1)
                        mm.then_inc(down_ready, 1)

                    def up(t):
                        for h in range(2):
                            if t:
                                pe.wait_ge(up_added, 2 * (t - 1) + h + 1)
                            nc.tensor.matmul(ps[:, UP0 + h, :], h_out[:, t * P:(t + 1) * P], par["up_t"][:, h * HALF:(h + 1) * HALF],
                                             start=True, stop=True).then_inc(up_ready, 1)

                    def hydra(q):
                        h = h_mid if q == 0 else h_next
                        if q == 0:
                            pe.wait_ge(h_done, TILES)
                        else:
                            pe.wait_ge(h_new, 1)
                        nc.tensor.matmul(ps[:, 4, :], par["wx_t"][:, 0:P], h[:, :], start=True, stop=True).then_inc(xbc_ready, 1)
                        nc.tensor.matmul(ps[:, 5, :], par["wx_t"][:, P:2 * P], h[:, :], start=True, stop=True).then_inc(xbc_ready, 1)
                        nc.tensor.matmul(ps[0:C_ROW + DST, 6, :], par["wbc_t"][:, :], h[:, :], start=True, stop=True).then_inc(xbc_ready, 1)
                        for t in range(TILES):
                            nc.tensor.matmul(ps[:, 7, t * 2 * NH:(t + 1) * 2 * NH], h[:, t * P:(t + 1) * P], par["wdt_t"][:, :],
                                             start=True, stop=True).then_inc(dt_ready, 1)
                        taps = 3 * (TAPS - 1) * q + 3 * (TAPS - 2)
                        for k in range(2):
                            pe.wait_ge(taps_done, taps + k + 1)
                            for t in range(2 * k, 2 * k + 2):
                                mm = nc.tensor.matmul(ps[:, 4 + k, (t % 2) * DIN:(t % 2 + 1) * DIN], h[:, t * P:(t + 1) * P],
                                                      par["wz_t"][:, :], start=True, stop=True)
                            mm.then_inc(z_ready, 1)
                        pe.wait_ge(xf_done, 2 * (q + 1))
                        for k in range(2):
                            if k == 0:
                                pe.wait_ge(taps_done, taps + 3)
                            else:
                                pe.wait_ge(dt_step, 4 * q + 1)
                            for t in range(2 * k, 2 * k + 2):
                                for m in range(2):
                                    mm = nc.tensor.transpose(ps[:, 6 + k, (t % 2) * DIN + m * P:(t % 2) * DIN + (m + 1) * P],
                                                             x_feat[:, m, t * P:(t + 1) * P], con["ident"][:, :])
                            mm.then_inc(xtok_ready, 1)
                        pe.wait_ge(bc_done, 2 * (q + 1))
                        pe.wait_ge(z_done, 2 * q + 1)
                        for t in range(TILES):
                            cols = slice(t * P, (t + 1) * P)
                            mm = nc.tensor.matmul(ps[:, 4, cols], b_feat[:, cols], c_feat[:, cols], start=True, stop=True)
                        mm.then_inc(cb_ready, 1)
                        pe.wait_ge(z_done, 2 * q + 2)
                        for t in range(TILES):
                            for m in range(2):
                                nc.tensor.matmul(ps[:, 5, 256 + t * NH:256 + (t + 1) * NH], x_feat[:, m, t * P:(t + 1) * P],
                                                 par["fcd_t"][:, m, :], start=(m == 0), stop=(m == 1))
                        pe.wait_ge(reach_done, q + 1)
                        for d, between in ((0, "later"), (1, "earlier")):
                            n = TILES * NH * L
                            mm = nc.tensor.matmul(ps[:, 5, d * n:(d + 1) * n], con[between][:, :],
                                                  dt_reach[:, :, d * NH:(d + 1) * NH, :].rearrange("p t h l -> p t (h l)"),
                                                  start=True, stop=True)
                        mm.then_inc(decay_ready, 1)
                        pe.wait_ge(xtok_done, 2 * (q + 1))
                        for t in range(TILES):
                            pe.wait_ge(mixer_done, TILES * q + t + 1)
                            if t >= 2:
                                pe.wait_ge(yz_done, TILES * q + t - 1)
                            for n in range(NH):
                                cols = slice(n * HD, (n + 1) * HD)
                                mm = nc.tensor.matmul(ps[:, 6 + t % 2, cols], mixer[:, t % 2, n, :], x_tok[:, t, cols],
                                                      start=True, stop=True)
                            mm.then_inc(ym_ready, 1)
                        pe.wait_ge(w_done, q + 1)
                        pe.wait_ge(yn_done, TILES * (q + 1))
                        for k in range(2):
                            for t in range(TILES):
                                mm = nc.tensor.transpose(ps[:, 4 + k, t * P:(t + 1) * P], yz[:, t, k * P:(k + 1) * P], con["ident"][:, :])
                            mm.then_inc(yf_ready, 1)
                        pe.wait_ge(yz_done, TILES * (q + 1))
                        for k in range(2):
                            pe.wait_ge(yf_done, 2 * q + k + 1)
                            mm = nc.tensor.matmul(ps[:, 6, :], wout[:, k, :], yn_feat[:, k, :], start=(k == 0), stop=(k == 1))
                        mm.then_inc(o_ready, 1)

                    for e in range(0, 8, 2):
                        transposes(e)
                        transposes(e + 1)
                        for f in (e, e + 1):
                            if NORMS[f][0] == 2:
                                down(f)
                            else:
                                gemm(f)
                    hydra(0)
                    hydra(1)
                    pe.wait_ge(h_new, 2)
                    up(0)
                    up(1)
                    transposes(8)
                    transposes(9)
                    gemm(8)
                    up(2)
                    gemm(9)
                    up(3)
                    transposes(10)
                    transposes(11)
                    gemm(10)
                    gemm(11)

            nc.all_engine_barrier(sems_to_clear=range(step_sems[0].num, step_sems[-1].num + 1))

def inverse_transform(n):
    import numpy as np

    k = np.arange(n)
    out = np.empty((n, n))
    out[0] = 1.0 / np.sqrt(n)
    for f in range(1, (n - 1) // 2 + 1):
        angle = 2.0 * np.pi * ((f * k) % n) / n
        out[2 * f - 1] = np.sqrt(2.0 / n) * np.cos(angle)
        out[2 * f] = np.sqrt(2.0 / n) * np.sin(angle)
    if n % 2 == 0:
        out[n - 1] = np.where(k % 2 == 0, 1.0, -1.0) / np.sqrt(n)
    return out.astype(np.float32)


def kernel(**inputs):
    import ml_dtypes
    import numpy as np
    import concourse.bacc as bacc
    from concourse import mybir as mb
    from concourse.bass_utils import run_bass_kernel_spmd as run

    f32, bf16 = np.float32, ml_dtypes.bfloat16
    a = {n: np.asarray(v) for n, v in inputs.items()}
    att = {n[len("L0_attn_a_"):]: v for n, v in a.items() if n.startswith("L0_attn_a_")}
    hyd = {n[len("L0_attn_b_"):]: v for n, v in a.items() if n.startswith("L0_attn_b_")}
    ffn = {n[len("L0_ffn_"):]: v for n, v in a.items() if n.startswith("L0_ffn_")}
    x = att["x"]
    L, T, D = x.shape
    head = att["wk_w"].shape[0]
    PB = P // L
    NH, DIN = hyd["hy_fcD_w"].shape
    DM = hyd["w_down"].shape[0]
    DST = (hyd["hy_in_w"].shape[0] - 2 * DIN - 2 * NH) // 2
    TAPS = hyd["hy_conv_w"].shape[2]
    C_ROW = 32

    def rows(v, n=P):
        return np.broadcast_to(v.reshape(1, -1), (n, v.size))

    def chunks(m):
        return m.reshape(-1, P, m.shape[1]).transpose(1, 0, 2)

    def bc_rows(m):
        out = np.zeros((C_ROW + DST,) + m.shape[1:], m.dtype)
        out[:DST], out[C_ROW:] = m[:DST], m[DST:]
        return out

    def conv_rows(m):
        out = np.zeros((P, 3, m.shape[1]), m.dtype)
        out[:, 0], out[:, 1], out[:C_ROW + DST, 2] = m[:P], m[P:2 * P], bc_rows(m[DIN:])
        return out

    row, pos = np.arange(P) // PB, np.arange(P) % PB
    t = np.arange(L)
    same_pos = pos[:, None] == pos[None, :]
    lt, gt = row[:, None] < row[None, :], row[:, None] > row[None, :]
    kv_scale = np.ones((P, 1), f32)
    kv_scale[:3 * head] = 1.0 / np.sqrt(f32(head))
    reach = np.stack([row[:, None] <= t - 1] * NH + [row[:, None] >= t + 1] * NH, 1)
    consts = {
        "ident": np.eye(P), "before": same_pos & lt, "after": same_pos & gt, "later": same_pos & gt,
        "earlier": same_pos & lt, "reach": reach, "side": np.stack([row[:, None] < t, row[:, None] > t], 1),
        "same": row[:, None] == t, "dft_t": inverse_transform(D),
    }
    consts = {n: v.astype(f32) for n, v in consts.items()}
    attn = {
        "x": x, "wq_t": att["wq_w"].T, "wkv_t": np.concatenate([att["wk_w"]] * 3 + [att["wv_w"]]).T, "wo_t": att["wo_w"].T,
        "bq": att["wq_b"].reshape(-1, P).T, "bkv": np.concatenate([att["wk_b"]] * 3 + [att["wv_b"]])[:, None],
        "kv_scale": kv_scale, "bo": rows(att["wo_b"]), "ident": consts["ident"], "ident_b": np.eye(P).astype(bf16),
        "causal_b": np.where(np.tril(np.ones((P, P), bool)), 0.0, -1e30).astype(bf16),
    }
    in_w = hyd["hy_in_w"]
    mix = {
        "base_t": ffn["W_base"].T, "enc": np.concatenate([ffn["enc0"], ffn["enc1"]]),
        "coefs": np.concatenate([ffn["coefs0"], ffn["coefs1"]], 2).transpose(1, 0, 2),
        "masks": np.concatenate([ffn["mask0"], ffn["mask1"]], 2).transpose(1, 0, 2),
        "base_b": rows(ffn["b_base"]), "up_t": hyd["w_up"].T, "up_b": rows(hyd["b_up"]), "down_b": hyd["b_down"][:, None],
        "down_t": chunks(hyd["w_down"].T).reshape(P, -1), "gate": rows(hyd["gate1"]),
        "wz_t": in_w[:DIN].T, "wx_t": in_w[DIN:2 * DIN].T, "wbc_t": bc_rows(in_w[2 * DIN:2 * DIN + 2 * DST]).T,
        "wdt_t": in_w[2 * DIN + 2 * DST:].T, "conv_w": conv_rows(hyd["hy_conv_w"][:, 0, :]),
        "conv_b": conv_rows(hyd["hy_conv_b"][:, None])[:, :, 0], "dt_b": rows(np.concatenate([hyd["hy_dt_bias"]] * 2)),
        "a_log": rows(np.concatenate([hyd["hy_A_log"]] * 2)), "d_row": rows(hyd["hy_D"]), "fcd_t": chunks(hyd["hy_fcD_w"].T),
        "norm_w": hyd["hy_norm_w"].reshape(-1, P).T, "wout_t": chunks(hyd["hy_out_w"].T),
    }
    mix["coefs"] = chunks(mix["coefs"].reshape(D, -1)).reshape(P, D // P, *mix["coefs"].shape[1:])
    mix["masks"] = chunks(mix["masks"].reshape(D, -1)).reshape(P, D // P, *mix["masks"].shape[1:])

    nc = bacc.Bacc("TRN2", target_bir_lowering=False, num_devices=1)
    arrays = {}

    def declare(group, prefix):
        aps = {}
        for n, v in group.items():
            v = arrays[prefix + n] = np.ascontiguousarray(v)
            aps[n] = nc.dram_tensor(prefix + n, v.shape, mb.dt.from_np(v.dtype), kind="ExternalInput").ap()
        return aps

    at, mx, cn = declare(attn, "in_a_"), declare(mix, "in_m_"), declare(consts, "in_c_")
    out = nc.dram_tensor("out_0", x.shape, F32, kind="ExternalOutput").ap()
    wq_split = nc.dram_tensor("wq_split", (2, D // P, P, D // P, P), F32).ap()
    x1 = nc.dram_tensor("x1", x.shape, F32).ap()
    attention_program(nc, *(at[n] for n in ("x", "wq_t", "wkv_t", "wo_t", "bq", "bkv", "kv_scale", "bo", "ident", "ident_b",
                                            "causal_b")), wq_split, x1)
    mixer_program(nc, x1, mx, cn, out)
    r = run(nc, [arrays], core_ids=[0])
    return r.results[0]["out_0"]
```

```python
from contextlib import ExitStack

import concourse.bass as bass
from concourse import mybir

P = 128
EPS = 1e-5
ALU = mybir.AluOpType
ACT = mybir.ActivationFunctionType
AX = mybir.AxisListType
F32 = mybir.dt.float32
F32R = mybir.dt.float32r
BF16 = mybir.dt.bfloat16
U8 = mybir.dt.uint8
def attention_program(nc, x, wq_t, wkv_t, wo_t, bq, bkv, kv_scale, bo, ident, ident_b, causal_b, wq_split, x1):
    BATCH, T, D = x.shape
    HEAD = wkv_t.shape[1] // 4
    TILES, CH = T // P, D // P
    GROUPS, GH = D // P, P // HEAD
    HALF = 512
    KROWS = 3 * HEAD
    FIT = [min(GH, TILES // (i + 1)) for i in range(TILES)]
    IN_GROUP = [(i, range(j, j + FIT[i])) for i in range(TILES) for j in range(0, GH, FIT[i])]
    PER_GROUP = len(IN_GROUP)
    UNITS = GROUPS * PER_GROUP
    S_RING, P_RING, T_RING, STAT = 3, 3, 2, 8
    T_LAG, AV_LAG = 2, 3
    KV, PROJ, XT0 = 2, 3, 4
    Q_UNITS = 3
    INV_AT, SPREAD_AT, COPY_AT, SCALE_AT, HIGH_AT, LOW_AT = 2, 8, 9, 9, 10, 10

    def unit(u):
        i, heads = IN_GROUP[u % PER_GROUP]
        return u // PER_GROUP, i, heads, (i + 1) * P

    def finishing(s, at):
        return s // PER_GROUP - 1 if s >= PER_GROUP and s % PER_GROUP == at else None

    with ExitStack() as ctx:
        def sb(name, shape, dt=F32):
            return ctx.enter_context(nc.sbuf_tensor(name, shape, dt))

        def sem(name):
            return ctx.enter_context(nc.semaphore(name))

        wo_hi, wo_lo = sb("wo_hi", [P, CH, D], F32R), sb("wo_lo", [P, CH, D], F32R)
        wkv_hi, wkv_lo = sb("wkv_hi", [P, CH, P], F32R), sb("wkv_lo", [P, CH, P], F32R)
        wq_hi, wq_lo = sb("wq_hi", [P, CH, P], F32R), sb("wq_lo", [P, CH, P], F32R)
        x_ring = sb("x_ring", [P, 2, D])
        r_ring = sb("r_ring", [P, 2, D])
        xn_hi, xn_lo = sb("xn_hi", [P, CH, T], F32R), sb("xn_lo", [P, CH, T], F32R)
        at_hi, at_lo = sb("at_hi", [P, CH, T], F32R), sb("at_lo", [P, CH, T], F32R)
        q_stack = sb("q_stack", [KROWS, 2, GH, T], F32R)
        k_stack = sb("k_stack", [KROWS, T], F32R)
        v_pad = sb("v_pad", [P, TILES, 7 * HEAD])
        probs = sb("probs", [P, P_RING, T])
        probs_t = sb("probs_t", [P, T_RING, T])
        neg_max = sb("neg_max", [P, STAT, GH])
        den, inv_den = sb("den", [P, 2, TILES, GH]), sb("inv_den", [P, 2, TILES, GH])
        inv_rows, att = sb("inv_rows", [P, T]), sb("att", [P, T])
        stats, mean_var = sb("stats", [P, 2, 2, 6]), sb("mean_var", [P, 2, 2])
        var_eps, inv_std, neg_half = sb("var_eps", [P, 2]), sb("inv_std", [P, 2]), sb("neg_half", [P, 1])
        bo_rows = sb("bo_rows", [P, D])
        bq_sb, bkv_sb, kvs_sb, bkv_scaled = sb("bq_sb", [P, CH]), sb("bkv_sb", [P, 1]), sb("kvs_sb", [P, 1]), sb("bkv_scaled", [P, 1])
        ident_sb, identb_sb, causal_sb = sb("ident_sb", [P, P]), sb("identb_sb", [P, P], BF16), sb("causal_sb", [P, P], BF16)
        ps = ctx.enter_context(nc.psum_tensor("ps_attn", [P, 8, HALF], F32))

        params_in, stage_in, stage_used, staged_hi, staged_lo = (sem("params_in"), [sem("stage_in_0"), sem("stage_in_1")], sem("stage_used"),
                                                                 sem("staged_hi"), sem("staged_lo"))
        wq_out, setup_done, bkv_ready = sem("wq_out"), sem("setup_done"), sem("bkv_ready")
        DMA = 16
        staged = [(wkv_t.rearrange("(c p) m -> p c m", p=P), wkv_hi[:, :, :], wkv_lo[:, :, :])]
        for w in (wq_t, wo_t):
            staged += [(w[c * P:(c + 1) * P, :], wo_hi[:, c, :], wo_lo[:, c, :]) for c in range(CH)]
        WQ_STAGED = 1 + CH

        def stage(n):
            s = r_ring[:, n % 2, :]
            return s.rearrange("p (c m) -> p c m", c=CH) if n == 0 else s

        with nc.Block() as block:
            @block.sync
            def _(sp):
                params = [(ident_sb[:, :], ident), (identb_sb[:, :], ident_b), (causal_sb[:, :], causal_b),
                          (bo_rows[:, :], bo), (bq_sb[:, :], bq), (bkv_sb[:, :], bkv), (kvs_sb[:, :], kv_scale)]
                for dst, src in params:
                    sp.dma_start(dst, src).then_inc(params_in, DMA)
                for n, (src, _, _) in enumerate(staged):
                    if n >= 2:
                        sp.wait_ge(staged_lo, n - 1)
                    sp.dma_start(stage(n), src).then_inc(stage_in[n % 2], DMA)
                    if n == WQ_STAGED - 1:
                        sp.wait_ge(staged_lo, WQ_STAGED)
                        for c in range(CH):
                            for part, w in ((0, wo_hi), (1, wo_lo)):
                                sp.dma_start(wq_split[part, :, :, c, :].rearrange("g p m -> p g m"),
                                             w[:, c, :].bitcast(F32).rearrange("p (g m) -> p g m", g=GROUPS)).then_inc(wq_out, DMA)
                        sp.wait_ge(wq_out, 2 * CH * DMA)

            @block.gpsimd
            def _(pool):
                nc.gpsimd.memset(neg_half[:, :], -0.5).then_inc(setup_done, 1)
                nc.gpsimd.memset(v_pad[:, :, :], 0.0).then_inc(setup_done, 1)
                pool.wait_ge(params_in, 7 * DMA)
                nc.gpsimd.tensor_tensor(bkv_scaled[:, :], bkv_sb[:, :], kvs_sb[:, :], ALU.mult).then_inc(bkv_ready, 1)
                pool.wait_ge(setup_done, 2)

            @block.scalar
            def _(act):
                for n, (_, hi, _) in enumerate(staged):
                    act.wait_ge(stage_in[n % 2], DMA * (n // 2 + 1))
                    if n == WQ_STAGED:
                        act.wait_ge(wq_out, 2 * CH * DMA)
                    nc.scalar.copy(hi, stage(n)).then_inc(staged_hi, 1)
                act.wait_ge(bkv_ready, 1)
                act.wait_ge(params_in, 7 * DMA)

            @block.vector
            def _(dve):
                for n, (_, hi, lo) in enumerate(staged):
                    dve.wait_ge(staged_hi, n + 1)
                    nc.vector.tensor_tensor(lo, stage(n), hi.bitcast(F32), ALU.subtract).then_inc(staged_lo, 1)
                dve.wait_ge(setup_done, 2)
                dve.wait_ge(params_in, 7 * DMA)

            @block.tensor
            def _(pe):
                pe.wait_ge(params_in, 7 * DMA)
                pe.wait_ge(staged_lo, len(staged))

        row_sems = []

        def row_sem(name):
            row_sems.append(sem(name))
            return row_sems[-1]

        x_in, stats_done, mv_done, eps_done, std_done, xn_done = ([row_sem("x_in_0"), row_sem("x_in_1")], row_sem("stats_done"), row_sem("mv_done"),
                                                                  row_sem("eps_done"), row_sem("std_done"), row_sem("xn_done"))
        xt_ready, xhi_done, xlo_done = row_sem("xt_ready"), row_sem("xhi_done"), row_sem("xlo_done")
        kv_ready, kv_done, khi_done, k_done, vt_ready, v_done = (row_sem("kv_ready"), row_sem("kv_done"), row_sem("khi_done"),
                                                                 row_sem("k_done"), row_sem("vt_ready"), row_sem("v_done"))
        wq_in, q_ready, qhi_done, qlo_done, qre_in = (row_sem("wq_in"), row_sem("q_ready"), row_sem("qhi_done"), row_sem("qlo_done"),
                                                        row_sem("qre_in"))
        s_ready, max_done, exp_done, inv_done, wide_done, spread_ready, spread_done, att_done = (
            row_sem("s_ready"), row_sem("max_done"), row_sem("exp_done"), row_sem("inv_done"), row_sem("wide_done"), row_sem("spread_ready"),
            row_sem("spread_done"), row_sem("att_done"))
        pt_ready, pt_done, av_done, ohi_done, olo_done = (row_sem("pt_ready"), row_sem("pt_done"), row_sem("av_done"),
                                                          row_sem("ohi_done"), row_sem("olo_done"))
        r_in, r_bias, y_ready, y_used, x1_done, x1_out = ([row_sem("r_in_0"), row_sem("r_in_1")], row_sem("r_bias"), row_sem("y_ready"), row_sem("y_used"),
                                                          row_sem("x1_done"), [row_sem("x1_out_0"), row_sem("x1_out_1")])

        def row(b, nxt):
            def q_count(g):
                return g if b is not None else g - GROUPS + 1

            def wq_count(g):
                return g - 1 if b is not None else g - GROUPS + 1

            with nc.Block(no_gpsimd_drain=True) as block:

                @block.sync
                def _(sp):
                    def load_x(t):
                        if t >= 2:
                            sp.wait_ge(xt_ready, 2 * (t - 1))
                        sp.dma_start(x_ring[:, t % 2, :], x[nxt, t * P:(t + 1) * P, :]).then_inc(x_in[t % 2], DMA)

                    def load_wq(g):
                        if b is not None or g > GROUPS:
                            sp.wait_ge(q_ready, q_count(g - 1))
                        for part, w in ((0, wq_hi), (1, wq_lo)):
                            sp.dma_start(w[:, :, :].bitcast(F32), wq_split[part, g % GROUPS]).then_inc(wq_in, DMA)

                    def q_repeat(g):
                        sp.wait_ge(qhi_done, q_count(g) * GH)
                        if 2 <= g < GROUPS:
                            sp.wait_ge(s_ready, (g - 1) * PER_GROUP)
                        sp.dma_start(q_stack[2 * HEAD:3 * HEAD, g % 2, :, :].bitcast(F32),
                                     q_stack[0:HEAD, g % 2, :, :].bitcast(F32)).then_inc(qre_in, DMA)

                    def load_r(t):
                        if t >= 2:
                            sp.wait_ge(x1_out[t % 2], (t // 2) * DMA)
                        sp.dma_start(r_ring[:, t % 2, :], x[b, t * P:(t + 1) * P, :]).then_inc(r_in[t % 2], DMA)

                    def store(t):
                        sp.wait_ge(x1_done, t + 1)
                        sp.dma_start(x1[b, t * P:(t + 1) * P, :], r_ring[:, t % 2, :]).then_inc(x1_out[t % 2], DMA)

                    if nxt is not None:
                        load_x(0)
                        load_x(1)
                    if b is not None:
                        load_r(0)
                        load_r(1)
                        for g in range(1, GROUPS):
                            if g + 1 < GROUPS or nxt is not None:
                                load_wq(g + 1)
                            q_repeat(g)
                    elif nxt is not None:
                        load_wq(GROUPS)
                    if nxt is not None:
                        load_x(2)
                        load_x(3)
                    if b is not None:
                        store(0)
                        load_r(2)
                        store(1)
                        load_r(3)
                    if nxt is not None:
                        load_wq(GROUPS + 1)
                        q_repeat(GROUPS)
                    if b is not None:
                        store(2)
                        store(3)
                        for n in range(2):
                            sp.wait_ge(x1_out[n], TILES // 2 * DMA)
                    if nxt is not None:
                        sp.wait_ge(wq_in, wq_count(GROUPS + 1) * 2 * DMA)
                        sp.wait_ge(qre_in, q_count(GROUPS) * DMA)

                @block.gpsimd
                def _(pool):
                    def inv_sqrt(t):
                        pool.wait_ge(mv_done, t + 1)
                        nc.gpsimd.tensor_scalar(var_eps[:, t % 2:t % 2 + 1], mean_var[:, t % 2, 1:2], EPS, None,
                                                ALU.add).then_inc(eps_done, 1)
                        pool.wait_ge(eps_done, t + 1)
                        nc.gpsimd.tensor_tensor(inv_std[:, t % 2:t % 2 + 1], var_eps[:, t % 2:t % 2 + 1], neg_half[:, :],
                                                ALU.pow).then_inc(std_done, 1)

                    def widen(g):
                        pool.wait_ge(inv_done, g + 1)
                        if g:
                            pool.wait_ge(olo_done, g)
                        nc.gpsimd.tensor_copy(att[:, :].rearrange("p (i j d) -> p i j d", i=TILES, j=GH),
                                              inv_den[:, g % 2, :, :, None].to_broadcast([P, TILES, GH, HEAD])).then_inc(wide_done, 1)

                    def add_bias(t):
                        pool.wait_ge(r_in[t % 2], (t // 2 + 1) * DMA)
                        nc.gpsimd.tensor_tensor(r_ring[:, t % 2, :], r_ring[:, t % 2, :], bo_rows[:, :],
                                                ALU.add).then_inc(r_bias, 1)

                    if b is not None:
                        add_bias(0)
                        add_bias(1)
                        for g in range(GROUPS - 1):
                            widen(g)
                    if nxt is not None:
                        inv_sqrt(0)
                        inv_sqrt(1)
                    if b is not None:
                        widen(GROUPS - 1)
                    if nxt is not None:
                        inv_sqrt(2)
                        inv_sqrt(3)
                    if b is not None:
                        add_bias(2)
                        add_bias(3)

                @block.scalar
                def _(act):
                    def q_high(g, j):
                        if j == 0:
                            act.wait_ge(q_ready, q_count(g))
                            if 2 <= g < GROUPS:
                                act.wait_ge(s_ready, (g - 1) * PER_GROUP)
                        rows = slice(j * HEAD, (j + 1) * HEAD)
                        nc.scalar.activation(q_stack[0:HEAD, g % 2, j, :], ps[rows, PROJ, :], ACT.Identity,
                                             bias=bq_sb[rows, g % GROUPS:g % GROUPS + 1]).then_inc(qhi_done, 1)

                    def finish_copy(g):
                        act.wait_ge(spread_ready, g + 1)
                        if g:
                            act.wait_ge(att_done, g)
                        nc.scalar.copy(inv_rows[:, :], ps[:, PROJ, :]).then_inc(spread_done, 1)

                    def finish_high(g):
                        act.wait_ge(att_done, g + 1)
                        nc.scalar.copy(at_hi[:, g, :], att[:, :]).then_inc(ohi_done, 1)

                    def x_high(t):
                        for h in range(2):
                            act.wait_ge(xt_ready, 2 * t + h + 1)
                            nc.scalar.copy(xn_hi[:, 4 * h:4 * h + 4, t * P:(t + 1) * P],
                                           ps[:, XT0 + h, :].rearrange("p (c t) -> p c t", t=P)).then_inc(xhi_done, 1)

                    if b is not None:
                        for s in range(UNITS):
                            g, i, heads, n = unit(s)
                            if s % PER_GROUP == 0 and g >= 2:
                                act.wait_ge(inv_done, g - 1)
                            act.wait_ge(max_done, s + 1)
                            if s >= P_RING:
                                act.wait_ge(pt_ready, s - P_RING + 1)
                            for m, j in enumerate(heads):
                                exp = nc.scalar.activation(probs[:, s % P_RING, m * n:(m + 1) * n],
                                                           ps[:, s % S_RING, m * n:(m + 1) * n], ACT.Exp,
                                                           bias=neg_max[:, s % STAT, m:m + 1], accum_out=den[:, g % 2, i, j:j + 1])
                            exp.then_inc(exp_done, 1)
                            if g + 1 < GROUPS and 0 <= s % PER_GROUP - Q_UNITS < GH:
                                q_high(g + 1, s % PER_GROUP - Q_UNITS)
                            if (done := finishing(s, COPY_AT)) is not None:
                                finish_copy(done)
                            if (done := finishing(s, HIGH_AT)) is not None:
                                finish_high(done)
                    if nxt is not None:
                        x_high(0)
                    if b is not None:
                        finish_copy(GROUPS - 1)
                    if nxt is not None:
                        x_high(1)
                    if b is not None:
                        finish_high(GROUPS - 1)
                    if nxt is not None:
                        x_high(2)
                        x_high(3)
                        act.wait_ge(kv_ready, 1)
                        if b is not None:
                            act.wait_ge(olo_done, GROUPS)
                        nc.scalar.activation(att[:, :], ps[:, KV, :], ACT.Identity, bias=bkv_scaled[:, :],
                                             scale=kvs_sb[:, :]).then_inc(kv_done, 1)
                        for j in range(GH):
                            q_high(GROUPS, j)

                @block.vector
                def _(dve):
                    def q_low(g, j):
                        dve.wait_ge(qhi_done, (q_count(g) - 1) * GH + j + 1)
                        rows = slice(j * HEAD, (j + 1) * HEAD)
                        nc.vector.scalar_tensor_tensor(q_stack[HEAD:2 * HEAD, g % 2, j, :], ps[rows, PROJ, :],
                                                       bq_sb[rows, g % GROUPS:g % GROUPS + 1],
                                                       q_stack[0:HEAD, g % 2, j, :].bitcast(F32), ALU.add, ALU.subtract
                                                       ).then_inc(qlo_done, 1)

                    def finish_inverse(g):
                        dve.wait_ge(exp_done, (g + 1) * PER_GROUP)
                        if g >= 2:
                            dve.wait_ge(wide_done, g - 1)
                        nc.vector.reciprocal(inv_den[:, g % 2, :, :], den[:, g % 2, :, :]).then_inc(inv_done, 1)

                    def finish_scale(g):
                        dve.wait_ge(av_done, (g + 1) * PER_GROUP)
                        dve.wait_ge(spread_done, g + 1)
                        if g:
                            dve.wait_ge(olo_done, g)
                        nc.vector.tensor_tensor(att[:, :], ps[:, 6 + g % 2, :], inv_rows[:, :], ALU.mult).then_inc(att_done, 1)

                    def finish_low(g):
                        dve.wait_ge(ohi_done, g + 1)
                        nc.vector.tensor_tensor(at_lo[:, g, :], att[:, :], at_hi[:, g, :].bitcast(F32),
                                                ALU.subtract).then_inc(olo_done, 1)

                    def moments(t):
                        dve.wait_ge(x_in[t % 2], (t // 2 + 1) * DMA)
                        for h in range(2):
                            nc.vector.bn_stats(stats[:, t % 2, h, :], x_ring[:, t % 2, h * HALF:(h + 1) * HALF]).then_inc(stats_done, 1)
                        dve.wait_ge(stats_done, (t + 1) * 2)
                        nc.vector.bn_aggr(mean_var[:, t % 2, :], stats[:, t % 2, :, :]).then_inc(mv_done, 1)

                    def normalise(t):
                        dve.wait_ge(mv_done, t + 1)
                        dve.wait_ge(std_done, t + 1)
                        nc.vector.tensor_scalar(x_ring[:, t % 2, :], x_ring[:, t % 2, :], mean_var[:, t % 2, 0:1],
                                                inv_std[:, t % 2:t % 2 + 1], ALU.subtract, ALU.mult).then_inc(xn_done, 1)

                    def x_low(t):
                        for h in range(2):
                            dve.wait_ge(xhi_done, 2 * t + h + 1)
                            cols = (slice(None), slice(4 * h, 4 * h + 4), slice(t * P, (t + 1) * P))
                            nc.vector.tensor_tensor(xn_lo[cols], ps[:, XT0 + h, :].rearrange("p (c t) -> p c t", t=P),
                                                    xn_hi[cols].bitcast(F32), ALU.subtract).then_inc(xlo_done, 1)

                    def add_residual(t):
                        dve.wait_ge(r_bias, t + 1)
                        for h in range(2):
                            dve.wait_ge(y_ready, 2 * t + h + 1)
                            half = r_ring[:, t % 2, h * HALF:(h + 1) * HALF]
                            add = nc.vector.tensor_tensor(half, ps[:, h, :], half, ALU.add)
                            if h == 0:
                                add.then_inc(y_used, 1)
                            else:
                                add.then_inc(x1_done, 1)

                    if b is not None:
                        for s in range(UNITS + T_LAG):
                            if s < UNITS:
                                g, i, heads, n = unit(s)
                                dve.wait_ge(s_ready, s + 1)
                                nc.vector.tensor_reduce(neg_max[:, s % STAT, 0:len(heads)],
                                                        ps[:, s % S_RING, 0:n * len(heads)].rearrange("p (j k) -> p j k", k=n),
                                                        AX.X, ALU.max, negate=True).then_inc(max_done, 1)
                            if s >= T_LAG:
                                u = s - T_LAG
                                _, _, heads, n = unit(u)
                                dve.wait_ge(pt_ready, u + 1)
                                if u >= T_RING:
                                    dve.wait_ge(av_done, u - T_RING + 1)
                                cols = slice(0, n * len(heads))
                                nc.vector.tensor_copy(probs_t[:, u % T_RING, cols], ps[:, 4 + u % T_RING, cols]).then_inc(pt_done, 1)
                            if s < UNITS:
                                if g + 1 < GROUPS and 0 <= s % PER_GROUP - Q_UNITS - 1 < GH:
                                    q_low(g + 1, s % PER_GROUP - Q_UNITS - 1)
                                if (done := finishing(s, INV_AT)) is not None:
                                    finish_inverse(done)
                                if (done := finishing(s, SCALE_AT)) is not None:
                                    finish_scale(done)
                                if (done := finishing(s, LOW_AT)) is not None:
                                    finish_low(done)
                                if nxt is not None and s // PER_GROUP == GROUPS - 1 and s % PER_GROUP in (3, 4, 5, 6):
                                    tile, part = divmod(s % PER_GROUP - 3, 2)
                                    (normalise if part else moments)(tile)
                        finish_inverse(GROUPS - 1)
                    elif nxt is not None:
                        for t in range(2):
                            moments(t)
                            normalise(t)
                    if nxt is not None:
                        x_low(0)
                        x_low(1)
                    if b is not None:
                        finish_scale(GROUPS - 1)
                        finish_low(GROUPS - 1)
                    if nxt is not None:
                        for t in (2, 3):
                            moments(t)
                            normalise(t)
                    if b is not None:
                        add_residual(0)
                    if nxt is not None:
                        x_low(2)
                    if b is not None:
                        add_residual(1)
                    if nxt is not None:
                        x_low(3)
                        dve.wait_ge(kv_done, 1)
                        nc.vector.tensor_copy(k_stack[:, :], att[0:KROWS, :]).then_inc(khi_done, 1)
                        dve.wait_ge(khi_done, 1)
                        low = slice(2 * HEAD, 3 * HEAD)
                        nc.vector.tensor_tensor(k_stack[low, :], att[low, :], k_stack[low, :].bitcast(F32),
                                                ALU.subtract).then_inc(k_done, 1)
                        dve.wait_ge(vt_ready, 1)
                        nc.vector.tensor_copy(v_pad[:, :, (GH - 1) * HEAD:GH * HEAD],
                                              ps[:, KV, 0:TILES * HEAD].rearrange("p (k d) -> p k d", d=HEAD)).then_inc(v_done, 1)
                        for j in range(GH):
                            q_low(GROUPS, j)
                        dve.wait_ge(k_done, 1)
                        dve.wait_ge(v_done, 1)
                    if b is not None:
                        add_residual(2)
                        add_residual(3)

                @block.tensor
                def _(pe):
                    def split_product(out, a_hi, a_lo, b_hi, b_lo, first, last):
                        nc.tensor.matmul(out, a_hi, b_hi, start=first, stop=False)
                        nc.tensor.matmul(out, a_lo, b_hi, start=False, stop=False)
                        return nc.tensor.matmul(out, a_hi, b_lo, start=False, stop=last)

                    def q_part(g, chunks):
                        for c in chunks:
                            if c == 0:
                                if wq_count(g):
                                    pe.wait_ge(wq_in, wq_count(g) * 2 * DMA)
                            mm = split_product(ps[:, PROJ, :], wq_hi[:, c, :], wq_lo[:, c, :], xn_hi[:, c, :], xn_lo[:, c, :],
                                               c == 0, c == CH - 1)
                            if c == CH - 1:
                                mm.then_inc(q_ready, 1)

                    def finish_spread(g):
                        pe.wait_ge(wide_done, g + 1)
                        pe.wait_ge(qlo_done, min(g + 2, GROUPS - 1) * GH)
                        if g:
                            pe.wait_ge(spread_done, g)
                        for i in range(TILES):
                            mm = nc.tensor.matmul(ps[:, PROJ, i * P:(i + 1) * P], att[:, i * P:(i + 1) * P], ident_sb[:, :],
                                                  start=True, stop=True)
                        mm.then_inc(spread_ready, 1)

                    def transposes(t):
                        pe.wait_ge(xn_done, t + 1)
                        for h in range(2):
                            if t:
                                pe.wait_ge(xlo_done, 2 * (t - 1) + h + 1)
                            for c in range(4):
                                mm = nc.tensor.transpose(ps[:, XT0 + h, c * P:(c + 1) * P],
                                                         x_ring[:, t % 2, (4 * h + c) * P:(4 * h + c + 1) * P], ident_sb[:, :])
                            mm.then_inc(xt_ready, 1)

                    def output(t):
                        for h in range(2):
                            if t:
                                if h:
                                    pe.wait_ge(x1_done, t)
                                else:
                                    pe.wait_ge(y_used, t)
                            for c in range(CH):
                                if t == 0 and h == 0 and c >= CH - 2:
                                    pe.wait_ge(olo_done, c + 1)
                                tok = slice(t * P, (t + 1) * P)
                                out = slice(h * HALF, (h + 1) * HALF)
                                mm = split_product(ps[:, h, :], at_hi[:, c, tok], at_lo[:, c, tok], wo_hi[:, c, out],
                                                   wo_lo[:, c, out], c == 0, c == CH - 1)
                            mm.then_inc(y_ready, 1)

                    if b is not None:
                        for s in range(UNITS + AV_LAG):
                            if s < UNITS:
                                g, i, heads, n = unit(s)
                                if s % PER_GROUP == 0 and g:
                                    pe.wait_ge(qlo_done, g * GH)
                                    pe.wait_ge(qre_in, g * DMA)
                                if s >= S_RING:
                                    pe.wait_ge(exp_done, s - S_RING + 1)
                                for m, j in enumerate(heads):
                                    cols = ps[:, s % S_RING, m * n:(m + 1) * n]
                                    nc.tensor.matmul(cols, q_stack[:, g % 2, j, i * P:(i + 1) * P], k_stack[:, 0:n],
                                                     start=True, stop=False)
                                    mm = nc.tensor.matmul(cols[:, n - P:n], identb_sb[:, :], causal_sb[:, :], start=False, stop=True)
                                mm.then_inc(s_ready, 1)
                                q_unit = s % PER_GROUP
                                if q_unit < Q_UNITS and g + 1 < GROUPS:
                                    if q_unit == 0 and g:
                                        pe.wait_ge(qlo_done, g * GH)
                                        if g >= 2:
                                            pe.wait_ge(spread_done, g - 1)
                                    q_part(g + 1, range(q_unit * CH // Q_UNITS, (q_unit + 1) * CH // Q_UNITS))
                                if (done := finishing(s, SPREAD_AT)) is not None:
                                    finish_spread(done)
                            if T_LAG <= s < UNITS + T_LAG:
                                u = s - T_LAG
                                g, i, heads, n = unit(u)
                                pe.wait_ge(exp_done, u + 1)
                                if u >= T_RING:
                                    pe.wait_ge(pt_done, u - T_RING + 1)
                                for k in range(n * len(heads) // P):
                                    mm = nc.tensor.transpose(ps[:, 4 + u % T_RING, k * P:(k + 1) * P],
                                                             probs[:, u % P_RING, k * P:(k + 1) * P], ident_sb[:, :])
                                mm.then_inc(pt_ready, 1)
                            if s >= AV_LAG:
                                u = s - AV_LAG
                                g, i, heads, n = unit(u)
                                pe.wait_ge(pt_done, u + 1)
                                if u % PER_GROUP == 0 and g >= 2:
                                    pe.wait_ge(att_done, g - 1)
                                for m, j in enumerate(heads):
                                    for k in range(i + 1):
                                        lead = (GH - 1 - j) * HEAD
                                        cols = slice(m * n + k * P, m * n + (k + 1) * P)
                                        mm = nc.tensor.matmul(ps[:, 6 + g % 2, i * P:(i + 1) * P], v_pad[:, k, lead:lead + P],
                                                              probs_t[:, u % T_RING, cols],
                                                              start=(j == 0 and k == 0), stop=(j == GH - 1 and k == i))
                                mm.then_inc(av_done, 1)
                    if nxt is not None:
                        transposes(0)
                    if b is not None:
                        finish_spread(GROUPS - 1)
                    if nxt is not None:
                        transposes(1)
                    if b is not None:
                        output(0)
                    if nxt is not None:
                        transposes(2)
                    if b is not None:
                        output(1)
                    if nxt is not None:
                        transposes(3)
                        pe.wait_ge(xlo_done, 2 * TILES)
                        for c in range(CH):
                            mm = split_product(ps[:, KV, :], wkv_hi[:, c, :], wkv_lo[:, c, :], xn_hi[:, c, :], xn_lo[:, c, :],
                                               c == 0, c == CH - 1)
                        mm.then_inc(kv_ready, 1)
                        if b is not None:
                            pe.wait_ge(spread_done, GROUPS)
                        q_part(GROUPS, range(CH))
                        pe.wait_ge(kv_done, 1)
                        for k in range(TILES):
                            mm = nc.tensor.transpose(ps[:, KV, k * HEAD:(k + 1) * HEAD], att[3 * HEAD:4 * HEAD, k * P:(k + 1) * P],
                                                     ident_sb[3 * HEAD:4 * HEAD, 3 * HEAD:4 * HEAD])
                        mm.then_inc(vt_ready, 1)
                    if b is not None:
                        output(2)
                        output(3)

            nc.all_engine_barrier(sems_to_clear=range(row_sems[0].num, row_sems[-1].num + 1))

        row(None, 0)
        with nc.Fori(0, BATCH - 1) as b:
            row(b, b + 1)
        row(BATCH - 1, None)


def mixer_program(nc, x1, w, c, out):
    L, T, D = x1.shape
    PB = P // L
    TILES = 4
    STEPS = T // (PB * TILES)
    CH = D // P
    HALF = 512
    COLS = TILES * P
    DM = 128
    DIN, NH, DST, TAPS = 2 * DM, 4, 16, 7
    HD = DIN // NH
    C_ROW = 32
    RANK = w["enc"].shape[0]
    EXPERTS = w["coefs"].shape[2]
    SCALING = 0.5
    SP_STEPS = 13
    DMA = 16
    NORMS = [(1, 0), (1, 1), (2, 0), (1, 2), (2, 1), (1, 3), (2, 2), (2, 3), (3, 0), (3, 1), (3, 2), (3, 3)]
    KIND2 = [e for e, (k, _) in enumerate(NORMS) if k == 2]
    GEMMS = [e for e, (k, _) in enumerate(NORMS) if k != 2]
    Y0, XT0, DOWN, UP0 = 0, 2, 4, 5

    with ExitStack() as ctx:
        def sb(name, shape, dt=F32):
            return ctx.enter_context(nc.sbuf_tensor("m_" + name, shape, dt))

        def sem(name):
            return ctx.enter_context(nc.semaphore("m_" + name))

        w_hi, w_lo = sb("w_hi", [P, CH, D], F32R), sb("w_lo", [P, CH, D], F32R)
        wd_hi, wd_lo = sb("wd_hi", [P, CH, DM], F32R), sb("wd_lo", [P, CH, DM], F32R)
        xs = sb("xs", [P, TILES, D])
        xn = sb("xn", [P, 2, D])
        xt_hi, xt_lo = sb("xt_hi", [P, 2, CH, P], F32R), sb("xt_lo", [P, 2, CH, P], F32R)
        stats, mean_var = sb("stats", [P, 2, 2, 6]), sb("mean_var", [P, 2, 2])
        var_eps, inv_std, neg_half = sb("var_eps", [P, 2]), sb("inv_std", [P, 2]), sb("neg_half", [P, TILES])
        h_mid, h_next, h_out, h_skip = sb("h_mid", [P, COLS]), sb("h_next", [P, COLS]), sb("h_out", [P, COLS]), sb("h_skip", [P, COLS])
        conv = sb("conv", [P, 3, COLS])
        x_feat = sb("x_feat", [P, 2, COLS])
        b_feat, c_feat = sb("b_feat", [DST, COLS]), sb("c_feat", [DST, COLS])
        x_tok, z_gate = sb("x_tok", [P, TILES, DIN]), sb("z_gate", [P, TILES, DIN])
        dt_raw, dt_tmp, dt, dta = (sb("dt_raw", [P, TILES, 2 * NH]), sb("dt_tmp", [P, TILES, 2 * NH]),
                                   sb("dt", [P, TILES, 2 * NH]), sb("dta", [P, TILES, 2 * NH]))
        sp_s, sp_s2, sp_t, sp_log = (sb(n, [P, TILES, 2 * NH]) for n in ("sp_s", "sp_s2", "sp_t", "sp_log"))
        dt_reach = sb("dt_reach", [P, TILES, 2 * NH, L])
        decay = sb("decay", [P, 2, TILES, NH, L])
        dt_mask = sb("dt_mask", [P, 2, TILES, NH, L])
        weight = sb("weight", [P, TILES, NH, L])
        d_term, d_diag = sb("d_term", [P, TILES, NH]), sb("d_diag", [P, TILES, NH, L])
        cb_fw, cb_bw, cb = sb("cb_fw", [P, TILES, P]), sb("cb_bw", [P, TILES, P]), sb("cb", [P, TILES, P])
        mixer = sb("mixer", [P, 2, NH, P])
        yz, square, sum_sq, y_std, y_inv = (sb("yz", [P, TILES, DIN]), sb("square", [P, DIN]), sb("sum_sq", [P, TILES]),
                                            sb("y_std", [P, TILES]), sb("y_inv", [P, TILES]))
        yn_feat = sb("yn_feat", [P, 2, COLS])
        enc, coef, mask, wsum3, wsum, basis = (sb("enc", [RANK, D]), sb("coef", [P, CH, EXPERTS, RANK]),
                                               sb("mask", [P, CH, EXPERTS, RANK], U8), sb("wsum3", [P, CH, EXPERTS, RANK]),
                                               sb("wsum", [P, CH, RANK]), sb("basis", [RANK, D]))
        names = ["up_t", "base_b", "up_b", "down_b", "gate", "wx_t", "wbc_t", "wz_t", "wdt_t", "conv_w", "conv_b", "dt_b",
                 "a_log", "d_row", "fcd_t", "norm_w", "wout_t"]
        par = {n: sb("p_" + n, list(w[n].shape)) for n in names}
        con = {n: sb("c_" + n, list(a.shape)) for n, a in c.items() if n != "dft_t"}
        a_row, wout, alpha, keep, skip = (sb("a_row", [P, 2 * NH]), sb("wout", [P, 2, DM]), sb("alpha", [P, 1]),
                                          sb("keep", [P, 1]), sb("skip", [P, 1]))
        ps = ctx.enter_context(nc.psum_tensor("ps_mixer", [P, 8, HALF], F32))
        PARAMS = (len(names) + len(con) + 3) * DMA

        params_in, stage_in = sem("params_in"), [sem("stage_in_0"), sem("stage_in_1")]
        wsum_step, wsum_done, basis_part, basis_ready, basis_done = (sem("wsum_step"), sem("wsum_done"), sem("basis_part"),
                                                                     sem("basis_ready"), sem("basis_done"))
        delta_ready, sum_done, whi_done, wlo_done = sem("delta_ready"), sem("sum_done"), sem("whi_done"), sem("wlo_done")
        setup, small, gate_exp, a_exp = sem("setup"), sem("small"), sem("gate_exp"), sem("a_exp")

        def stage(n):
            return xs[:, n % 2, :]

        with nc.Block() as block:
            @block.sync
            def _(sp):
                for n in names:
                    sp.dma_start(par[n][:], w[n]).then_inc(params_in, DMA)
                for n in con:
                    sp.dma_start(con[n][:], c[n]).then_inc(params_in, DMA)
                for dst, n in ((enc, "enc"), (coef, "coefs"), (mask, "masks")):
                    sp.dma_start(dst[:], w[n]).then_inc(params_in, DMA)
                for n in range(2 * CH + 1):
                    if 2 <= n < CH + 2:
                        if n - 2 < CH - 1:
                            sp.wait_ge(basis_part, n - 1)
                        else:
                            sp.wait_ge(basis_ready, 2)
                    elif n >= CH + 2:
                        sp.wait_ge(sum_done, n - CH - 1)
                    src = (c["dft_t"][n * P:(n + 1) * P, :] if n < CH else
                           w["base_t"][(n - CH) * P:(n - CH + 1) * P, :] if n < 2 * CH else w["down_t"])
                    sp.dma_start(stage(n), src).then_inc(stage_in[n % 2], DMA)

            @block.gpsimd
            def _(pool):
                nc.gpsimd.memset(neg_half[:, :], -0.5).then_inc(setup, 1)
                nc.gpsimd.memset(cb_fw[:, :, :], 0.0).then_inc(setup, 1)
                nc.gpsimd.memset(cb_bw[:, :, :], 0.0).then_inc(setup, 1)
                pool.wait_ge(setup, 3)

            @block.scalar
            def _(act):
                act.wait_ge(params_in, PARAMS)
                nc.scalar.activation(alpha[:, :], par["gate"][:, :], ACT.Exp, scale=-1.0).then_inc(gate_exp, 1)
                nc.scalar.activation(a_row[:, :], par["a_log"][:, :], ACT.Exp).then_inc(a_exp, 1)
                for n in range(CH + 1):
                    act.wait_ge(sum_done, n + 1)
                    if n < CH:
                        nc.scalar.copy(w_hi[:, n, :], xn[:, n % 2, :]).then_inc(whi_done, 1)
                    else:
                        nc.scalar.copy(wd_hi[:, :, :], xn[:, n % 2, :].rearrange("p (c m) -> p c m", c=CH)).then_inc(whi_done, 1)

            @block.vector
            def _(dve):
                dve.wait_ge(params_in, PARAMS)
                nc.vector.tensor_tensor(wsum3[:, :, :, :], coef[:, :, :, :], mask[:, :, :, :], ALU.mult).then_inc(wsum_step, 1)
                dve.wait_ge(wsum_step, 1)
                nc.vector.tensor_tensor(wsum[:, :, :], wsum3[:, :, 0, :], wsum3[:, :, 1, :], ALU.add).then_inc(wsum_step, 1)
                for n in range(2, EXPERTS):
                    dve.wait_ge(wsum_step, n)
                    nc.vector.tensor_tensor(wsum[:, :, :], wsum[:, :, :], wsum3[:, :, n, :], ALU.add).then_inc(
                        wsum_done if n == EXPERTS - 1 else wsum_step, 1)
                dve.wait_ge(gate_exp, 1)
                nc.vector.tensor_scalar(keep[:, :], alpha[:, :], 1.0, None, ALU.add).then_inc(small, 1)
                dve.wait_ge(small, 1)
                nc.vector.reciprocal(alpha[:, :], keep[:, :]).then_inc(small, 1)
                dve.wait_ge(small, 2)
                nc.vector.tensor_scalar(keep[:, :], alpha[:, :], -1.0, 1.0, ALU.mult, ALU.add).then_inc(small, 1)
                nc.vector.tensor_scalar(skip[:, :], alpha[:, :], 1.0, None, ALU.add).then_inc(small, 1)
                dve.wait_ge(a_exp, 1)
                nc.vector.tensor_scalar(a_row[:, :], a_row[:, :], -1.0, None, ALU.mult).then_inc(small, 1)
                for k in range(2):
                    nc.vector.tensor_scalar(wout[:, k, :], par["wout_t"][:, k, :], par["norm_w"][:, k:k + 1], None,
                                            ALU.mult).then_inc(small, 1)
                dve.wait_ge(basis_ready, 2)
                nc.vector.tensor_copy(basis[:, :].rearrange("r (h n) -> r h n", h=2), ps[0:RANK, 0:2, :]).then_inc(basis_done, 1)
                for n in range(CH + 1):
                    dve.wait_ge(stage_in[(n + CH) % 2], DMA * ((n + CH) // 2 + 1))
                    if n >= 2:
                        dve.wait_ge(wlo_done, n - 1)
                    if n < CH:
                        dve.wait_ge(delta_ready, 2 * (n + 1))
                        nc.vector.scalar_tensor_tensor(xn[:, n % 2, :].rearrange("p (h n) -> p h n", h=2),
                                                       ps[:, 2 + 2 * (n % 2):4 + 2 * (n % 2), :], SCALING,
                                                       stage(n + CH).rearrange("p (h n) -> p h n", h=2), ALU.mult, ALU.add
                                                       ).then_inc(sum_done, 1)
                    else:
                        nc.vector.tensor_copy(xn[:, n % 2, :], stage(n + CH)).then_inc(sum_done, 1)
                    dve.wait_ge(whi_done, n + 1)
                    if n < CH:
                        nc.vector.tensor_tensor(w_lo[:, n, :], xn[:, n % 2, :], w_hi[:, n, :].bitcast(F32),
                                                ALU.subtract).then_inc(wlo_done, 1)
                    else:
                        nc.vector.tensor_tensor(wd_lo[:, :, :], xn[:, n % 2, :].rearrange("p (c m) -> p c m", c=CH),
                                                wd_hi[:, :, :].bitcast(F32), ALU.subtract).then_inc(wlo_done, 1)

            @block.tensor
            def _(pe):
                pe.wait_ge(wsum_done, 1)
                for n in range(CH):
                    pe.wait_ge(stage_in[n % 2], DMA * (n // 2 + 1))
                    for h in range(2):
                        mm = nc.tensor.matmul(ps[0:RANK, h, :], wsum[:, n, :], stage(n)[:, h * HALF:(h + 1) * HALF],
                                              start=(n == 0), stop=(n == CH - 1))
                        if n == CH - 1:
                            mm.then_inc(basis_ready, 1)
                        elif h == 1:
                            mm.then_inc(basis_part, 1)
                pe.wait_ge(basis_done, 1)
                for n in range(CH):
                    if n >= 2:
                        pe.wait_ge(sum_done, n - 1)
                    for h in range(2):
                        nc.tensor.matmul(ps[:, 2 + 2 * (n % 2) + h, :], enc[:, n * P:(n + 1) * P],
                                         basis[:, h * HALF:(h + 1) * HALF], start=True, stop=True).then_inc(delta_ready, 1)

        step_sems = []

        def step_sem(name):
            step_sems.append(sem(name))
            return step_sems[-1]

        x_in = [step_sem(f"x_in_{t}") for t in range(TILES)]
        out_sent = step_sem("out_sent")
        stats_done, mv_done, eps_done, std_done, xn_done, post_done, up_bias = (
            step_sem("stats_done"), step_sem("mv_done"), step_sem("eps_done"), step_sem("std_done"), step_sem("xn_done"),
            step_sem("post_done"), step_sem("up_bias"))
        xt_ready, xhi_done, xlo_done = step_sem("xt_ready"), step_sem("xhi_done"), step_sem("xlo_done")
        y_ready, y_added, down_ready, h_done = step_sem("y_ready"), step_sem("y_added"), step_sem("down_ready"), step_sem("h_done")
        up_ready, up_added, skip_done = step_sem("up_ready"), step_sem("up_added"), step_sem("skip_done")
        xbc_ready, dt_ready, tap0_done, taps_done = (step_sem("xbc_ready"), step_sem("dt_ready"), step_sem("tap0_done"),
                                                     step_sem("taps_done"))
        dt_step, nabs_done, sp_exp, sp_inv, sp_step, sp_done, reach_done = (
            step_sem("dt_step"), step_sem("nabs_done"), step_sem("sp_exp"), step_sem("sp_inv"), step_sem("sp_step"), step_sem("sp_done"),
            step_sem("reach_done"))
        xf_done, bc_done, z_ready, z_done, xtok_ready, xtok_done = (step_sem("xf_done"), step_sem("bc_done"), step_sem("z_ready"),
                                                                    step_sem("z_done"), step_sem("xtok_ready"), step_sem("xtok_done"))
        cb_ready, cb_step, cb_done, decay_ready, decay_done, w_step, w_done = (
            step_sem("cb_ready"), step_sem("cb_step"), step_sem("cb_done"), step_sem("decay_ready"), step_sem("decay_done"),
            step_sem("w_step"), step_sem("w_done"))
        mixer_done, ym_ready, yz_done, sq_done, ystd_done, yinv_done, yn_done = (
            step_sem("mixer_done"), step_sem("ym_ready"), step_sem("yz_done"), step_sem("sq_done"), step_sem("ystd_done"),
            step_sem("yinv_done"), step_sem("yn_done"))
        yf_ready, yf_done, o_ready, h_new = step_sem("yf_ready"), step_sem("yf_done"), step_sem("o_ready"), step_sem("h_new")

        x1_v = x1.rearrange("l (i t b) d -> i t l b d", t=TILES, b=PB)
        out_v = out.rearrange("l (i t b) d -> i t l b d", t=TILES, b=PB)

        with nc.Fori(0, STEPS) as i:
            with nc.Block(no_gpsimd_drain=True) as block:
                @block.sync
                def _(sp):
                    for t in range(TILES):
                        sp.dma_start(xs[:, t, :], x1_v[i, t]).then_inc(x_in[t], DMA)
                    for t in range(TILES):
                        sp.wait_ge(y_added, 2 * (TILES + t + 1))
                        sp.dma_start(out_v[i, t], xs[:, t, :]).then_inc(out_sent, DMA)
                    sp.wait_ge(out_sent, TILES * DMA)

                @block.gpsimd
                def _(pool):
                    def inv_sqrt(e):
                        pool.wait_ge(mv_done, e + 1)
                        s = slice(e % 2, e % 2 + 1)
                        nc.gpsimd.tensor_scalar(var_eps[:, s], mean_var[:, e % 2, 1:2], EPS, None, ALU.add).then_inc(eps_done, 1)
                        pool.wait_ge(eps_done, e + 1)
                        nc.gpsimd.tensor_tensor(inv_std[:, s], var_eps[:, s], neg_half[:, 0:1], ALU.pow).then_inc(std_done, 1)

                    def post(e):
                        kind, t = NORMS[e]
                        pool.wait_ge(xn_done, e + 1)
                        if kind == 2:
                            nc.gpsimd.tensor_tensor(xs[:, t, :], xs[:, t, :], xn[:, e % 2, :], ALU.add).then_inc(up_bias, 1)
                            pool.wait_ge(up_bias, KIND2.index(e) + 1)
                        b = par["up_b"] if kind == 2 else par["base_b"]
                        nc.gpsimd.tensor_tensor(xs[:, t, :], xs[:, t, :], b[:, :], ALU.add).then_inc(post_done, 1)

                    def softplus(q):
                        step = [SP_STEPS * q]

                        def then(op):
                            op.then_inc(sp_step, 1)
                            step[0] += 1
                            pool.wait_ge(sp_step, step[0])

                        y, s, s2, t = dt_tmp[:, :, :], sp_s[:, :, :], sp_s2[:, :, :], sp_t[:, :, :]
                        pool.wait_ge(sp_inv, 2 * (q + 1))
                        then(nc.gpsimd.tensor_tensor(s, y, t, ALU.mult))
                        then(nc.gpsimd.tensor_tensor(s2, s, s, ALU.mult))
                        then(nc.gpsimd.tensor_scalar(t, s2, 1.0 / 13, 1.0 / 11, ALU.mult, ALU.add))
                        for n in (9, 7, 5, 3, 1):
                            then(nc.gpsimd.tensor_tensor(t, t, s2, ALU.mult))
                            then(nc.gpsimd.tensor_scalar(t, t, 1.0 / n, None, ALU.add))
                        nc.gpsimd.tensor_tensor(sp_log[:, :, :], t, s, ALU.mult).then_inc(sp_done, 1)

                    def hydra_inv_std(q):
                        pool.wait_ge(sq_done, TILES * (q + 1))
                        nc.gpsimd.tensor_scalar(y_std[:, :], sum_sq[:, :], 1.0 / DIN, EPS, ALU.mult, ALU.add).then_inc(ystd_done, 1)
                        pool.wait_ge(ystd_done, q + 1)
                        nc.gpsimd.tensor_tensor(y_inv[:, :], y_std[:, :], neg_half[:, :], ALU.pow).then_inc(yinv_done, 1)

                    first = [e for e in range(len(NORMS)) if NORMS[e][0] != 3]
                    for e in first:
                        inv_sqrt(e)
                        if e:
                            post(e - 1)
                    post(first[-1])
                    pool.wait_ge(h_done, TILES)
                    nc.gpsimd.tensor_scalar(h_skip[:, :], h_mid[:, :], skip[:, :], None, ALU.mult).then_inc(skip_done, 1)
                    for q in range(2):
                        softplus(q)
                        hydra_inv_std(q)
                    for e in range(len(first), len(NORMS)):
                        inv_sqrt(e)
                        if e > len(first):
                            post(e - 1)
                    post(len(NORMS) - 1)

                @block.scalar
                def _(act):
                    def x_high(e):
                        for h in range(2):
                            act.wait_ge(xt_ready, 2 * e + h + 1)
                            nc.scalar.copy(xt_hi[:, e % 2, 4 * h:4 * h + 4, :],
                                           ps[:, XT0 + h, :].rearrange("p (c t) -> p c t", t=P)).then_inc(xhi_done, 1)

                    def gelu(e):
                        t = NORMS[e][1]
                        act.wait_ge(down_ready, KIND2.index(e) + 1)
                        nc.scalar.activation(h_mid[:, t * P:(t + 1) * P], ps[:, DOWN, 0:P], ACT.Gelu,
                                             bias=par["down_b"][:, :]).then_inc(h_done, 1)

                    def hydra(q):
                        for m in range(3):
                            rows = slice(0, P if m < 2 else C_ROW + DST)
                            act.wait_ge(xbc_ready, 3 * q + m + 1)
                            nc.scalar.activation(conv[rows, m, :], ps[rows, 4 + m, :], ACT.Identity, bias=par["conv_b"][rows, m:m + 1],
                                                 scale=par["conv_w"][rows, m, TAPS - 1:TAPS]).then_inc(tap0_done, 1)
                        act.wait_ge(nabs_done, q + 1)
                        nc.scalar.activation(dt_tmp[:, :, :], dt_tmp[:, :, :], ACT.Exp).then_inc(sp_exp, 1)
                        for m in range(2):
                            act.wait_ge(taps_done, 3 * (TAPS - 1) * q + 3 * (TAPS - 2) + m + 1)
                            nc.scalar.activation(x_feat[:, m, :], conv[:, m, :], ACT.Silu).then_inc(xf_done, 1)
                        act.wait_ge(taps_done, 3 * (TAPS - 1) * (q + 1))
                        nc.scalar.activation(b_feat[:, :], conv[0:DST, 2, :], ACT.Silu).then_inc(bc_done, 1)
                        nc.scalar.activation(c_feat[:, :], conv[C_ROW:C_ROW + DST, 2, :], ACT.Silu).then_inc(bc_done, 1)
                        for k in range(2):
                            act.wait_ge(z_ready, 2 * q + k + 1)
                            nc.scalar.activation(z_gate[:, 2 * k:2 * k + 2, :], ps[:, 4 + k, :].rearrange("p (t n) -> p t n", t=2),
                                                 ACT.Silu).then_inc(z_done, 1)
                        act.wait_ge(decay_ready, q + 1)
                        nc.scalar.activation(decay[:, :, :, :, :].rearrange("p d t h l -> p (d t h l)"), ps[:, 5, 0:2 * TILES * NH * L],
                                             ACT.Exp).then_inc(decay_done, 1)
                        for t in range(TILES):
                            act.wait_ge(yz_done, TILES * q + t + 1)
                            if t or q:
                                act.wait_ge(sq_done, TILES * q + t)
                            nc.scalar.activation(square[:, :], yz[:, t, :], ACT.Square,
                                                 accum_out=sum_sq[:, t:t + 1]).then_inc(sq_done, 1)
                        for k in range(2):
                            act.wait_ge(yf_ready, 2 * q + k + 1)
                            nc.scalar.copy(yn_feat[:, k, :], ps[:, 4 + k, :]).then_inc(yf_done, 1)
                        if q == 0:
                            act.wait_ge(o_ready, 1)
                            nc.scalar.copy(h_next[:, :], ps[:, 6, :]).then_inc(h_new, 1)

                    first = [e for e in range(len(NORMS)) if NORMS[e][0] != 3]
                    for e in range(0, len(first), 2):
                        x_high(e)
                        x_high(e + 1)
                        for f in (e, e + 1):
                            if NORMS[f][0] == 2:
                                gelu(f)
                    hydra(0)
                    hydra(1)
                    for e in range(len(first), len(NORMS)):
                        x_high(e)

                @block.vector
                def _(dve):
                    def norm(e):
                        kind, t = NORMS[e]
                        if kind == 1:
                            dve.wait_ge(x_in[t], DMA)
                        elif kind == 2:
                            dve.wait_ge(y_added, 2 * (t + 1))
                        else:
                            dve.wait_ge(up_added, 2 * (t + 1))
                        for h in range(2):
                            nc.vector.bn_stats(stats[:, e % 2, h, :], xs[:, t, h * HALF:(h + 1) * HALF]).then_inc(stats_done, 1)
                        dve.wait_ge(stats_done, 2 * (e + 1))
                        nc.vector.bn_aggr(mean_var[:, e % 2, :], stats[:, e % 2, :, :]).then_inc(mv_done, 1)
                        dve.wait_ge(mv_done, e + 1)
                        dve.wait_ge(std_done, e + 1)
                        if e >= 2:
                            dve.wait_ge(xt_ready, 2 * (e - 1))
                            dve.wait_ge(post_done, e - 1)
                        nc.vector.tensor_scalar(xn[:, e % 2, :], xs[:, t, :], mean_var[:, e % 2, 0:1], inv_std[:, e % 2:e % 2 + 1],
                                                ALU.subtract, ALU.mult).then_inc(xn_done, 1)

                    def x_low(e):
                        for h in range(2):
                            dve.wait_ge(xhi_done, 2 * e + h + 1)
                            part = (slice(None), e % 2, slice(4 * h, 4 * h + 4), slice(None))
                            nc.vector.tensor_tensor(xt_lo[part], ps[:, XT0 + h, :].rearrange("p (c t) -> p c t", t=P),
                                                    xt_hi[part].bitcast(F32), ALU.subtract).then_inc(xlo_done, 1)

                    def add(e):
                        t, g = NORMS[e][1], GEMMS.index(e)
                        dve.wait_ge(post_done, e + 1)
                        for h in range(2):
                            dve.wait_ge(y_ready, 2 * g + h + 1)
                            half = xs[:, t, h * HALF:(h + 1) * HALF]
                            nc.vector.tensor_tensor(half, ps[:, Y0 + h, :], half, ALU.add).then_inc(y_added, 1)

                    def add_up(t):
                        dve.wait_ge(post_done, KIND2[t] + 1)
                        for h in range(2):
                            dve.wait_ge(up_ready, 2 * t + h + 1)
                            half = xs[:, t, h * HALF:(h + 1) * HALF]
                            nc.vector.tensor_tensor(half, ps[:, UP0 + h, :], half, ALU.add).then_inc(up_added, 1)

                    def hydra(q):
                        dve.wait_ge(dt_ready, TILES * (q + 1))
                        nc.vector.tensor_tensor(dt_raw[:, :, :], ps[:, 7, 0:TILES * 2 * NH].rearrange("p (t n) -> p t n", t=TILES),
                                                par["dt_b"][:, None, :].to_broadcast([P, TILES, 2 * NH]), ALU.add).then_inc(dt_step, 1)
                        dve.wait_ge(dt_step, 4 * q + 1)
                        nc.vector.scalar_tensor_tensor(dt_tmp[:, :, :], dt_raw[:, :, :], -1.0, dt_raw[:, :, :], ALU.mult,
                                                       ALU.min).then_inc(nabs_done, 1)
                        taps = 3 * (TAPS - 1) * q
                        for j in range(1, TAPS):
                            for m in range(3):
                                if j == 1:
                                    dve.wait_ge(tap0_done, 3 * q + m + 1)
                                else:
                                    dve.wait_ge(taps_done, taps + 3 * (j - 2) + m + 1)
                                rows = slice(0, P if m < 2 else C_ROW + DST)
                                acc = conv[rows, m, :].rearrange("p (t n) -> p t n", t=TILES)[:, :, j * PB:P]
                                nc.vector.scalar_tensor_tensor(
                                    acc, ps[rows, 4 + m, :].rearrange("p (t n) -> p t n", t=TILES)[:, :, 0:P - j * PB],
                                    par["conv_w"][rows, m, TAPS - 1 - j:TAPS - j], acc, ALU.mult, ALU.add).then_inc(taps_done, 1)
                            if j == 2:
                                dve.wait_ge(sp_exp, q + 1)
                                nc.vector.tensor_scalar(sp_t[:, :, :], dt_tmp[:, :, :], 2.0, None, ALU.add).then_inc(sp_inv, 1)
                            if j == 3:
                                dve.wait_ge(sp_inv, 2 * q + 1)
                                nc.vector.reciprocal(sp_t[:, :, :], sp_t[:, :, :]).then_inc(sp_inv, 1)
                        dve.wait_ge(sp_done, q + 1)
                        nc.vector.tensor_scalar(dt_raw[:, :, :], dt_raw[:, :, :], 0.0, None, ALU.max).then_inc(dt_step, 1)
                        dve.wait_ge(dt_step, 4 * q + 2)
                        nc.vector.scalar_tensor_tensor(dt[:, :, :], sp_log[:, :, :], 2.0, dt_raw[:, :, :], ALU.mult,
                                                       ALU.add).then_inc(dt_step, 1)
                        dve.wait_ge(dt_step, 4 * q + 3)
                        nc.vector.tensor_tensor(dta[:, :, :], dt[:, :, :], a_row[:, None, :].to_broadcast([P, TILES, 2 * NH]),
                                                ALU.mult).then_inc(dt_step, 1)
                        dve.wait_ge(dt_step, 4 * q + 4)
                        nc.vector.tensor_tensor(dt_reach[:, :, :, :], dta[:, :, :, None].to_broadcast([P, TILES, 2 * NH, L]),
                                                con["reach"][:, None, :, :].to_broadcast([P, TILES, 2 * NH, L]),
                                                ALU.mult).then_inc(reach_done, 1)
                        for d in range(2):
                            nc.vector.tensor_tensor(dt_mask[:, d, :, :, :],
                                                    dt[:, :, d * NH:(d + 1) * NH, None].to_broadcast([P, TILES, NH, L]),
                                                    con["side"][:, d, None, None, :].to_broadcast([P, TILES, NH, L]),
                                                    ALU.mult).then_inc(w_step, 1)
                        for k in range(2):
                            dve.wait_ge(xtok_ready, 2 * q + k + 1)
                            nc.vector.tensor_copy(x_tok[:, 2 * k:2 * k + 2, :],
                                                  ps[:, 6 + k, :].rearrange("p (t n) -> p t n", t=2)).then_inc(xtok_done, 1)
                        dve.wait_ge(cb_ready, q + 1)
                        cb_ps = ps[:, 4, :].rearrange("p (t n) -> p t n", t=TILES)
                        cut = P - PB
                        nc.vector.tensor_tensor(cb_fw[:, :, PB:P], cb_ps[:, :, 0:cut],
                                                con["before"][:, None, PB:P].to_broadcast([P, TILES, cut]), ALU.mult).then_inc(cb_step, 1)
                        nc.vector.tensor_tensor(cb_bw[:, :, 0:cut], cb_ps[:, :, PB:P],
                                                con["after"][:, None, 0:cut].to_broadcast([P, TILES, cut]), ALU.mult).then_inc(cb_step, 1)
                        dve.wait_ge(cb_step, 3 * q + 2)
                        nc.vector.tensor_tensor(cb[:, :, :], cb_fw[:, :, :], cb_bw[:, :, :], ALU.add).then_inc(cb_step, 1)
                        dve.wait_ge(cb_step, 3 * q + 3)
                        nc.vector.tensor_tensor(cb[:, :, :], cb[:, :, :], con["ident"][:, None, :].to_broadcast([P, TILES, P]),
                                                ALU.add).then_inc(cb_done, 1)
                        dve.wait_ge(decay_ready, q + 1)
                        dve.wait_ge(decay_done, q + 1)
                        nc.vector.tensor_tensor(d_term[:, :, :], ps[:, 5, 256:256 + TILES * NH].rearrange("p (t h) -> p t h", t=TILES),
                                                par["d_row"][:, None, :].to_broadcast([P, TILES, NH]), ALU.add).then_inc(w_step, 1)
                        nc.vector.tensor_tensor(decay[:, :, :, :, :].rearrange("p d t h l -> p (d t h l)"),
                                                decay[:, :, :, :, :].rearrange("p d t h l -> p (d t h l)"),
                                                dt_mask[:, :, :, :, :].rearrange("p d t h l -> p (d t h l)"), ALU.mult).then_inc(w_step, 1)
                        dve.wait_ge(w_step, 6 * q + 4)
                        nc.vector.tensor_tensor(d_diag[:, :, :, :], d_term[:, :, :, None].to_broadcast([P, TILES, NH, L]),
                                                con["same"][:, None, None, :].to_broadcast([P, TILES, NH, L]), ALU.mult).then_inc(w_step, 1)
                        nc.vector.tensor_tensor(weight[:, :, :, :], decay[:, 0, :, :, :], decay[:, 1, :, :, :], ALU.add).then_inc(w_step, 1)
                        dve.wait_ge(w_step, 6 * q + 6)
                        nc.vector.tensor_tensor(weight[:, :, :, :], weight[:, :, :, :], d_diag[:, :, :, :], ALU.add).then_inc(w_done, 1)
                        dve.wait_ge(w_done, q + 1)
                        dve.wait_ge(cb_done, q + 1)

                        def mix(t):
                            if t >= 2:
                                dve.wait_ge(ym_ready, TILES * q + t - 1)
                            nc.vector.tensor_tensor(
                                mixer[:, t % 2, :, :].rearrange("p h (l b) -> p h l b", b=PB),
                                cb[:, t, :].rearrange("p (l b) -> p l b", b=PB)[:, None, :, :].to_broadcast([P, NH, L, PB]),
                                weight[:, t, :, :, None].to_broadcast([P, NH, L, PB]), ALU.mult).then_inc(mixer_done, 1)

                        def gate(t):
                            dve.wait_ge(ym_ready, TILES * q + t + 1)
                            if t == 0:
                                dve.wait_ge(z_done, 2 * (q + 1))
                            nc.vector.tensor_tensor(yz[:, t, :], ps[:, 6 + t % 2, 0:DIN], z_gate[:, t, :], ALU.mult).then_inc(yz_done, 1)

                        mix(0)
                        for t in range(TILES):
                            if t + 1 < TILES:
                                mix(t + 1)
                            gate(t)
                        dve.wait_ge(yinv_done, q + 1)
                        for t in range(TILES):
                            nc.vector.tensor_scalar(yz[:, t, :], yz[:, t, :], y_inv[:, t:t + 1], None, ALU.mult).then_inc(yn_done, 1)
                        if q == 1:
                            dve.wait_ge(o_ready, 2)
                            dve.wait_ge(skip_done, 1)
                            nc.vector.scalar_tensor_tensor(h_out[:, :], ps[:, 6, :], keep[:, :], h_skip[:, :], ALU.mult,
                                                           ALU.add).then_inc(h_new, 1)

                    norm(0)
                    norm(1)
                    for e in range(0, 8, 2):
                        x_low(e)
                        x_low(e + 1)
                        for f in (e, e + 1):
                            if NORMS[f][0] != 2:
                                add(f)
                            if f + 2 < 8:
                                norm(f + 2)
                    hydra(0)
                    hydra(1)
                    add_up(0)
                    norm(8)
                    add_up(1)
                    norm(9)
                    x_low(8)
                    x_low(9)
                    add_up(2)
                    norm(10)
                    add(8)
                    add_up(3)
                    norm(11)
                    add(9)
                    x_low(10)
                    x_low(11)
                    add(10)
                    add(11)

                @block.tensor
                def _(pe):
                    def transposes(e):
                        pe.wait_ge(xn_done, e + 1)
                        for h in range(2):
                            if e:
                                pe.wait_ge(xlo_done, 2 * (e - 1) + h + 1)
                            for k in range(4):
                                mm = nc.tensor.transpose(ps[:, XT0 + h, k * P:(k + 1) * P],
                                                         xn[:, e % 2, (4 * h + k) * P:(4 * h + k + 1) * P], con["ident"][:, :])
                            mm.then_inc(xt_ready, 1)

                    def split_product(out, a_hi, a_lo, b_hi, b_lo, first, last):
                        nc.tensor.matmul(out, a_hi, b_hi, start=first, stop=False)
                        nc.tensor.matmul(out, a_lo, b_hi, start=False, stop=False)
                        return nc.tensor.matmul(out, a_hi, b_lo, start=False, stop=last)

                    def gemm(e):
                        g, s = GEMMS.index(e), e % 2
                        pe.wait_ge(xlo_done, 2 * (e + 1))
                        for h in range(2):
                            if g:
                                pe.wait_ge(y_added, 2 * (g - 1) + h + 1)
                            cols = slice(h * HALF, (h + 1) * HALF)
                            for k in range(CH):
                                mm = split_product(ps[:, Y0 + h, :], xt_hi[:, s, k, :], xt_lo[:, s, k, :], w_hi[:, k, cols],
                                                   w_lo[:, k, cols], k == 0, k == CH - 1)
                            mm.then_inc(y_ready, 1)

                    def down(e):
                        s, n = e % 2, KIND2.index(e)
                        pe.wait_ge(xlo_done, 2 * (e + 1))
                        if n:
                            pe.wait_ge(h_done, n)
                        for k in range(CH):
                            mm = split_product(ps[:, DOWN, 0:P], wd_hi[:, k, :], wd_lo[:, k, :], xt_hi[:, s, k, :],
                                               xt_lo[:, s, k, :], k == 0, k == CH - 1)
                        mm.then_inc(down_ready, 1)

                    def up(t):
                        for h in range(2):
                            if t:
                                pe.wait_ge(up_added, 2 * (t - 1) + h + 1)
                            nc.tensor.matmul(ps[:, UP0 + h, :], h_out[:, t * P:(t + 1) * P], par["up_t"][:, h * HALF:(h + 1) * HALF],
                                             start=True, stop=True).then_inc(up_ready, 1)

                    def hydra(q):
                        h = h_mid if q == 0 else h_next
                        if q == 0:
                            pe.wait_ge(h_done, TILES)
                        else:
                            pe.wait_ge(h_new, 1)
                        nc.tensor.matmul(ps[:, 4, :], par["wx_t"][:, 0:P], h[:, :], start=True, stop=True).then_inc(xbc_ready, 1)
                        nc.tensor.matmul(ps[:, 5, :], par["wx_t"][:, P:2 * P], h[:, :], start=True, stop=True).then_inc(xbc_ready, 1)
                        nc.tensor.matmul(ps[0:C_ROW + DST, 6, :], par["wbc_t"][:, :], h[:, :], start=True, stop=True).then_inc(xbc_ready, 1)
                        for t in range(TILES):
                            nc.tensor.matmul(ps[:, 7, t * 2 * NH:(t + 1) * 2 * NH], h[:, t * P:(t + 1) * P], par["wdt_t"][:, :],
                                             start=True, stop=True).then_inc(dt_ready, 1)
                        taps = 3 * (TAPS - 1) * q + 3 * (TAPS - 2)
                        for k in range(2):
                            pe.wait_ge(taps_done, taps + k + 1)
                            for t in range(2 * k, 2 * k + 2):
                                mm = nc.tensor.matmul(ps[:, 4 + k, (t % 2) * DIN:(t % 2 + 1) * DIN], h[:, t * P:(t + 1) * P],
                                                      par["wz_t"][:, :], start=True, stop=True)
                            mm.then_inc(z_ready, 1)
                        pe.wait_ge(xf_done, 2 * (q + 1))
                        for k in range(2):
                            if k == 0:
                                pe.wait_ge(taps_done, taps + 3)
                            else:
                                pe.wait_ge(dt_step, 4 * q + 1)
                            for t in range(2 * k, 2 * k + 2):
                                for m in range(2):
                                    mm = nc.tensor.transpose(ps[:, 6 + k, (t % 2) * DIN + m * P:(t % 2) * DIN + (m + 1) * P],
                                                             x_feat[:, m, t * P:(t + 1) * P], con["ident"][:, :])
                            mm.then_inc(xtok_ready, 1)
                        pe.wait_ge(bc_done, 2 * (q + 1))
                        pe.wait_ge(z_done, 2 * q + 1)
                        for t in range(TILES):
                            cols = slice(t * P, (t + 1) * P)
                            mm = nc.tensor.matmul(ps[:, 4, cols], b_feat[:, cols], c_feat[:, cols], start=True, stop=True)
                        mm.then_inc(cb_ready, 1)
                        pe.wait_ge(z_done, 2 * q + 2)
                        for t in range(TILES):
                            for m in range(2):
                                nc.tensor.matmul(ps[:, 5, 256 + t * NH:256 + (t + 1) * NH], x_feat[:, m, t * P:(t + 1) * P],
                                                 par["fcd_t"][:, m, :], start=(m == 0), stop=(m == 1))
                        pe.wait_ge(reach_done, q + 1)
                        for d, between in ((0, "later"), (1, "earlier")):
                            n = TILES * NH * L
                            mm = nc.tensor.matmul(ps[:, 5, d * n:(d + 1) * n], con[between][:, :],
                                                  dt_reach[:, :, d * NH:(d + 1) * NH, :].rearrange("p t h l -> p t (h l)"),
                                                  start=True, stop=True)
                        mm.then_inc(decay_ready, 1)
                        pe.wait_ge(xtok_done, 2 * (q + 1))
                        for t in range(TILES):
                            pe.wait_ge(mixer_done, TILES * q + t + 1)
                            if t >= 2:
                                pe.wait_ge(yz_done, TILES * q + t - 1)
                            for n in range(NH):
                                cols = slice(n * HD, (n + 1) * HD)
                                mm = nc.tensor.matmul(ps[:, 6 + t % 2, cols], mixer[:, t % 2, n, :], x_tok[:, t, cols],
                                                      start=True, stop=True)
                            mm.then_inc(ym_ready, 1)
                        pe.wait_ge(w_done, q + 1)
                        pe.wait_ge(yn_done, TILES * (q + 1))
                        for k in range(2):
                            for t in range(TILES):
                                mm = nc.tensor.transpose(ps[:, 4 + k, t * P:(t + 1) * P], yz[:, t, k * P:(k + 1) * P], con["ident"][:, :])
                            mm.then_inc(yf_ready, 1)
                        pe.wait_ge(yz_done, TILES * (q + 1))
                        for k in range(2):
                            pe.wait_ge(yf_done, 2 * q + k + 1)
                            mm = nc.tensor.matmul(ps[:, 6, :], wout[:, k, :], yn_feat[:, k, :], start=(k == 0), stop=(k == 1))
                        mm.then_inc(o_ready, 1)

                    for e in range(0, 8, 2):
                        transposes(e)
                        transposes(e + 1)
                        for f in (e, e + 1):
                            if NORMS[f][0] == 2:
                                down(f)
                            else:
                                gemm(f)
                    hydra(0)
                    hydra(1)
                    pe.wait_ge(h_new, 2)
                    up(0)
                    up(1)
                    transposes(8)
                    transposes(9)
                    gemm(8)
                    up(2)
                    gemm(9)
                    up(3)
                    transposes(10)
                    transposes(11)
                    gemm(10)
                    gemm(11)

            nc.all_engine_barrier(sems_to_clear=range(step_sems[0].num, step_sems[-1].num + 1))

def inverse_transform(n):
    import numpy as np

    k = np.arange(n)
    out = np.empty((n, n))
    out[0] = 1.0 / np.sqrt(n)
    for f in range(1, (n - 1) // 2 + 1):
        angle = 2.0 * np.pi * ((f * k) % n) / n
        out[2 * f - 1] = np.sqrt(2.0 / n) * np.cos(angle)
        out[2 * f] = np.sqrt(2.0 / n) * np.sin(angle)
    if n % 2 == 0:
        out[n - 1] = np.where(k % 2 == 0, 1.0, -1.0) / np.sqrt(n)
    return out.astype(np.float32)


def kernel(**inputs):
    import ml_dtypes
    import numpy as np
    import concourse.bacc as bacc
    from concourse import mybir as mb
    from concourse.bass_utils import run_bass_kernel_spmd as run

    f32, bf16 = np.float32, ml_dtypes.bfloat16
    a = {n: np.asarray(v) for n, v in inputs.items()}
    att = {n[len("L0_attn_a_"):]: v for n, v in a.items() if n.startswith("L0_attn_a_")}
    hyd = {n[len("L0_attn_b_"):]: v for n, v in a.items() if n.startswith("L0_attn_b_")}
    ffn = {n[len("L0_ffn_"):]: v for n, v in a.items() if n.startswith("L0_ffn_")}
    x = att["x"]
    L, T, D = x.shape
    head = att["wk_w"].shape[0]
    PB = P // L
    NH, DIN = hyd["hy_fcD_w"].shape
    DM = hyd["w_down"].shape[0]
    DST = (hyd["hy_in_w"].shape[0] - 2 * DIN - 2 * NH) // 2
    TAPS = hyd["hy_conv_w"].shape[2]
    C_ROW = 32

    def rows(v, n=P):
        return np.broadcast_to(v.reshape(1, -1), (n, v.size))

    def chunks(m):
        return m.reshape(-1, P, m.shape[1]).transpose(1, 0, 2)

    def bc_rows(m):
        out = np.zeros((C_ROW + DST,) + m.shape[1:], m.dtype)
        out[:DST], out[C_ROW:] = m[:DST], m[DST:]
        return out

    def conv_rows(m):
        out = np.zeros((P, 3, m.shape[1]), m.dtype)
        out[:, 0], out[:, 1], out[:C_ROW + DST, 2] = m[:P], m[P:2 * P], bc_rows(m[DIN:])
        return out

    row, pos = np.arange(P) // PB, np.arange(P) % PB
    t = np.arange(L)
    same_pos = pos[:, None] == pos[None, :]
    lt, gt = row[:, None] < row[None, :], row[:, None] > row[None, :]
    kv_scale = np.ones((P, 1), f32)
    kv_scale[:3 * head] = 1.0 / np.sqrt(f32(head))
    reach = np.stack([row[:, None] <= t - 1] * NH + [row[:, None] >= t + 1] * NH, 1)
    consts = {
        "ident": np.eye(P), "before": same_pos & lt, "after": same_pos & gt, "later": same_pos & gt,
        "earlier": same_pos & lt, "reach": reach, "side": np.stack([row[:, None] < t, row[:, None] > t], 1),
        "same": row[:, None] == t, "dft_t": inverse_transform(D),
    }
    consts = {n: v.astype(f32) for n, v in consts.items()}
    attn = {
        "x": x, "wq_t": att["wq_w"].T, "wkv_t": np.concatenate([att["wk_w"]] * 3 + [att["wv_w"]]).T, "wo_t": att["wo_w"].T,
        "bq": att["wq_b"].reshape(-1, P).T, "bkv": np.concatenate([att["wk_b"]] * 3 + [att["wv_b"]])[:, None],
        "kv_scale": kv_scale, "bo": rows(att["wo_b"]), "ident": consts["ident"], "ident_b": np.eye(P).astype(bf16),
        "causal_b": np.where(np.tril(np.ones((P, P), bool)), 0.0, -1e30).astype(bf16),
    }
    in_w = hyd["hy_in_w"]
    mix = {
        "base_t": ffn["W_base"].T, "enc": np.concatenate([ffn["enc0"], ffn["enc1"]]),
        "coefs": np.concatenate([ffn["coefs0"], ffn["coefs1"]], 2).transpose(1, 0, 2),
        "masks": np.concatenate([ffn["mask0"], ffn["mask1"]], 2).transpose(1, 0, 2),
        "base_b": rows(ffn["b_base"]), "up_t": hyd["w_up"].T, "up_b": rows(hyd["b_up"]), "down_b": hyd["b_down"][:, None],
        "down_t": chunks(hyd["w_down"].T).reshape(P, -1), "gate": rows(hyd["gate1"]),
        "wz_t": in_w[:DIN].T, "wx_t": in_w[DIN:2 * DIN].T, "wbc_t": bc_rows(in_w[2 * DIN:2 * DIN + 2 * DST]).T,
        "wdt_t": in_w[2 * DIN + 2 * DST:].T, "conv_w": conv_rows(hyd["hy_conv_w"][:, 0, :]),
        "conv_b": conv_rows(hyd["hy_conv_b"][:, None])[:, :, 0], "dt_b": rows(np.concatenate([hyd["hy_dt_bias"]] * 2)),
        "a_log": rows(np.concatenate([hyd["hy_A_log"]] * 2)), "d_row": rows(hyd["hy_D"]), "fcd_t": chunks(hyd["hy_fcD_w"].T),
        "norm_w": hyd["hy_norm_w"].reshape(-1, P).T, "wout_t": chunks(hyd["hy_out_w"].T),
    }
    mix["coefs"] = chunks(mix["coefs"].reshape(D, -1)).reshape(P, D // P, *mix["coefs"].shape[1:])
    mix["masks"] = chunks(mix["masks"].reshape(D, -1)).reshape(P, D // P, *mix["masks"].shape[1:])

    nc = bacc.Bacc("TRN2", target_bir_lowering=False, num_devices=1)
    arrays = {}

    def declare(group, prefix):
        aps = {}
        for n, v in group.items():
            v = arrays[prefix + n] = np.ascontiguousarray(v)
            aps[n] = nc.dram_tensor(prefix + n, v.shape, mb.dt.from_np(v.dtype), kind="ExternalInput").ap()
        return aps

    at, mx, cn = declare(attn, "in_a_"), declare(mix, "in_m_"), declare(consts, "in_c_")
    out = nc.dram_tensor("out_0", x.shape, F32, kind="ExternalOutput").ap()
    wq_split = nc.dram_tensor("wq_split", (2, D // P, P, D // P, P), F32).ap()
    x1 = nc.dram_tensor("x1", x.shape, F32).ap()
    attention_program(nc, *(at[n] for n in ("x", "wq_t", "wkv_t", "wo_t", "bq", "bkv", "kv_scale", "bo", "ident", "ident_b",
                                            "causal_b")), wq_split, x1)
    mixer_program(nc, x1, mx, cn, out)
    r = run(nc, [arrays], core_ids=[0])
    return r.results[0]["out_0"]
```

```python
from contextlib import ExitStack

import concourse.bass as bass
from concourse import mybir

P = 128
EPS = 1e-5
ALU = mybir.AluOpType
ACT = mybir.ActivationFunctionType
AX = mybir.AxisListType
F32 = mybir.dt.float32
F32R = mybir.dt.float32r
BF16 = mybir.dt.bfloat16
U8 = mybir.dt.uint8
def attention_program(nc, x, wq_t, wkv_t, wo_t, bq, bkv, kv_scale, bo, ident, ident_b, causal_b, wq_split, x1):
    BATCH, T, D = x.shape
    HEAD = wkv_t.shape[1] // 4
    TILES, CH = T // P, D // P
    GROUPS, GH = D // P, P // HEAD
    HALF = 512
    KROWS = 3 * HEAD
    FIT = [min(GH, TILES // (i + 1)) for i in range(TILES)]
    IN_GROUP = [(i, range(j, j + FIT[i])) for i in range(TILES) for j in range(0, GH, FIT[i])]
    PER_GROUP = len(IN_GROUP)
    UNITS = GROUPS * PER_GROUP
    S_RING, P_RING, T_RING, STAT = 3, 3, 2, 8
    T_LAG, AV_LAG = 2, 3
    KV, PROJ, XT0 = 2, 3, 4
    Q_UNITS = 3
    INV_AT, SPREAD_AT, COPY_AT, SCALE_AT, HIGH_AT, LOW_AT = 2, 6, 7, 8, 9, 9

    def unit(u):
        i, heads = IN_GROUP[u % PER_GROUP]
        return u // PER_GROUP, i, heads, (i + 1) * P

    def finishing(s, at):
        return s // PER_GROUP - 1 if s >= PER_GROUP and s % PER_GROUP == at else None

    with ExitStack() as ctx:
        def sb(name, shape, dt=F32):
            return ctx.enter_context(nc.sbuf_tensor(name, shape, dt))

        def sem(name):
            return ctx.enter_context(nc.semaphore(name))

        wo_hi, wo_lo = sb("wo_hi", [P, CH, D], F32R), sb("wo_lo", [P, CH, D], F32R)
        wkv_hi, wkv_lo = sb("wkv_hi", [P, CH, P], F32R), sb("wkv_lo", [P, CH, P], F32R)
        wq_hi, wq_lo = sb("wq_hi", [P, CH, P], F32R), sb("wq_lo", [P, CH, P], F32R)
        x_ring = sb("x_ring", [P, 2, D])
        r_ring = sb("r_ring", [P, 2, D])
        xn_hi, xn_lo = sb("xn_hi", [P, CH, T], F32R), sb("xn_lo", [P, CH, T], F32R)
        at_hi, at_lo = sb("at_hi", [P, CH, T], F32R), sb("at_lo", [P, CH, T], F32R)
        q_hi, q_lo = sb("q_hi", [P, T], F32R), sb("q_lo", [P, T], F32R)
        q_stack = sb("q_stack", [KROWS, 2, GH, T], F32R)
        k_stack = sb("k_stack", [KROWS, T], F32R)
        v_pad = sb("v_pad", [P, TILES, 7 * HEAD])
        probs = sb("probs", [P, P_RING, T])
        probs_t = sb("probs_t", [P, T_RING, T])
        neg_max = sb("neg_max", [P, STAT, GH])
        den, inv_den = sb("den", [P, 2, TILES, GH]), sb("inv_den", [P, 2, TILES, GH])
        inv_rows, att = sb("inv_rows", [P, T]), sb("att", [P, T])
        stats, mean_var = sb("stats", [P, 2, 2, 6]), sb("mean_var", [P, 2, 2])
        var_eps, inv_std, neg_half = sb("var_eps", [P, 2]), sb("inv_std", [P, 2]), sb("neg_half", [P, 1])
        bo_rows = sb("bo_rows", [P, D])
        bq_sb, bkv_sb, kvs_sb, bkv_scaled = sb("bq_sb", [P, CH]), sb("bkv_sb", [P, 1]), sb("kvs_sb", [P, 1]), sb("bkv_scaled", [P, 1])
        ident_sb, identb_sb, causal_sb = sb("ident_sb", [P, P]), sb("identb_sb", [P, P], BF16), sb("causal_sb", [P, P], BF16)
        ps = ctx.enter_context(nc.psum_tensor("ps_attn", [P, 8, HALF], F32))

        params_in, stage_in, staged_hi, staged_lo = (sem("params_in"), [sem("stage_in_0"), sem("stage_in_1")], sem("staged_hi"),
                                                     sem("staged_lo"))
        wq_out, setup_done, bkv_ready = sem("wq_out"), sem("setup_done"), sem("bkv_ready")
        DMA = 16
        STACK_DMAS = 3 * GH
        def wq_chunk(a, b, c):
            return (a if c < CH // 2 else b)[:, 2 * (c % (CH // 2)):2 * (c % (CH // 2)) + 2, :].rearrange("p a m -> p (a m)")

        staged = [(wkv_t.rearrange("(c p) m -> p c m", p=P), wkv_hi[:, :, :], wkv_lo[:, :, :])]
        staged += [(wq_t[c * P:(c + 1) * P, :], wq_chunk(at_hi, at_lo, c), wq_chunk(xn_hi, xn_lo, c)) for c in range(CH)]
        staged += [(wo_t[c * P:(c + 1) * P, :], wo_hi[:, c, :], wo_lo[:, c, :]) for c in range(CH)]

        def stage(n):
            s = r_ring[:, n % 2, :]
            return s.rearrange("p (c m) -> p c m", c=CH) if n == 0 else s

        with nc.Block() as block:
            @block.sync
            def _(sp):
                for n, (src, _, _) in enumerate(staged):
                    if n >= 2:
                        sp.wait_ge(staged_lo, n - 1)
                    sp.dma_start(stage(n), src).then_inc(stage_in[n % 2], DMA)
                    if 0 <= n - 3 < CH:
                        for part, w in enumerate(staged[n - 2][1:]):
                            sp.dma_start(wq_split[part, :, :, n - 3, :].rearrange("g p m -> p g m"),
                                         w.bitcast(F32).rearrange("p (g m) -> p g m", g=GROUPS)).then_inc(wq_out, DMA)
                sp.wait_ge(wq_out, 2 * CH * DMA)

            @block.gpsimd
            def _(pool):
                nc.gpsimd.memset(neg_half[:, :], -0.5).then_inc(setup_done, 1)
                nc.gpsimd.memset(v_pad[:, :, :], 0.0).then_inc(setup_done, 1)
                pool.wait_ge(params_in, 7 * DMA)
                nc.gpsimd.tensor_tensor(bkv_scaled[:, :], bkv_sb[:, :], kvs_sb[:, :], ALU.mult).then_inc(bkv_ready, 1)
                pool.wait_ge(setup_done, 2)

            @block.scalar
            def _(act):
                params = [(ident_sb[:, :], ident), (identb_sb[:, :], ident_b), (causal_sb[:, :], causal_b),
                          (bo_rows[:, :], bo), (bq_sb[:, :], bq), (bkv_sb[:, :], bkv), (kvs_sb[:, :], kv_scale)]
                for dst, src in params:
                    act.dma_start(dst, src).then_inc(params_in, DMA)
                for n, (_, hi, _) in enumerate(staged):
                    act.wait_ge(stage_in[n % 2], DMA * (n // 2 + 1))
                    nc.scalar.copy(hi, stage(n)).then_inc(staged_hi, 1)
                act.wait_ge(bkv_ready, 1)
                act.wait_ge(params_in, 7 * DMA)

            @block.vector
            def _(dve):
                for n, (_, hi, lo) in enumerate(staged):
                    dve.wait_ge(staged_hi, n + 1)
                    nc.vector.tensor_tensor(lo, stage(n), hi.bitcast(F32), ALU.subtract).then_inc(staged_lo, 1)
                dve.wait_ge(setup_done, 2)
                dve.wait_ge(params_in, 7 * DMA)

            @block.tensor
            def _(pe):
                pe.wait_ge(params_in, 7 * DMA)
                pe.wait_ge(staged_lo, len(staged))

        row_sems = []

        def row_sem(name):
            row_sems.append(sem(name))
            return row_sems[-1]

        x_in, stats_done, mv_done, eps_done, std_done, xn_done = ([row_sem("x_in_0"), row_sem("x_in_1")],
                                                                  row_sem("stats_done"), row_sem("mv_done"),
                                                                  row_sem("eps_done"), row_sem("std_done"), row_sem("xn_done"))
        xt_ready, xhi_done, xlo_done = row_sem("xt_ready"), row_sem("xhi_done"), row_sem("xlo_done")
        kv_ready, kv_done, khi_done, k_done, vt_ready, v_done = (row_sem("kv_ready"), row_sem("kv_done"), row_sem("khi_done"),
                                                                 row_sem("k_done"), row_sem("vt_ready"), row_sem("v_done"))
        wq_in, q_ready, qhi_done, qlo_done, qs_in = (row_sem("wq_in"), row_sem("q_ready"), row_sem("qhi_done"), row_sem("qlo_done"),
                                                        row_sem("qs_in"))
        s_ready, max_done, exp_done, inv_done, wide_done, spread_ready, spread_done, att_done = (
            row_sem("s_ready"), row_sem("max_done"), row_sem("exp_done"), row_sem("inv_done"), row_sem("wide_done"), row_sem("spread_ready"),
            row_sem("spread_done"), row_sem("att_done"))
        pt_ready, pt_done, av_done, ohi_done, olo_done = (row_sem("pt_ready"), row_sem("pt_done"), row_sem("av_done"),
                                                          row_sem("ohi_done"), row_sem("olo_done"))
        r_in, r_bias, y_ready, y_used, x1_done, x1_out = ([row_sem("r_in_0"), row_sem("r_in_1")], row_sem("r_bias"), row_sem("y_ready"), row_sem("y_used"),
                                                          row_sem("x1_done"), [row_sem("x1_out_0"), row_sem("x1_out_1")])

        def row(b, nxt):
            def q_count(g):
                return g if b is not None else g - GROUPS + 1

            def wq_count(g):
                return g - 1 if b is not None else g - GROUPS + 1

            with nc.Block(no_gpsimd_drain=True) as block:

                @block.sync
                def _(sp):
                    def load_x(t):
                        if t >= 2:
                            sp.wait_ge(xt_ready, 2 * (t - 1))
                        sp.dma_start(x_ring[:, t % 2, :], x[nxt, t * P:(t + 1) * P, :]).then_inc(x_in[t % 2], DMA)

                    def load_wq(g):
                        if b is not None or g > GROUPS:
                            sp.wait_ge(q_ready, q_count(g - 1))
                        for part, w in ((0, wq_hi), (1, wq_lo)):
                            sp.dma_start(w[:, :, :].bitcast(F32), wq_split[part, g % GROUPS]).then_inc(wq_in, DMA)

                    def stack(g):
                        sp.wait_ge(qhi_done, q_count(g))
                        if 2 <= g < GROUPS:
                            sp.wait_ge(s_ready, (g - 1) * PER_GROUP)
                        for place, src in ((0, q_hi), (2, q_hi), (1, q_lo)):
                            if place == 1:
                                sp.wait_ge(qlo_done, q_count(g))
                            for j in range(GH):
                                sp.dma_start(q_stack[place * HEAD:(place + 1) * HEAD, g % 2, j, :].bitcast(F32),
                                             src[j * HEAD:(j + 1) * HEAD, :].bitcast(F32)).then_inc(qs_in, DMA)

                    def load_r(t):
                        if t >= 2:
                            sp.wait_ge(x1_out[t % 2], (t // 2) * DMA)
                        sp.dma_start(r_ring[:, t % 2, :], x[b, t * P:(t + 1) * P, :]).then_inc(r_in[t % 2], DMA)

                    def store(t):
                        sp.wait_ge(x1_done, t + 1)
                        sp.dma_start(x1[b, t * P:(t + 1) * P, :], r_ring[:, t % 2, :]).then_inc(x1_out[t % 2], DMA)

                    if nxt is not None:
                        load_x(0)
                        load_x(1)
                    if b is not None:
                        load_r(0)
                        load_r(1)
                        for g in range(1, GROUPS):
                            if g + 1 < GROUPS or nxt is not None:
                                load_wq(g + 1)
                            stack(g)
                    elif nxt is not None:
                        load_wq(GROUPS)
                    if nxt is not None:
                        load_x(2)
                        load_x(3)
                    if b is not None:
                        store(0)
                        load_r(2)
                        store(1)
                        load_r(3)
                    if nxt is not None:
                        load_wq(GROUPS + 1)
                        stack(GROUPS)
                    if b is not None:
                        store(2)
                        store(3)
                        for n in range(2):
                            sp.wait_ge(x1_out[n], TILES // 2 * DMA)
                    if nxt is not None:
                        sp.wait_ge(wq_in, wq_count(GROUPS + 1) * 2 * DMA)
                        sp.wait_ge(qs_in, q_count(GROUPS) * STACK_DMAS * DMA)

                @block.gpsimd
                def _(pool):
                    def inv_sqrt(t):
                        pool.wait_ge(mv_done, t + 1)
                        nc.gpsimd.tensor_scalar(var_eps[:, t % 2:t % 2 + 1], mean_var[:, t % 2, 1:2], EPS, None,
                                                ALU.add).then_inc(eps_done, 1)
                        pool.wait_ge(eps_done, t + 1)
                        nc.gpsimd.tensor_tensor(inv_std[:, t % 2:t % 2 + 1], var_eps[:, t % 2:t % 2 + 1], neg_half[:, :],
                                                ALU.pow).then_inc(std_done, 1)

                    def widen(g):
                        pool.wait_ge(inv_done, g + 1)
                        if g:
                            pool.wait_ge(olo_done, g)
                        nc.gpsimd.tensor_copy(att[:, :].rearrange("p (i j d) -> p i j d", i=TILES, j=GH),
                                              inv_den[:, g % 2, :, :, None].to_broadcast([P, TILES, GH, HEAD])).then_inc(wide_done, 1)

                    def add_bias(t):
                        pool.wait_ge(r_in[t % 2], (t // 2 + 1) * DMA)
                        nc.gpsimd.tensor_tensor(r_ring[:, t % 2, :], r_ring[:, t % 2, :], bo_rows[:, :],
                                                ALU.add).then_inc(r_bias, 1)

                    if b is not None:
                        add_bias(0)
                        add_bias(1)
                        for g in range(GROUPS - 1):
                            widen(g)
                    if nxt is not None:
                        inv_sqrt(0)
                        inv_sqrt(1)
                    if b is not None:
                        widen(GROUPS - 1)
                    if nxt is not None:
                        inv_sqrt(2)
                        inv_sqrt(3)
                    if b is not None:
                        add_bias(2)
                        add_bias(3)

                @block.scalar
                def _(act):
                    def q_high(g):
                        act.wait_ge(q_ready, q_count(g))
                        if q_count(g) > 1:
                            act.wait_ge(qs_in, (q_count(g) - 1) * STACK_DMAS * DMA)
                        nc.scalar.activation(q_hi[:, :], ps[:, PROJ, :], ACT.Identity,
                                             bias=bq_sb[:, g % GROUPS:g % GROUPS + 1]).then_inc(qhi_done, 1)

                    def finish_copy(g):
                        act.wait_ge(spread_ready, g + 1)
                        if g:
                            act.wait_ge(att_done, g)
                        nc.scalar.copy(inv_rows[:, :], ps[:, PROJ, :]).then_inc(spread_done, 1)

                    def finish_high(g):
                        act.wait_ge(att_done, g + 1)
                        nc.scalar.copy(at_hi[:, g, :], att[:, :]).then_inc(ohi_done, 1)

                    def x_high(t):
                        for h in range(2):
                            act.wait_ge(xt_ready, 2 * t + h + 1)
                            nc.scalar.copy(xn_hi[:, 4 * h:4 * h + 4, t * P:(t + 1) * P],
                                           ps[:, XT0 + h, :].rearrange("p (c t) -> p c t", t=P)).then_inc(xhi_done, 1)

                    if b is not None:
                        for s in range(UNITS):
                            g, i, heads, n = unit(s)
                            if s % PER_GROUP == 0 and g >= 2:
                                act.wait_ge(inv_done, g - 1)
                            act.wait_ge(max_done, s + 1)
                            if s >= P_RING:
                                act.wait_ge(pt_ready, s - P_RING + 1)
                            for m, j in enumerate(heads):
                                exp = nc.scalar.activation(probs[:, s % P_RING, m * n:(m + 1) * n],
                                                           ps[:, s % S_RING, m * n:(m + 1) * n], ACT.Exp,
                                                           bias=neg_max[:, s % STAT, m:m + 1], accum_out=den[:, g % 2, i, j:j + 1])
                            exp.then_inc(exp_done, 1)
                            if s % PER_GROUP == Q_UNITS and g + 1 < GROUPS:
                                q_high(g + 1)
                            if (done := finishing(s, COPY_AT)) is not None:
                                finish_copy(done)
                            if (done := finishing(s, HIGH_AT)) is not None:
                                finish_high(done)
                    if nxt is not None:
                        x_high(0)
                    if b is not None:
                        finish_copy(GROUPS - 1)
                    if nxt is not None:
                        x_high(1)
                    if b is not None:
                        finish_high(GROUPS - 1)
                    if nxt is not None:
                        x_high(2)
                        x_high(3)
                        act.wait_ge(kv_ready, 1)
                        if b is not None:
                            act.wait_ge(olo_done, GROUPS)
                        nc.scalar.activation(att[:, :], ps[:, KV, :], ACT.Identity, bias=bkv_scaled[:, :],
                                             scale=kvs_sb[:, :]).then_inc(kv_done, 1)
                        q_high(GROUPS)

                @block.vector
                def _(dve):
                    def q_low(g):
                        dve.wait_ge(qhi_done, q_count(g))
                        if q_count(g) > 1:
                            dve.wait_ge(qs_in, (q_count(g) - 1) * STACK_DMAS * DMA)
                        nc.vector.scalar_tensor_tensor(q_lo[:, :], ps[:, PROJ, :], bq_sb[:, g % GROUPS:g % GROUPS + 1],
                                                       q_hi[:, :].bitcast(F32), ALU.add, ALU.subtract).then_inc(qlo_done, 1)

                    def finish_inverse(g):
                        dve.wait_ge(exp_done, (g + 1) * PER_GROUP)
                        if g >= 2:
                            dve.wait_ge(wide_done, g - 1)
                        nc.vector.reciprocal(inv_den[:, g % 2, :, :], den[:, g % 2, :, :]).then_inc(inv_done, 1)

                    def finish_scale(g):
                        dve.wait_ge(av_done, (g + 1) * PER_GROUP)
                        dve.wait_ge(spread_done, g + 1)
                        if g:
                            dve.wait_ge(olo_done, g)
                        nc.vector.tensor_tensor(att[:, :], ps[:, 6 + g % 2, :], inv_rows[:, :], ALU.mult).then_inc(att_done, 1)

                    def finish_low(g):
                        dve.wait_ge(ohi_done, g + 1)
                        nc.vector.tensor_tensor(at_lo[:, g, :], att[:, :], at_hi[:, g, :].bitcast(F32),
                                                ALU.subtract).then_inc(olo_done, 1)

                    def moments(t):
                        dve.wait_ge(x_in[t % 2], (t // 2 + 1) * DMA)
                        for h in range(2):
                            nc.vector.bn_stats(stats[:, t % 2, h, :], x_ring[:, t % 2, h * HALF:(h + 1) * HALF]).then_inc(stats_done, 1)
                        dve.wait_ge(stats_done, (t + 1) * 2)
                        nc.vector.bn_aggr(mean_var[:, t % 2, :], stats[:, t % 2, :, :]).then_inc(mv_done, 1)

                    def normalise(t):
                        dve.wait_ge(mv_done, t + 1)
                        dve.wait_ge(std_done, t + 1)
                        nc.vector.tensor_scalar(x_ring[:, t % 2, :], x_ring[:, t % 2, :], mean_var[:, t % 2, 0:1],
                                                inv_std[:, t % 2:t % 2 + 1], ALU.subtract, ALU.mult).then_inc(xn_done, 1)

                    def x_low(t):
                        for h in range(2):
                            dve.wait_ge(xhi_done, 2 * t + h + 1)
                            cols = (slice(None), slice(4 * h, 4 * h + 4), slice(t * P, (t + 1) * P))
                            nc.vector.tensor_tensor(xn_lo[cols], ps[:, XT0 + h, :].rearrange("p (c t) -> p c t", t=P),
                                                    xn_hi[cols].bitcast(F32), ALU.subtract).then_inc(xlo_done, 1)

                    def add_residual(t):
                        dve.wait_ge(r_bias, t + 1)
                        for h in range(2):
                            dve.wait_ge(y_ready, 2 * t + h + 1)
                            half = r_ring[:, t % 2, h * HALF:(h + 1) * HALF]
                            add = nc.vector.tensor_tensor(half, ps[:, h, :], half, ALU.add)
                            if h == 0:
                                add.then_inc(y_used, 1)
                            else:
                                add.then_inc(x1_done, 1)

                    if b is not None:
                        for s in range(UNITS + T_LAG):
                            if s < UNITS:
                                g, i, heads, n = unit(s)
                                dve.wait_ge(s_ready, s + 1)
                                nc.vector.tensor_reduce(neg_max[:, s % STAT, 0:len(heads)],
                                                        ps[:, s % S_RING, 0:n * len(heads)].rearrange("p (j k) -> p j k", k=n),
                                                        AX.X, ALU.max, negate=True).then_inc(max_done, 1)
                            if s >= T_LAG:
                                u = s - T_LAG
                                _, _, heads, n = unit(u)
                                dve.wait_ge(pt_ready, u + 1)
                                if u >= T_RING:
                                    dve.wait_ge(av_done, u - T_RING + 1)
                                cols = slice(0, n * len(heads))
                                nc.vector.tensor_copy(probs_t[:, u % T_RING, cols], ps[:, 4 + u % T_RING, cols]).then_inc(pt_done, 1)
                            if s < UNITS:
                                if s % PER_GROUP == Q_UNITS + 1 and g + 1 < GROUPS:
                                    q_low(g + 1)
                                if (done := finishing(s, INV_AT)) is not None:
                                    finish_inverse(done)
                                if (done := finishing(s, SCALE_AT)) is not None:
                                    finish_scale(done)
                                if (done := finishing(s, LOW_AT)) is not None:
                                    finish_low(done)
                                if nxt is not None and s // PER_GROUP == GROUPS - 1 and s % PER_GROUP in (3, 4, 5, 6):
                                    tile, part = divmod(s % PER_GROUP - 3, 2)
                                    (normalise if part else moments)(tile)
                        finish_inverse(GROUPS - 1)
                    elif nxt is not None:
                        for t in range(2):
                            moments(t)
                            normalise(t)
                    if nxt is not None:
                        x_low(0)
                        x_low(1)
                    if b is not None:
                        finish_scale(GROUPS - 1)
                        finish_low(GROUPS - 1)
                    if nxt is not None:
                        for t in (2, 3):
                            moments(t)
                            normalise(t)
                    if b is not None:
                        add_residual(0)
                    if nxt is not None:
                        x_low(2)
                    if b is not None:
                        add_residual(1)
                    if nxt is not None:
                        x_low(3)
                        dve.wait_ge(kv_done, 1)
                        nc.vector.tensor_copy(k_stack[:, :], att[0:KROWS, :]).then_inc(khi_done, 1)
                        dve.wait_ge(khi_done, 1)
                        low = slice(2 * HEAD, 3 * HEAD)
                        nc.vector.tensor_tensor(k_stack[low, :], att[low, :], k_stack[low, :].bitcast(F32),
                                                ALU.subtract).then_inc(k_done, 1)
                        dve.wait_ge(vt_ready, 1)
                        nc.vector.tensor_copy(v_pad[:, :, (GH - 1) * HEAD:GH * HEAD],
                                              ps[:, KV, 0:TILES * HEAD].rearrange("p (k d) -> p k d", d=HEAD)).then_inc(v_done, 1)
                        q_low(GROUPS)
                        dve.wait_ge(k_done, 1)
                        dve.wait_ge(v_done, 1)
                    if b is not None:
                        add_residual(2)
                        add_residual(3)

                @block.tensor
                def _(pe):
                    def split_product(out, a_hi, a_lo, b_hi, b_lo, first, last):
                        nc.tensor.matmul(out, a_hi, b_hi, start=first, stop=False)
                        nc.tensor.matmul(out, a_lo, b_hi, start=False, stop=False)
                        return nc.tensor.matmul(out, a_hi, b_lo, start=False, stop=last)

                    def q_part(g, chunks):
                        for c in chunks:
                            if c == 0:
                                if wq_count(g):
                                    pe.wait_ge(wq_in, wq_count(g) * 2 * DMA)
                            mm = split_product(ps[:, PROJ, :], wq_hi[:, c, :], wq_lo[:, c, :], xn_hi[:, c, :], xn_lo[:, c, :],
                                               c == 0, c == CH - 1)
                            if c == CH - 1:
                                mm.then_inc(q_ready, 1)

                    def finish_spread(g):
                        pe.wait_ge(wide_done, g + 1)
                        pe.wait_ge(qlo_done, min(g + 2, GROUPS - 1))
                        if g:
                            pe.wait_ge(spread_done, g)
                        for i in range(TILES):
                            mm = nc.tensor.matmul(ps[:, PROJ, i * P:(i + 1) * P], att[:, i * P:(i + 1) * P], ident_sb[:, :],
                                                  start=True, stop=True)
                        mm.then_inc(spread_ready, 1)

                    def transposes(t):
                        pe.wait_ge(xn_done, t + 1)
                        for h in range(2):
                            if t:
                                pe.wait_ge(xlo_done, 2 * (t - 1) + h + 1)
                            for c in range(4):
                                mm = nc.tensor.transpose(ps[:, XT0 + h, c * P:(c + 1) * P],
                                                         x_ring[:, t % 2, (4 * h + c) * P:(4 * h + c + 1) * P], ident_sb[:, :])
                            mm.then_inc(xt_ready, 1)

                    def output(t):
                        for h in range(2):
                            if t:
                                if h:
                                    pe.wait_ge(x1_done, t)
                                else:
                                    pe.wait_ge(y_used, t)
                            for c in range(CH):
                                if t == 0 and h == 0 and c >= CH - 2:
                                    pe.wait_ge(olo_done, c + 1)
                                tok = slice(t * P, (t + 1) * P)
                                out = slice(h * HALF, (h + 1) * HALF)
                                mm = split_product(ps[:, h, :], at_hi[:, c, tok], at_lo[:, c, tok], wo_hi[:, c, out],
                                                   wo_lo[:, c, out], c == 0, c == CH - 1)
                            mm.then_inc(y_ready, 1)

                    if b is not None:
                        for s in range(UNITS + AV_LAG):
                            if s < UNITS:
                                g, i, heads, n = unit(s)
                                if s % PER_GROUP == 0 and g:
                                    pe.wait_ge(qs_in, g * STACK_DMAS * DMA)
                                if s >= S_RING:
                                    pe.wait_ge(exp_done, s - S_RING + 1)
                                for m, j in enumerate(heads):
                                    cols = ps[:, s % S_RING, m * n:(m + 1) * n]
                                    nc.tensor.matmul(cols, q_stack[:, g % 2, j, i * P:(i + 1) * P], k_stack[:, 0:n],
                                                     start=True, stop=False)
                                    mm = nc.tensor.matmul(cols[:, n - P:n], identb_sb[:, :], causal_sb[:, :], start=False, stop=True)
                                mm.then_inc(s_ready, 1)
                                q_unit = s % PER_GROUP
                                if q_unit < Q_UNITS and g + 1 < GROUPS:
                                    if q_unit == 0 and g:
                                        pe.wait_ge(qlo_done, g)
                                        if g >= 2:
                                            pe.wait_ge(spread_done, g - 1)
                                    q_part(g + 1, range(q_unit * CH // Q_UNITS, (q_unit + 1) * CH // Q_UNITS))
                                if (done := finishing(s, SPREAD_AT)) is not None:
                                    finish_spread(done)
                            if T_LAG <= s < UNITS + T_LAG:
                                u = s - T_LAG
                                g, i, heads, n = unit(u)
                                pe.wait_ge(exp_done, u + 1)
                                if u >= T_RING:
                                    pe.wait_ge(pt_done, u - T_RING + 1)
                                for k in range(n * len(heads) // P):
                                    mm = nc.tensor.transpose(ps[:, 4 + u % T_RING, k * P:(k + 1) * P],
                                                             probs[:, u % P_RING, k * P:(k + 1) * P], ident_sb[:, :])
                                mm.then_inc(pt_ready, 1)
                            if s >= AV_LAG:
                                u = s - AV_LAG
                                g, i, heads, n = unit(u)
                                pe.wait_ge(pt_done, u + 1)
                                if u % PER_GROUP == 0 and g >= 2:
                                    pe.wait_ge(att_done, g - 1)
                                for m, j in enumerate(heads):
                                    for k in range(i + 1):
                                        lead = (GH - 1 - j) * HEAD
                                        cols = slice(m * n + k * P, m * n + (k + 1) * P)
                                        mm = nc.tensor.matmul(ps[:, 6 + g % 2, i * P:(i + 1) * P], v_pad[:, k, lead:lead + P],
                                                              probs_t[:, u % T_RING, cols],
                                                              start=(j == 0 and k == 0), stop=(j == GH - 1 and k == i))
                                mm.then_inc(av_done, 1)
                    if nxt is not None:
                        transposes(0)
                    if b is not None:
                        finish_spread(GROUPS - 1)
                    if nxt is not None:
                        transposes(1)
                    if b is not None:
                        output(0)
                    if nxt is not None:
                        transposes(2)
                    if b is not None:
                        output(1)
                    if nxt is not None:
                        transposes(3)
                        pe.wait_ge(xlo_done, 2 * TILES)
                        for c in range(CH):
                            mm = split_product(ps[:, KV, :], wkv_hi[:, c, :], wkv_lo[:, c, :], xn_hi[:, c, :], xn_lo[:, c, :],
                                               c == 0, c == CH - 1)
                        mm.then_inc(kv_ready, 1)
                        if b is not None:
                            pe.wait_ge(spread_done, GROUPS)
                        q_part(GROUPS, range(CH))
                        pe.wait_ge(kv_done, 1)
                        for k in range(TILES):
                            mm = nc.tensor.transpose(ps[:, KV, k * HEAD:(k + 1) * HEAD], att[3 * HEAD:4 * HEAD, k * P:(k + 1) * P],
                                                     ident_sb[3 * HEAD:4 * HEAD, 3 * HEAD:4 * HEAD])
                        mm.then_inc(vt_ready, 1)
                    if b is not None:
                        output(2)
                        output(3)

            nc.all_engine_barrier(sems_to_clear=range(row_sems[0].num, row_sems[-1].num + 1))

        row(None, 0)
        with nc.Fori(0, BATCH - 1) as b:
            row(b, b + 1)
        row(BATCH - 1, None)


def mixer_program(nc, x1, w, c, out):
    L, T, D = x1.shape
    PB = P // L
    TILES = 4
    STEPS = T // (PB * TILES)
    CH = D // P
    HALF = 512
    COLS = TILES * P
    DM = 128
    DIN, NH, DST, TAPS = 2 * DM, 4, 16, 7
    HD = DIN // NH
    C_ROW = 32
    RANK = w["enc"].shape[0]
    EXPERTS = w["coefs"].shape[2]
    SCALING = 0.5
    SP_STEPS = 13
    DMA = 16
    ORDER = [
        ("norm", (1, 0)), ("h_in", 0), ("norm", (1, 1)), ("turn", (1, 0)), ("gemm", (1, 0), 0), ("h_conv", 0, 0),
        ("gemm", (1, 0), 1), ("h_conv", 0, 1), ("add", (1, 0), 0), ("h_gates", 0), ("turn", (1, 1)), ("h_turn", 0), ("h_cb", 0),
        ("gemm", (1, 1), 0), ("add", (1, 0), 1), ("h_weight", 0), ("h_mix", 0), ("gemm", (1, 1), 1), ("norm", (2, 0)),
        ("h_norm", 0), ("h_back", 0), ("add", (1, 1), 0), ("turn", (2, 0)), ("norm", (1, 2)), ("h_out", 0),
        ("add", (1, 1), 1), ("h_in", 1), ("down", (2, 0)), ("turn", (1, 2)), ("gemm", (1, 2), 0), ("h_conv", 1, 0),
        ("gemm", (1, 2), 1), ("h_conv", 1, 1), ("norm", (2, 1)), ("h_gates", 1), ("add", (1, 2), 0), ("turn", (2, 1)),
        ("norm", (1, 3)), ("h_turn", 1), ("h_cb", 1), ("down", (2, 1)), ("add", (1, 2), 1), ("turn", (1, 3)),
        ("gemm", (1, 3), 0), ("h_weight", 1), ("h_mix", 1), ("gemm", (1, 3), 1), ("norm", (2, 2)), ("h_norm", 1),
        ("h_back", 1), ("add", (1, 3), 0), ("turn", (2, 2)), ("h_out", 1), ("add", (1, 3), 1), ("up", 0), ("down", (2, 2)),
        ("add_up", 0),
        ("norm", (2, 3)), ("up", 1), ("turn", (2, 3)), ("add_up", 1), ("norm", (3, 0)), ("down", (2, 3)), ("up", 2),
        ("turn", (3, 0)), ("norm", (3, 1)), ("gemm", (3, 0), 0), ("add_up", 2), ("turn", (3, 1)), ("gemm", (3, 0), 1),
        ("add", (3, 0), 0), ("norm", (3, 2)), ("up", 3), ("add", (3, 0), 1), ("gemm", (3, 1), 0), ("add_up", 3),
        ("turn", (3, 2)), ("norm", (3, 3)), ("gemm", (3, 1), 1), ("add", (3, 1), 0), ("turn", (3, 3)), ("add", (3, 1), 1),
        ("gemm", (3, 2), 0), ("gemm", (3, 2), 1), ("add", (3, 2), 0), ("add", (3, 2), 1), ("gemm", (3, 3), 0),
        ("gemm", (3, 3), 1), ("add", (3, 3), 0), ("add", (3, 3), 1),
    ]
    Y0, XT0, DOWN, UP0 = 0, 2, 0, 5

    with ExitStack() as ctx:
        def sb(name, shape, dt=F32):
            return ctx.enter_context(nc.sbuf_tensor("m_" + name, shape, dt))

        def sem(name):
            return ctx.enter_context(nc.semaphore("m_" + name))

        w_hi, w_lo = sb("w_hi", [P, CH, D], F32R), sb("w_lo", [P, CH, D], F32R)
        wd_hi, wd_lo = sb("wd_hi", [P, CH, DM], F32R), sb("wd_lo", [P, CH, DM], F32R)
        xs = sb("xs", [P, 2, TILES, D])
        xn = sb("xn", [P, 2, D])
        xt_hi, xt_lo = sb("xt_hi", [P, 2, CH, P], F32R), sb("xt_lo", [P, 2, CH, P], F32R)
        stats, mean_var = sb("stats", [P, 2, 2, 6]), sb("mean_var", [P, 2, 2])
        var_eps, inv_std, neg_half = sb("var_eps", [P, 2]), sb("inv_std", [P, 2]), sb("neg_half", [P, TILES])
        h_mid, h_next, h_last, h_skip = sb("h_mid", [P, 2, COLS]), sb("h_next", [P, COLS]), sb("h_last", [P, COLS]), sb("h_skip", [P, COLS])
        conv = sb("conv", [P, 3, COLS])
        x_feat = sb("x_feat", [P, 2, COLS])
        b_feat, c_feat = sb("b_feat", [DST, COLS]), sb("c_feat", [DST, COLS])
        x_tok, z_gate = sb("x_tok", [P, TILES, DIN]), sb("z_gate", [P, TILES, DIN])
        dt_raw, dt_tmp, dt, dta = (sb("dt_raw", [P, TILES, 2 * NH]), sb("dt_tmp", [P, TILES, 2 * NH]),
                                   sb("dt", [P, TILES, 2 * NH]), sb("dta", [P, TILES, 2 * NH]))
        sp_s, sp_s2, sp_t, sp_log = (sb(n, [P, TILES, 2 * NH]) for n in ("sp_s", "sp_s2", "sp_t", "sp_log"))
        dt_reach = sb("dt_reach", [P, TILES, 2 * NH, L])
        decay = sb("decay", [P, 2, TILES, NH, L])
        dt_mask = sb("dt_mask", [P, 2, TILES, NH, L])
        weight = sb("weight", [P, TILES, NH, L])
        d_term, d_diag = sb("d_term", [P, TILES, NH]), sb("d_diag", [P, TILES, NH, L])
        cb_fw, cb_bw, cb = sb("cb_fw", [P, TILES, P]), sb("cb_bw", [P, TILES, P]), sb("cb", [P, TILES, P])
        mixer = sb("mixer", [P, 2, NH, P])
        yz, square, sum_sq, y_std, y_inv = (sb("yz", [P, TILES, DIN]), sb("square", [P, DIN]), sb("sum_sq", [P, TILES]),
                                            sb("y_std", [P, TILES]), sb("y_inv", [P, TILES]))
        yn_feat = sb("yn_feat", [P, 2, COLS])
        def coefs(n):
            return xs[:, 1, n, 0:CH * EXPERTS * RANK].rearrange("p (c e r) -> p c e r", c=CH, e=EXPERTS)

        enc, basis, coef, wsum3 = xs[0:RANK, 1, 0, :], xs[0:RANK, 1, 1, :], coefs(2), coefs(3)
        mask, wsum = sb("mask", [P, CH, EXPERTS, RANK], U8), sb("wsum", [P, CH, RANK])
        names = ["up_t", "base_b", "up_b", "down_b", "gate", "wx_t", "wbc_t", "wz_t", "wdt_t", "conv_w", "conv_b", "dt_b",
                 "a_log", "d_row", "fcd_t", "norm_w", "wout_t"]
        par = {n: sb("p_" + n, list(w[n].shape)) for n in names}
        con = {n: sb("c_" + n, list(a.shape)) for n, a in c.items() if n != "dft_t"}
        a_row, wout, alpha, keep, skip = (sb("a_row", [P, 2 * NH]), sb("wout", [P, 2, DM]), sb("alpha", [P, 1]),
                                          sb("keep", [P, 1]), sb("skip", [P, 1]))
        ps = ctx.enter_context(nc.psum_tensor("ps_mixer", [P, 8, HALF], F32))
        PARAMS = (len(names) + len(con) + 1) * DMA

        coefs_in, params_in, stage_in = sem("coefs_in"), sem("params_in"), [sem("stage_in_0"), sem("stage_in_1")]
        wsum_step, wsum_done, basis_part, basis_ready, basis_done = (sem("wsum_step"), sem("wsum_done"), sem("basis_part"),
                                                                     sem("basis_ready"), sem("basis_done"))
        delta_ready, sum_done, whi_done, wlo_done = sem("delta_ready"), sem("sum_done"), sem("whi_done"), sem("wlo_done")
        setup, small, gate_exp, a_exp = sem("setup"), sem("small"), sem("gate_exp"), sem("a_exp")

        def stage(n):
            return xs[:, 0, n % 2, :]

        with nc.Block() as block:
            @block.sync
            def _(sp):
                for dst, n in ((coef, "coefs"), (mask[:], "masks")):
                    sp.dma_start(dst, w[n]).then_inc(coefs_in, DMA)
                for n in range(2 * CH + 1):
                    if 2 <= n < CH + 2:
                        if n - 2 < CH - 1:
                            sp.wait_ge(basis_part, n - 1)
                        else:
                            sp.wait_ge(basis_ready, 2)
                    elif n >= CH + 2:
                        sp.wait_ge(sum_done, n - CH - 1)
                    src = (c["dft_t"][n * P:(n + 1) * P, :] if n < CH else
                           w["base_t"][(n - CH) * P:(n - CH + 1) * P, :] if n < 2 * CH else w["down_t"])
                    sp.dma_start(stage(n), src).then_inc(stage_in[n % 2], DMA)

            @block.gpsimd
            def _(pool):
                nc.gpsimd.memset(neg_half[:, :], -0.5).then_inc(setup, 1)
                nc.gpsimd.memset(cb_fw[:, :, :], 0.0).then_inc(setup, 1)
                nc.gpsimd.memset(cb_bw[:, :, :], 0.0).then_inc(setup, 1)
                pool.wait_ge(setup, 3)

            @block.scalar
            def _(act):
                for n in names:
                    act.dma_start(par[n][:], w[n]).then_inc(params_in, DMA)
                for n in con:
                    act.dma_start(con[n][:], c[n]).then_inc(params_in, DMA)
                act.dma_start(enc, w["enc"]).then_inc(params_in, DMA)
                act.wait_ge(params_in, PARAMS)
                nc.scalar.activation(alpha[:, :], par["gate"][:, :], ACT.Exp, scale=-1.0).then_inc(gate_exp, 1)
                nc.scalar.activation(a_row[:, :], par["a_log"][:, :], ACT.Exp).then_inc(a_exp, 1)
                for n in range(CH + 1):
                    act.wait_ge(sum_done, n + 1)
                    if n < CH:
                        nc.scalar.copy(w_hi[:, n, :], xn[:, n % 2, :]).then_inc(whi_done, 1)
                    else:
                        nc.scalar.copy(wd_hi[:, :, :], xn[:, n % 2, :].rearrange("p (c m) -> p c m", c=CH)).then_inc(whi_done, 1)

            @block.vector
            def _(dve):
                dve.wait_ge(coefs_in, 2 * DMA)
                nc.vector.tensor_tensor(wsum3[:, :, :, :], coef[:, :, :, :], mask[:, :, :, :], ALU.mult).then_inc(wsum_step, 1)
                dve.wait_ge(wsum_step, 1)
                nc.vector.tensor_tensor(wsum[:, :, :], wsum3[:, :, 0, :], wsum3[:, :, 1, :], ALU.add).then_inc(wsum_step, 1)
                for n in range(2, EXPERTS):
                    dve.wait_ge(wsum_step, n)
                    nc.vector.tensor_tensor(wsum[:, :, :], wsum[:, :, :], wsum3[:, :, n, :], ALU.add).then_inc(
                        wsum_done if n == EXPERTS - 1 else wsum_step, 1)
                dve.wait_ge(params_in, PARAMS)
                dve.wait_ge(gate_exp, 1)
                nc.vector.tensor_scalar(keep[:, :], alpha[:, :], 1.0, None, ALU.add).then_inc(small, 1)
                dve.wait_ge(small, 1)
                nc.vector.reciprocal(alpha[:, :], keep[:, :]).then_inc(small, 1)
                dve.wait_ge(small, 2)
                nc.vector.tensor_scalar(keep[:, :], alpha[:, :], -1.0, 1.0, ALU.mult, ALU.add).then_inc(small, 1)
                nc.vector.tensor_scalar(skip[:, :], alpha[:, :], 1.0, None, ALU.add).then_inc(small, 1)
                dve.wait_ge(a_exp, 1)
                nc.vector.tensor_scalar(a_row[:, :], a_row[:, :], -1.0, None, ALU.mult).then_inc(small, 1)
                for k in range(2):
                    nc.vector.tensor_scalar(wout[:, k, :], par["wout_t"][:, k, :], par["norm_w"][:, k:k + 1], None,
                                            ALU.mult).then_inc(small, 1)
                dve.wait_ge(basis_ready, 2)
                nc.vector.tensor_copy(basis[:, :].rearrange("r (h n) -> r h n", h=2), ps[0:RANK, 0:2, :]).then_inc(basis_done, 1)
                for n in range(CH + 1):
                    dve.wait_ge(stage_in[(n + CH) % 2], DMA * ((n + CH) // 2 + 1))
                    if n >= 2:
                        dve.wait_ge(wlo_done, n - 1)
                    if n < CH:
                        dve.wait_ge(delta_ready, 2 * (n + 1))
                        nc.vector.scalar_tensor_tensor(xn[:, n % 2, :].rearrange("p (h n) -> p h n", h=2),
                                                       ps[:, 2 + 2 * (n % 2):4 + 2 * (n % 2), :], SCALING,
                                                       stage(n + CH).rearrange("p (h n) -> p h n", h=2), ALU.mult, ALU.add
                                                       ).then_inc(sum_done, 1)
                    else:
                        nc.vector.tensor_copy(xn[:, n % 2, :], stage(n + CH)).then_inc(sum_done, 1)
                    dve.wait_ge(whi_done, n + 1)
                    if n < CH:
                        nc.vector.tensor_tensor(w_lo[:, n, :], xn[:, n % 2, :], w_hi[:, n, :].bitcast(F32),
                                                ALU.subtract).then_inc(wlo_done, 1)
                    else:
                        nc.vector.tensor_tensor(wd_lo[:, :, :], xn[:, n % 2, :].rearrange("p (c m) -> p c m", c=CH),
                                                wd_hi[:, :, :].bitcast(F32), ALU.subtract).then_inc(wlo_done, 1)

            @block.tensor
            def _(pe):
                pe.wait_ge(wsum_done, 1)
                for n in range(CH):
                    pe.wait_ge(stage_in[n % 2], DMA * (n // 2 + 1))
                    for h in range(2):
                        mm = nc.tensor.matmul(ps[0:RANK, h, :], wsum[:, n, :], stage(n)[:, h * HALF:(h + 1) * HALF],
                                              start=(n == 0), stop=(n == CH - 1))
                        if n == CH - 1:
                            mm.then_inc(basis_ready, 1)
                        elif h == 1:
                            mm.then_inc(basis_part, 1)
                pe.wait_ge(params_in, PARAMS)
                pe.wait_ge(basis_done, 1)
                for n in range(CH):
                    if n >= 2:
                        pe.wait_ge(sum_done, n - 1)
                    for h in range(2):
                        nc.tensor.matmul(ps[:, 2 + 2 * (n % 2) + h, :], enc[:, n * P:(n + 1) * P],
                                         basis[:, h * HALF:(h + 1) * HALF], start=True, stop=True).then_inc(delta_ready, 1)

        step_sems = []

        def step_sem(name):
            step_sems.append(sem(name))
            return step_sems[-1]

        x_in = [step_sem(f"x_in_{t}") for t in range(TILES)]
        out_sent = step_sem("out_sent")
        stats_done, mv_done, eps_done, std_done, xn_done, post_done, up_bias = (
            step_sem("stats_done"), step_sem("mv_done"), step_sem("eps_done"), step_sem("std_done"), step_sem("xn_done"),
            step_sem("post_done"), step_sem("up_bias"))
        xt_ready, xhi_done, xlo_done = step_sem("xt_ready"), step_sem("xhi_done"), step_sem("xlo_done")
        y_ready, y_added, down_ready, h_done = step_sem("y_ready"), step_sem("y_added"), step_sem("down_ready"), step_sem("h_done")
        up_ready, up_added, skip_done = step_sem("up_ready"), step_sem("up_added"), step_sem("skip_done")
        xbc_ready, dt_ready, tap0_done, taps_done = (step_sem("xbc_ready"), step_sem("dt_ready"), step_sem("tap0_done"),
                                                     step_sem("taps_done"))
        dt_step, nabs_done, sp_exp, sp_inv, sp_step, sp_done, reach_done = (
            step_sem("dt_step"), step_sem("nabs_done"), step_sem("sp_exp"), step_sem("sp_inv"), step_sem("sp_step"), step_sem("sp_done"),
            step_sem("reach_done"))
        xf_done, bc_done, z_ready, z_done, xtok_ready, xtok_done = (step_sem("xf_done"), step_sem("bc_done"), step_sem("z_ready"),
                                                                    step_sem("z_done"), step_sem("xtok_ready"), step_sem("xtok_done"))
        cb_ready, cb_step, cb_done, decay_ready, decay_done, w_step, w_done = (
            step_sem("cb_ready"), step_sem("cb_step"), step_sem("cb_done"), step_sem("decay_ready"), step_sem("decay_done"),
            step_sem("w_step"), step_sem("w_done"))
        mixer_done, ym_ready, yz_done, sq_done, ystd_done, yinv_done, yn_done = (
            step_sem("mixer_done"), step_sem("ym_ready"), step_sem("yz_done"), step_sem("sq_done"), step_sem("ystd_done"),
            step_sem("yinv_done"), step_sem("yn_done"))
        yf_ready, yf_done, o_ready, h_new = step_sem("yf_ready"), step_sem("yf_done"), step_sem("o_ready"), step_sem("h_new")

        x1_v = x1.rearrange("l (i t b) d -> i t l b d", t=TILES, b=PB)
        out_v = out.rearrange("l (i t b) d -> i t l b d", t=TILES, b=PB)

        def step(i, gen, nxt):
            def runs(stage):
                kind = stage[1][0] if isinstance(stage[1], tuple) else 3
                return (i if kind == 3 else nxt) is not None

            order = [stage for stage in ORDER if runs(stage)]
            events = [stage[1] for stage in order if stage[0] == "turn"]
            kind2 = [e for e, (k, _) in enumerate(events) if k == 2]
            gemms = [e for e, (k, _) in enumerate(events) if k != 2]
            mid, mid_next = h_mid[:, gen, :], h_mid[:, 1 - gen, :]

            def tile_of(e):
                kind, t = events[e]
                return xs[:, gen if kind == 3 else 1 - gen, t, :]

            with nc.Block(no_gpsimd_drain=True) as block:
                @block.sync
                def _(sp):
                    if nxt is not None:
                        for t in range(TILES):
                            sp.dma_start(xs[:, 1 - gen, t, :], x1_v[nxt, t]).then_inc(x_in[t], DMA)
                    if i is not None:
                        for t in range(TILES):
                            sp.wait_ge(y_added, 2 * (gemms.index(events.index((3, t))) + 1))
                            sp.dma_start(out_v[i, t], xs[:, gen, t, :]).then_inc(out_sent, DMA)
                        sp.wait_ge(out_sent, TILES * DMA)

                @block.gpsimd
                def _(pool):
                    def inv_sqrt(e):
                        pool.wait_ge(mv_done, e + 1)
                        s = slice(e % 2, e % 2 + 1)
                        nc.gpsimd.tensor_scalar(var_eps[:, s], mean_var[:, e % 2, 1:2], EPS, None, ALU.add).then_inc(eps_done, 1)
                        pool.wait_ge(eps_done, e + 1)
                        nc.gpsimd.tensor_tensor(inv_std[:, s], var_eps[:, s], neg_half[:, 0:1], ALU.pow).then_inc(std_done, 1)

                    def post(e):
                        kind, stream = events[e][0], tile_of(e)
                        pool.wait_ge(xn_done, e + 1)
                        if kind == 2:
                            nc.gpsimd.tensor_tensor(stream, stream, xn[:, e % 2, :], ALU.add).then_inc(up_bias, 1)
                            pool.wait_ge(up_bias, kind2.index(e) + 1)
                        b = par["up_b"] if kind == 2 else par["base_b"]
                        nc.gpsimd.tensor_tensor(stream, stream, b[:, :], ALU.add).then_inc(post_done, 1)

                    def softplus(q):
                        step = [SP_STEPS * q]

                        def then(op):
                            op.then_inc(sp_step, 1)
                            step[0] += 1
                            pool.wait_ge(sp_step, step[0])

                        y, s, s2, t = dt_tmp[:, :, :], sp_s[:, :, :], sp_s2[:, :, :], sp_t[:, :, :]
                        pool.wait_ge(sp_inv, 2 * (q + 1))
                        then(nc.gpsimd.tensor_tensor(s, y, t, ALU.mult))
                        then(nc.gpsimd.tensor_tensor(s2, s, s, ALU.mult))
                        then(nc.gpsimd.tensor_scalar(t, s2, 1.0 / 13, 1.0 / 11, ALU.mult, ALU.add))
                        for n in (9, 7, 5, 3, 1):
                            then(nc.gpsimd.tensor_tensor(t, t, s2, ALU.mult))
                            then(nc.gpsimd.tensor_scalar(t, t, 1.0 / n, None, ALU.add))
                        nc.gpsimd.tensor_tensor(sp_log[:, :, :], t, s, ALU.mult).then_inc(sp_done, 1)

                    def hydra_inv_std(q):
                        pool.wait_ge(sq_done, TILES * (q + 1))
                        nc.gpsimd.tensor_scalar(y_std[:, :], sum_sq[:, :], 1.0 / DIN, EPS, ALU.mult, ALU.add).then_inc(ystd_done, 1)
                        pool.wait_ge(ystd_done, q + 1)
                        nc.gpsimd.tensor_tensor(y_inv[:, :], y_std[:, :], neg_half[:, :], ALU.pow).then_inc(yinv_done, 1)

                    if i is not None:
                        nc.gpsimd.tensor_scalar(h_skip[:, :], mid, skip[:, :], None, ALU.mult).then_inc(skip_done, 1)
                    for name, what, *part in order:
                        if name == "norm":
                            inv_sqrt(events.index(what))
                        elif name == "turn":
                            post(events.index(what))
                        elif name == "h_conv" and part == [1]:
                            softplus(what)
                        elif name == "h_norm":
                            hydra_inv_std(what)

                @block.scalar
                def _(act):
                    def x_high(e):
                        for h in range(2):
                            act.wait_ge(xt_ready, 2 * e + h + 1)
                            nc.scalar.copy(xt_hi[:, e % 2, 4 * h:4 * h + 4, :],
                                           ps[:, XT0 + h, :].rearrange("p (c t) -> p c t", t=P)).then_inc(xhi_done, 1)

                    def gelu(e):
                        t = events[e][1]
                        act.wait_ge(down_ready, kind2.index(e) + 1)
                        nc.scalar.activation(mid_next[:, t * P:(t + 1) * P], ps[:, DOWN, 0:P], ACT.Gelu,
                                             bias=par["down_b"][:, :]).then_inc(h_done, 1)

                    def h_in(q):
                        for m in range(3):
                            rows = slice(0, P if m < 2 else C_ROW + DST)
                            act.wait_ge(xbc_ready, 3 * q + m + 1)
                            nc.scalar.activation(conv[rows, m, :], ps[rows, 4 + m, :], ACT.Identity, bias=par["conv_b"][rows, m:m + 1],
                                                 scale=par["conv_w"][rows, m, TAPS - 1:TAPS]).then_inc(tap0_done, 1)
                        act.wait_ge(nabs_done, q + 1)
                        nc.scalar.activation(dt_tmp[:, :, :], dt_tmp[:, :, :], ACT.Exp).then_inc(sp_exp, 1)

                    def h_gates(q):
                        for m in range(2):
                            act.wait_ge(taps_done, 3 * (TAPS - 1) * q + 3 * (TAPS - 2) + m + 1)
                            nc.scalar.activation(x_feat[:, m, :], conv[:, m, :], ACT.Silu).then_inc(xf_done, 1)
                        act.wait_ge(taps_done, 3 * (TAPS - 1) * (q + 1))
                        nc.scalar.activation(b_feat[:, :], conv[0:DST, 2, :], ACT.Silu).then_inc(bc_done, 1)
                        nc.scalar.activation(c_feat[:, :], conv[C_ROW:C_ROW + DST, 2, :], ACT.Silu).then_inc(bc_done, 1)
                        for k in range(2):
                            act.wait_ge(z_ready, 2 * q + k + 1)
                            nc.scalar.activation(z_gate[:, 2 * k:2 * k + 2, :], ps[:, 4 + k, :].rearrange("p (t n) -> p t n", t=2),
                                                 ACT.Silu).then_inc(z_done, 1)

                    def h_cb(q):
                        act.wait_ge(decay_ready, q + 1)
                        nc.scalar.activation(decay[:, :, :, :, :].rearrange("p d t h l -> p (d t h l)"), ps[:, 5, 0:2 * TILES * NH * L],
                                             ACT.Exp).then_inc(decay_done, 1)

                    def h_norm(q):
                        for t in range(TILES):
                            act.wait_ge(yz_done, TILES * q + t + 1)
                            if t or q:
                                act.wait_ge(sq_done, TILES * q + t)
                            nc.scalar.activation(square[:, :], yz[:, t, :], ACT.Square,
                                                 accum_out=sum_sq[:, t:t + 1]).then_inc(sq_done, 1)

                    def h_back(q):
                        for k in range(2):
                            act.wait_ge(yf_ready, 2 * q + k + 1)
                            nc.scalar.copy(yn_feat[:, k, :], ps[:, 4 + k, :]).then_inc(yf_done, 1)

                    def h_out(q):
                        if q == 0:
                            act.wait_ge(o_ready, 1)
                            nc.scalar.copy(h_next[:, :], ps[:, 6, :]).then_inc(h_new, 1)

                    hydra = {"h_in": h_in, "h_gates": h_gates, "h_cb": h_cb, "h_norm": h_norm, "h_back": h_back, "h_out": h_out}
                    for name, what, *_ in order:
                        if name == "turn":
                            x_high(events.index(what))
                        elif name == "down":
                            gelu(events.index(what))
                        elif name in hydra:
                            hydra[name](what)

                @block.vector
                def _(dve):
                    def norm(e):
                        (kind, t), stream = events[e], tile_of(e)
                        if kind == 1:
                            dve.wait_ge(x_in[t], DMA)
                        elif kind == 2:
                            dve.wait_ge(y_added, 2 * (gemms.index(events.index((1, t))) + 1))
                        else:
                            dve.wait_ge(up_added, 2 * (t + 1))
                        for h in range(2):
                            nc.vector.bn_stats(stats[:, e % 2, h, :], stream[:, h * HALF:(h + 1) * HALF]).then_inc(stats_done, 1)
                        dve.wait_ge(stats_done, 2 * (e + 1))
                        nc.vector.bn_aggr(mean_var[:, e % 2, :], stats[:, e % 2, :, :]).then_inc(mv_done, 1)
                        dve.wait_ge(mv_done, e + 1)
                        dve.wait_ge(std_done, e + 1)
                        if e >= 2:
                            dve.wait_ge(xt_ready, 2 * (e - 1))
                            dve.wait_ge(post_done, e - 1)
                        nc.vector.tensor_scalar(xn[:, e % 2, :], stream, mean_var[:, e % 2, 0:1], inv_std[:, e % 2:e % 2 + 1],
                                                ALU.subtract, ALU.mult).then_inc(xn_done, 1)

                    def x_low(e):
                        for h in range(2):
                            dve.wait_ge(xhi_done, 2 * e + h + 1)
                            part = (slice(None), e % 2, slice(4 * h, 4 * h + 4), slice(None))
                            nc.vector.tensor_tensor(xt_lo[part], ps[:, XT0 + h, :].rearrange("p (c t) -> p c t", t=P),
                                                    xt_hi[part].bitcast(F32), ALU.subtract).then_inc(xlo_done, 1)

                    def add(e, h):
                        g = gemms.index(e)
                        dve.wait_ge(post_done, e + 1)
                        dve.wait_ge(y_ready, 2 * g + h + 1)
                        half = tile_of(e)[:, h * HALF:(h + 1) * HALF]
                        nc.vector.tensor_tensor(half, ps[:, Y0 + h, :], half, ALU.add).then_inc(y_added, 1)

                    def add_up(t):
                        for h in range(2):
                            dve.wait_ge(up_ready, 2 * t + h + 1)
                            half = xs[:, gen, t, h * HALF:(h + 1) * HALF]
                            nc.vector.tensor_tensor(half, ps[:, UP0 + h, :], half, ALU.add).then_inc(up_added, 1)

                    def h_in(q):
                        dve.wait_ge(dt_ready, TILES * (q + 1))
                        nc.vector.tensor_tensor(dt_raw[:, :, :], ps[:, 7, 0:TILES * 2 * NH].rearrange("p (t n) -> p t n", t=TILES),
                                                par["dt_b"][:, None, :].to_broadcast([P, TILES, 2 * NH]), ALU.add).then_inc(dt_step, 1)
                        dve.wait_ge(dt_step, 4 * q + 1)
                        nc.vector.scalar_tensor_tensor(dt_tmp[:, :, :], dt_raw[:, :, :], -1.0, dt_raw[:, :, :], ALU.mult,
                                                       ALU.min).then_inc(nabs_done, 1)

                    def h_conv(q, part):
                        taps = 3 * (TAPS - 1) * q
                        for j in range(1, 4) if part == 0 else range(4, TAPS):
                            for m in range(3):
                                if j == 1:
                                    dve.wait_ge(tap0_done, 3 * q + m + 1)
                                else:
                                    dve.wait_ge(taps_done, taps + 3 * (j - 2) + m + 1)
                                rows = slice(0, P if m < 2 else C_ROW + DST)
                                acc = conv[rows, m, :].rearrange("p (t n) -> p t n", t=TILES)[:, :, j * PB:P]
                                nc.vector.scalar_tensor_tensor(
                                    acc, ps[rows, 4 + m, :].rearrange("p (t n) -> p t n", t=TILES)[:, :, 0:P - j * PB],
                                    par["conv_w"][rows, m, TAPS - 1 - j:TAPS - j], acc, ALU.mult, ALU.add).then_inc(taps_done, 1)
                            if j == 2:
                                dve.wait_ge(sp_exp, q + 1)
                                nc.vector.tensor_scalar(sp_t[:, :, :], dt_tmp[:, :, :], 2.0, None, ALU.add).then_inc(sp_inv, 1)
                            if j == 3:
                                dve.wait_ge(sp_inv, 2 * q + 1)
                                nc.vector.reciprocal(sp_t[:, :, :], sp_t[:, :, :]).then_inc(sp_inv, 1)

                    def h_gates(q):
                        dve.wait_ge(sp_done, q + 1)
                        nc.vector.tensor_scalar(dt_raw[:, :, :], dt_raw[:, :, :], 0.0, None, ALU.max).then_inc(dt_step, 1)
                        dve.wait_ge(dt_step, 4 * q + 2)
                        nc.vector.scalar_tensor_tensor(dt[:, :, :], sp_log[:, :, :], 2.0, dt_raw[:, :, :], ALU.mult,
                                                       ALU.add).then_inc(dt_step, 1)
                        dve.wait_ge(dt_step, 4 * q + 3)
                        nc.vector.tensor_tensor(dta[:, :, :], dt[:, :, :], a_row[:, None, :].to_broadcast([P, TILES, 2 * NH]),
                                                ALU.mult).then_inc(dt_step, 1)
                        dve.wait_ge(dt_step, 4 * q + 4)
                        nc.vector.tensor_tensor(dt_reach[:, :, :, :], dta[:, :, :, None].to_broadcast([P, TILES, 2 * NH, L]),
                                                con["reach"][:, None, :, :].to_broadcast([P, TILES, 2 * NH, L]),
                                                ALU.mult).then_inc(reach_done, 1)
                        for d in range(2):
                            nc.vector.tensor_tensor(dt_mask[:, d, :, :, :],
                                                    dt[:, :, d * NH:(d + 1) * NH, None].to_broadcast([P, TILES, NH, L]),
                                                    con["side"][:, d, None, None, :].to_broadcast([P, TILES, NH, L]),
                                                    ALU.mult).then_inc(w_step, 1)

                    def h_turn(q):
                        for k in range(2):
                            dve.wait_ge(xtok_ready, 2 * q + k + 1)
                            nc.vector.tensor_copy(x_tok[:, 2 * k:2 * k + 2, :],
                                                  ps[:, 6 + k, :].rearrange("p (t n) -> p t n", t=2)).then_inc(xtok_done, 1)

                    def h_weight(q):
                        dve.wait_ge(cb_ready, q + 1)
                        cb_ps = ps[:, 4, :].rearrange("p (t n) -> p t n", t=TILES)
                        cut = P - PB
                        nc.vector.tensor_tensor(cb_fw[:, :, PB:P], cb_ps[:, :, 0:cut],
                                                con["before"][:, None, PB:P].to_broadcast([P, TILES, cut]), ALU.mult).then_inc(cb_step, 1)
                        nc.vector.tensor_tensor(cb_bw[:, :, 0:cut], cb_ps[:, :, PB:P],
                                                con["after"][:, None, 0:cut].to_broadcast([P, TILES, cut]), ALU.mult).then_inc(cb_step, 1)
                        dve.wait_ge(cb_step, 3 * q + 2)
                        nc.vector.tensor_tensor(cb[:, :, :], cb_fw[:, :, :], cb_bw[:, :, :], ALU.add).then_inc(cb_step, 1)
                        dve.wait_ge(cb_step, 3 * q + 3)
                        nc.vector.tensor_tensor(cb[:, :, :], cb[:, :, :], con["ident"][:, None, :].to_broadcast([P, TILES, P]),
                                                ALU.add).then_inc(cb_done, 1)
                        dve.wait_ge(decay_ready, q + 1)
                        dve.wait_ge(decay_done, q + 1)
                        nc.vector.tensor_tensor(d_term[:, :, :], ps[:, 5, 256:256 + TILES * NH].rearrange("p (t h) -> p t h", t=TILES),
                                                par["d_row"][:, None, :].to_broadcast([P, TILES, NH]), ALU.add).then_inc(w_step, 1)
                        nc.vector.tensor_tensor(decay[:, :, :, :, :].rearrange("p d t h l -> p (d t h l)"),
                                                decay[:, :, :, :, :].rearrange("p d t h l -> p (d t h l)"),
                                                dt_mask[:, :, :, :, :].rearrange("p d t h l -> p (d t h l)"), ALU.mult).then_inc(w_step, 1)
                        dve.wait_ge(w_step, 6 * q + 4)
                        nc.vector.tensor_tensor(d_diag[:, :, :, :], d_term[:, :, :, None].to_broadcast([P, TILES, NH, L]),
                                                con["same"][:, None, None, :].to_broadcast([P, TILES, NH, L]), ALU.mult).then_inc(w_step, 1)
                        nc.vector.tensor_tensor(weight[:, :, :, :], decay[:, 0, :, :, :], decay[:, 1, :, :, :], ALU.add).then_inc(w_step, 1)
                        dve.wait_ge(w_step, 6 * q + 6)
                        nc.vector.tensor_tensor(weight[:, :, :, :], weight[:, :, :, :], d_diag[:, :, :, :], ALU.add).then_inc(w_done, 1)

                    def h_mix(q):
                        dve.wait_ge(w_done, q + 1)
                        dve.wait_ge(cb_done, q + 1)

                        def mix(t):
                            if t >= 2:
                                dve.wait_ge(ym_ready, TILES * q + t - 1)
                            nc.vector.tensor_tensor(
                                mixer[:, t % 2, :, :].rearrange("p h (l b) -> p h l b", b=PB),
                                cb[:, t, :].rearrange("p (l b) -> p l b", b=PB)[:, None, :, :].to_broadcast([P, NH, L, PB]),
                                weight[:, t, :, :, None].to_broadcast([P, NH, L, PB]), ALU.mult).then_inc(mixer_done, 1)

                        def gate(t):
                            dve.wait_ge(ym_ready, TILES * q + t + 1)
                            if t == 0:
                                dve.wait_ge(z_done, 2 * (q + 1))
                            nc.vector.tensor_tensor(yz[:, t, :], ps[:, 6 + t % 2, 0:DIN], z_gate[:, t, :], ALU.mult).then_inc(yz_done, 1)

                        mix(0)
                        for t in range(TILES):
                            if t + 1 < TILES:
                                mix(t + 1)
                            gate(t)

                    def h_norm(q):
                        dve.wait_ge(yinv_done, q + 1)
                        for t in range(TILES):
                            nc.vector.tensor_scalar(yz[:, t, :], yz[:, t, :], y_inv[:, t:t + 1], None, ALU.mult).then_inc(yn_done, 1)

                    def h_out(q):
                        if q == 1:
                            dve.wait_ge(o_ready, 2)
                            dve.wait_ge(skip_done, 1)
                            nc.vector.scalar_tensor_tensor(h_last[:, :], ps[:, 6, :], keep[:, :], h_skip[:, :], ALU.mult,
                                                           ALU.add).then_inc(h_new, 1)

                    hydra = {"h_in": h_in, "h_conv": h_conv, "h_gates": h_gates, "h_turn": h_turn, "h_weight": h_weight,
                             "h_mix": h_mix, "h_norm": h_norm, "h_out": h_out}
                    for name, what, *part in order:
                        if name == "norm":
                            norm(events.index(what))
                        elif name == "turn":
                            x_low(events.index(what))
                        elif name == "add":
                            add(events.index(what), *part)
                        elif name == "add_up":
                            add_up(what)
                        elif name in hydra:
                            hydra[name](what, *part)

                @block.tensor
                def _(pe):
                    def transposes(e):
                        pe.wait_ge(xn_done, e + 1)
                        for h in range(2):
                            if e:
                                pe.wait_ge(xlo_done, 2 * (e - 1) + h + 1)
                            for k in range(4):
                                mm = nc.tensor.transpose(ps[:, XT0 + h, k * P:(k + 1) * P],
                                                         xn[:, e % 2, (4 * h + k) * P:(4 * h + k + 1) * P], con["ident"][:, :])
                            mm.then_inc(xt_ready, 1)

                    def split_product(out, a_hi, a_lo, b_hi, b_lo, first, last):
                        nc.tensor.matmul(out, a_hi, b_hi, start=first, stop=False)
                        nc.tensor.matmul(out, a_lo, b_hi, start=False, stop=False)
                        return nc.tensor.matmul(out, a_hi, b_lo, start=False, stop=last)

                    def gemm(e, h):
                        g, s = gemms.index(e), e % 2
                        downs = len([n for n in kind2 if n < e])
                        pe.wait_ge(xlo_done, 2 * (e + 1))
                        if g:
                            pe.wait_ge(y_added, 2 * (g - 1) + h + 1)
                        if h == 0 and downs:
                            pe.wait_ge(h_done, downs)
                        cols = slice(h * HALF, (h + 1) * HALF)
                        for k in range(CH):
                            mm = split_product(ps[:, Y0 + h, :], xt_hi[:, s, k, :], xt_lo[:, s, k, :], w_hi[:, k, cols],
                                               w_lo[:, k, cols], k == 0, k == CH - 1)
                        mm.then_inc(y_ready, 1)

                    def down(e):
                        s, n = e % 2, kind2.index(e)
                        pe.wait_ge(xlo_done, 2 * (e + 1))
                        pe.wait_ge(y_added, 2 * len([g for g in gemms if g < e]) - 1)
                        if n:
                            pe.wait_ge(h_done, n)
                        for k in range(CH):
                            mm = split_product(ps[:, DOWN, 0:P], wd_hi[:, k, :], wd_lo[:, k, :], xt_hi[:, s, k, :],
                                               xt_lo[:, s, k, :], k == 0, k == CH - 1)
                        mm.then_inc(down_ready, 1)

                    def up(t):
                        pe.wait_ge(h_new, 2)
                        for h in range(2):
                            if t:
                                pe.wait_ge(up_added, 2 * (t - 1) + h + 1)
                            nc.tensor.matmul(ps[:, UP0 + h, :], h_last[:, t * P:(t + 1) * P], par["up_t"][:, h * HALF:(h + 1) * HALF],
                                             start=True, stop=True).then_inc(up_ready, 1)

                    def h_of(q):
                        return mid if q == 0 else h_next[:, :]

                    def h_in(q):
                        h = h_of(q)
                        if q:
                            pe.wait_ge(h_new, 1)
                        nc.tensor.matmul(ps[:, 4, :], par["wx_t"][:, 0:P], h, start=True, stop=True).then_inc(xbc_ready, 1)
                        nc.tensor.matmul(ps[:, 5, :], par["wx_t"][:, P:2 * P], h, start=True, stop=True).then_inc(xbc_ready, 1)
                        nc.tensor.matmul(ps[0:C_ROW + DST, 6, :], par["wbc_t"][:, :], h, start=True, stop=True).then_inc(xbc_ready, 1)
                        for t in range(TILES):
                            nc.tensor.matmul(ps[:, 7, t * 2 * NH:(t + 1) * 2 * NH], h[:, t * P:(t + 1) * P], par["wdt_t"][:, :],
                                             start=True, stop=True).then_inc(dt_ready, 1)

                    def h_gates(q):
                        h = h_of(q)
                        taps = 3 * (TAPS - 1) * q + 3 * (TAPS - 2)
                        for k in range(2):
                            pe.wait_ge(taps_done, taps + k + 1)
                            for t in range(2 * k, 2 * k + 2):
                                mm = nc.tensor.matmul(ps[:, 4 + k, (t % 2) * DIN:(t % 2 + 1) * DIN], h[:, t * P:(t + 1) * P],
                                                      par["wz_t"][:, :], start=True, stop=True)
                            mm.then_inc(z_ready, 1)

                    def h_turn(q):
                        taps = 3 * (TAPS - 1) * q + 3 * (TAPS - 2)
                        pe.wait_ge(xf_done, 2 * (q + 1))
                        for k in range(2):
                            if k == 0:
                                pe.wait_ge(taps_done, taps + 3)
                            else:
                                pe.wait_ge(dt_step, 4 * q + 1)
                            for t in range(2 * k, 2 * k + 2):
                                for m in range(2):
                                    mm = nc.tensor.transpose(ps[:, 6 + k, (t % 2) * DIN + m * P:(t % 2) * DIN + (m + 1) * P],
                                                             x_feat[:, m, t * P:(t + 1) * P], con["ident"][:, :])
                            mm.then_inc(xtok_ready, 1)

                    def h_cb(q):
                        pe.wait_ge(bc_done, 2 * (q + 1))
                        pe.wait_ge(z_done, 2 * q + 1)
                        for t in range(TILES):
                            cols = slice(t * P, (t + 1) * P)
                            mm = nc.tensor.matmul(ps[:, 4, cols], b_feat[:, cols], c_feat[:, cols], start=True, stop=True)
                        mm.then_inc(cb_ready, 1)
                        pe.wait_ge(z_done, 2 * q + 2)
                        for t in range(TILES):
                            for m in range(2):
                                nc.tensor.matmul(ps[:, 5, 256 + t * NH:256 + (t + 1) * NH], x_feat[:, m, t * P:(t + 1) * P],
                                                 par["fcd_t"][:, m, :], start=(m == 0), stop=(m == 1))
                        pe.wait_ge(reach_done, q + 1)
                        for d, between in ((0, "later"), (1, "earlier")):
                            n = TILES * NH * L
                            mm = nc.tensor.matmul(ps[:, 5, d * n:(d + 1) * n], con[between][:, :],
                                                  dt_reach[:, :, d * NH:(d + 1) * NH, :].rearrange("p t h l -> p t (h l)"),
                                                  start=True, stop=True)
                        mm.then_inc(decay_ready, 1)

                    def h_mix(q):
                        pe.wait_ge(xtok_done, 2 * (q + 1))
                        for t in range(TILES):
                            pe.wait_ge(mixer_done, TILES * q + t + 1)
                            if t >= 2:
                                pe.wait_ge(yz_done, TILES * q + t - 1)
                            for n in range(NH):
                                cols = slice(n * HD, (n + 1) * HD)
                                mm = nc.tensor.matmul(ps[:, 6 + t % 2, cols], mixer[:, t % 2, n, :], x_tok[:, t, cols],
                                                      start=True, stop=True)
                            mm.then_inc(ym_ready, 1)

                    def h_back(q):
                        pe.wait_ge(w_done, q + 1)
                        pe.wait_ge(yn_done, TILES * (q + 1))
                        for k in range(2):
                            for t in range(TILES):
                                mm = nc.tensor.transpose(ps[:, 4 + k, t * P:(t + 1) * P], yz[:, t, k * P:(k + 1) * P], con["ident"][:, :])
                            mm.then_inc(yf_ready, 1)

                    def h_out(q):
                        pe.wait_ge(yz_done, TILES * (q + 1))
                        for k in range(2):
                            pe.wait_ge(yf_done, 2 * q + k + 1)
                            mm = nc.tensor.matmul(ps[:, 6, :], wout[:, k, :], yn_feat[:, k, :], start=(k == 0), stop=(k == 1))
                        mm.then_inc(o_ready, 1)

                    hydra = {"h_in": h_in, "h_gates": h_gates, "h_turn": h_turn, "h_cb": h_cb, "h_mix": h_mix, "h_back": h_back,
                             "h_out": h_out}
                    for name, what, *part in order:
                        if name == "turn":
                            transposes(events.index(what))
                        elif name == "gemm":
                            gemm(events.index(what), *part)
                        elif name == "down":
                            down(events.index(what))
                        elif name == "up":
                            up(what)
                        elif name in hydra:
                            hydra[name](what)

            nc.all_engine_barrier(sems_to_clear=range(step_sems[0].num, step_sems[-1].num + 1))

        step(None, 1, 0)
        with nc.Fori(0, STEPS - 2, 2) as i:
            step(i, 0, i + 1)
            step(i + 1, 1, i + 2)
        step(STEPS - 2, 0, STEPS - 1)
        step(STEPS - 1, 1, None)

def inverse_transform(n):
    import numpy as np

    k = np.arange(n)
    out = np.empty((n, n))
    out[0] = 1.0 / np.sqrt(n)
    for f in range(1, (n - 1) // 2 + 1):
        angle = 2.0 * np.pi * ((f * k) % n) / n
        out[2 * f - 1] = np.sqrt(2.0 / n) * np.cos(angle)
        out[2 * f] = np.sqrt(2.0 / n) * np.sin(angle)
    if n % 2 == 0:
        out[n - 1] = np.where(k % 2 == 0, 1.0, -1.0) / np.sqrt(n)
    return out.astype(np.float32)


def kernel(**inputs):
    import ml_dtypes
    import numpy as np
    import concourse.bacc as bacc
    from concourse import mybir as mb
    from concourse.bass_utils import run_bass_kernel_spmd as run

    f32, bf16 = np.float32, ml_dtypes.bfloat16
    a = {n: np.asarray(v) for n, v in inputs.items()}
    att = {n[len("L0_attn_a_"):]: v for n, v in a.items() if n.startswith("L0_attn_a_")}
    hyd = {n[len("L0_attn_b_"):]: v for n, v in a.items() if n.startswith("L0_attn_b_")}
    ffn = {n[len("L0_ffn_"):]: v for n, v in a.items() if n.startswith("L0_ffn_")}
    x = att["x"]
    L, T, D = x.shape
    head = att["wk_w"].shape[0]
    PB = P // L
    NH, DIN = hyd["hy_fcD_w"].shape
    DM = hyd["w_down"].shape[0]
    DST = (hyd["hy_in_w"].shape[0] - 2 * DIN - 2 * NH) // 2
    TAPS = hyd["hy_conv_w"].shape[2]
    C_ROW = 32

    def rows(v, n=P):
        return np.broadcast_to(v.reshape(1, -1), (n, v.size))

    def chunks(m):
        return m.reshape(-1, P, m.shape[1]).transpose(1, 0, 2)

    def bc_rows(m):
        out = np.zeros((C_ROW + DST,) + m.shape[1:], m.dtype)
        out[:DST], out[C_ROW:] = m[:DST], m[DST:]
        return out

    def conv_rows(m):
        out = np.zeros((P, 3, m.shape[1]), m.dtype)
        out[:, 0], out[:, 1], out[:C_ROW + DST, 2] = m[:P], m[P:2 * P], bc_rows(m[DIN:])
        return out

    row, pos = np.arange(P) // PB, np.arange(P) % PB
    t = np.arange(L)
    same_pos = pos[:, None] == pos[None, :]
    lt, gt = row[:, None] < row[None, :], row[:, None] > row[None, :]
    kv_scale = np.ones((P, 1), f32)
    kv_scale[:3 * head] = 1.0 / np.sqrt(f32(head))
    reach = np.stack([row[:, None] <= t - 1] * NH + [row[:, None] >= t + 1] * NH, 1)
    consts = {
        "ident": np.eye(P), "before": same_pos & lt, "after": same_pos & gt, "later": same_pos & gt,
        "earlier": same_pos & lt, "reach": reach, "side": np.stack([row[:, None] < t, row[:, None] > t], 1),
        "same": row[:, None] == t, "dft_t": inverse_transform(D),
    }
    consts = {n: v.astype(f32) for n, v in consts.items()}
    attn = {
        "x": x, "wq_t": att["wq_w"].T, "wkv_t": np.concatenate([att["wk_w"]] * 3 + [att["wv_w"]]).T, "wo_t": att["wo_w"].T,
        "bq": att["wq_b"].reshape(-1, P).T, "bkv": np.concatenate([att["wk_b"]] * 3 + [att["wv_b"]])[:, None],
        "kv_scale": kv_scale, "bo": rows(att["wo_b"]), "ident": consts["ident"], "ident_b": np.eye(P).astype(bf16),
        "causal_b": np.where(np.tril(np.ones((P, P), bool)), 0.0, -1e30).astype(bf16),
    }
    in_w = hyd["hy_in_w"]
    mix = {
        "base_t": ffn["W_base"].T, "enc": np.concatenate([ffn["enc0"], ffn["enc1"]]),
        "coefs": np.concatenate([ffn["coefs0"], ffn["coefs1"]], 2).transpose(1, 0, 2),
        "masks": np.concatenate([ffn["mask0"], ffn["mask1"]], 2).transpose(1, 0, 2),
        "base_b": rows(ffn["b_base"]), "up_t": hyd["w_up"].T, "up_b": rows(hyd["b_up"]), "down_b": hyd["b_down"][:, None],
        "down_t": chunks(hyd["w_down"].T).reshape(P, -1), "gate": rows(hyd["gate1"]),
        "wz_t": in_w[:DIN].T, "wx_t": in_w[DIN:2 * DIN].T, "wbc_t": bc_rows(in_w[2 * DIN:2 * DIN + 2 * DST]).T,
        "wdt_t": in_w[2 * DIN + 2 * DST:].T, "conv_w": conv_rows(hyd["hy_conv_w"][:, 0, :]),
        "conv_b": conv_rows(hyd["hy_conv_b"][:, None])[:, :, 0], "dt_b": rows(np.concatenate([hyd["hy_dt_bias"]] * 2)),
        "a_log": rows(np.concatenate([hyd["hy_A_log"]] * 2)), "d_row": rows(hyd["hy_D"]), "fcd_t": chunks(hyd["hy_fcD_w"].T),
        "norm_w": hyd["hy_norm_w"].reshape(-1, P).T, "wout_t": chunks(hyd["hy_out_w"].T),
    }
    mix["coefs"] = chunks(mix["coefs"].reshape(D, -1)).reshape(P, D // P, *mix["coefs"].shape[1:])
    mix["masks"] = chunks(mix["masks"].reshape(D, -1)).reshape(P, D // P, *mix["masks"].shape[1:])

    nc = bacc.Bacc("TRN2", target_bir_lowering=False, num_devices=1)
    arrays = {}

    def declare(group, prefix):
        aps = {}
        for n, v in group.items():
            v = arrays[prefix + n] = np.ascontiguousarray(v)
            aps[n] = nc.dram_tensor(prefix + n, v.shape, mb.dt.from_np(v.dtype), kind="ExternalInput").ap()
        return aps

    at, mx, cn = declare(attn, "in_a_"), declare(mix, "in_m_"), declare(consts, "in_c_")
    out = nc.dram_tensor("out_0", x.shape, F32, kind="ExternalOutput").ap()
    wq_split = nc.dram_tensor("wq_split", (2, D // P, P, D // P, P), F32).ap()
    x1 = nc.dram_tensor("x1", x.shape, F32).ap()
    attention_program(nc, *(at[n] for n in ("x", "wq_t", "wkv_t", "wo_t", "bq", "bkv", "kv_scale", "bo", "ident", "ident_b",
                                            "causal_b")), wq_split, x1)
    mixer_program(nc, x1, mx, cn, out)
    r = run(nc, [arrays], core_ids=[0])
    return r.results[0]["out_0"]
```
